# Optimizing a Trainium2 kernel written in Bass

```python
import numpy as np
import jax
import jax.numpy as jnp

def _softmax(x, axis=-1):
    return jax.nn.softmax(x, axis=axis)

def _gelu(x):
    return jax.nn.gelu(x, approximate=True)

def _silu(x):
    return jax.nn.silu(x)

def _sigmoid(x):
    return jax.nn.sigmoid(x)

def _layernorm(x, axis=-1, eps=1e-05):
    m = jnp.mean(x, axis=axis, keepdims=True)
    v = jnp.var(x, axis=axis, keepdims=True)
    return (x - m) / jnp.sqrt(v + eps)

def _scatter_add(tgt, idx, src, axis=0):
    return tgt.at[idx].add(src)

def _segment_sum(src, seg, n):
    return jax.ops.segment_sum(src, seg, n)
kernel_name = 'mk_gnn_resnorm_d2_gnn_r8_b24f14'

def setup_inputs(seed: int=0):
    np.random.seed(seed)
    _w = jnp.asarray

    def _rec_inputs():
        import jax
        import jax.numpy as jnp
        _gk = jax.random.key(seed)
        x = -8.776e-05 + 1 * jax.random.normal(jax.random.fold_in(_gk, 1), (2500, 256), jnp.float32)
        src = jax.random.randint(jax.random.fold_in(_gk, 2), (40000,), 0, 2500, jnp.int32)
        dst = jnp.minimum((2500 * jax.random.uniform(jax.random.fold_in(_gk, 3), (40000,)) ** 2.0).astype(jnp.int32), 19999)
        _o = jnp.argsort(dst, stable=True)
        src = src[_o]
        dst = dst[_o]
        edge_attr_64 = 0.000279952 + 1.00013 * jax.random.normal(jax.random.fold_in(_gk, 11), (40000, 64), jnp.float32)
        edge_type_8 = jax.random.randint(jax.random.fold_in(_gk, 13), (40000,), 0, 8, jnp.int32)
        return (x, src, dst, edge_attr_64, edge_type_8)
    x, src, dst, edge_attr_64, edge_type_8 = _rec_inputs()

    def _L0_gnn_setup():
        import jax, jax.numpy as jnp
        import numpy as np
        NUM_NODES = 2500
        NUM_EDGES = 40000
        NODE_DIM = 256
        EDGE_DIM = 64
        HIDDEN = 512

        def _glorot(key, shape):
            fan_in = shape[0]
            bound = 1.0 / np.sqrt(fan_in)
            return jax.random.uniform(key, shape, jnp.float32, -bound, bound)
        key = jax.random.key(seed)
        ks = jax.random.split(key, 12)
        node_features = jax.random.normal(ks[0], (NUM_NODES, NODE_DIM), jnp.float32)
        edge_index = jax.random.randint(ks[1], (2, NUM_EDGES), 0, NUM_NODES, jnp.int64 if jax.config.jax_enable_x64 else jnp.int32)
        edge_features = jax.random.normal(ks[2], (NUM_EDGES, EDGE_DIM), jnp.float32)
        edge_in = 2 * NODE_DIM + EDGE_DIM
        node_in = NODE_DIM + HIDDEN
        params = {'W1': _glorot(ks[3], (edge_in, HIDDEN)), 'b1': _glorot(ks[4], (HIDDEN,)), 'W2': _glorot(ks[5], (HIDDEN, HIDDEN)), 'b2': _glorot(ks[6], (HIDDEN,)), 'W3': _glorot(ks[7], (node_in, HIDDEN)), 'b3': _glorot(ks[8], (HIDDEN,)), 'W4': _glorot(ks[9], (HIDDEN, NODE_DIM)), 'b4': _glorot(ks[10], (NODE_DIM,))}
        return {'node_features': node_features, 'edge_index': edge_index, 'edge_features': edge_features, **params}
    _L0_gnn_all = _L0_gnn_setup()
    _L0_gnn_in = {k: v for k, v in _L0_gnn_all.items() if k in ('W1', 'b1', 'W2', 'b2', 'W3', 'b3', 'W4', 'b4')}
    del _L0_gnn_all

    def _L1_gnn_setup():
        import jax, jax.numpy as jnp
        import numpy as np
        N, E, R, H, D = (3750, 37500, 8, 8, 32)
        IN_F = 256
        NEG_SLOPE = 0.2
        key = jax.random.key(seed)
        k = jax.random.split(key, 6)
        x = jax.random.normal(k[0], (N, IN_F), dtype=jnp.float32)
        W = jax.random.normal(k[1], (R, H * D, IN_F), dtype=jnp.float32) * 0.05
        attn_src = jax.random.normal(k[2], (H, D), dtype=jnp.float32) * 0.1
        attn_dst = jax.random.normal(k[3], (H, D), dtype=jnp.float32) * 0.1
        edge_index = jax.random.randint(k[4], (2, E), 0, N, dtype=jnp.int64) if jax.config.read('jax_enable_x64') else jax.random.randint(k[4], (2, E), 0, N, dtype=jnp.int32)
        edge_type = jax.random.randint(k[5], (E,), 0, R, dtype=edge_index.dtype)
        return dict(x=x, W=W, attn_src=attn_src, attn_dst=attn_dst, edge_index=edge_index, edge_type=edge_type)
    _L1_gnn_all = _L1_gnn_setup()
    _L1_gnn_in = {k: v for k, v in _L1_gnn_all.items() if k in ('W', 'attn_src', 'attn_dst')}
    del _L1_gnn_all
    return {'x': x, 'src': src, 'dst': dst, 'edge_attr_64': edge_attr_64, 'edge_type_8': edge_type_8, 'L0_gnn_W1': _L0_gnn_in['W1'], 'L0_gnn_b1': _L0_gnn_in['b1'], 'L0_gnn_W2': _L0_gnn_in['W2'], 'L0_gnn_b2': _L0_gnn_in['b2'], 'L0_gnn_W3': _L0_gnn_in['W3'], 'L0_gnn_b3': _L0_gnn_in['b3'], 'L0_gnn_W4': _L0_gnn_in['W4'], 'L0_gnn_b4': _L0_gnn_in['b4'], 'L1_gnn_W': _L1_gnn_in['W'], 'L1_gnn_attn_src': _L1_gnn_in['attn_src'], 'L1_gnn_attn_dst': _L1_gnn_in['attn_dst']}

def reference(x, src, dst, edge_attr_64, edge_type_8, L0_gnn_W1, L0_gnn_b1, L0_gnn_W2, L0_gnn_b2, L0_gnn_W3, L0_gnn_b3, L0_gnn_W4, L0_gnn_b4, L1_gnn_W, L1_gnn_attn_src, L1_gnn_attn_dst):
    import jax
    import jax.numpy as jnp

    def _L0_gnn_ref(node_features, edge_index, edge_features, W1, b1, W2, b2, W3, b3, W4, b4):
        import jax, jax.numpy as jnp
        import numpy as np
        NUM_NODES = 2500
        NUM_EDGES = 40000
        NODE_DIM = 256
        EDGE_DIM = 64
        HIDDEN = 512

        def _glorot(key, shape):
            fan_in = shape[0]
            bound = 1.0 / np.sqrt(fan_in)
            return jax.random.uniform(key, shape, jnp.float32, -bound, bound)
        src_idx = edge_index[0]
        tgt_idx = edge_index[1]
        edge_input = jnp.concatenate([node_features[src_idx], node_features[tgt_idx], edge_features], axis=-1)
        h = jax.nn.relu(edge_input @ W1 + b1)
        messages = h @ W2 + b2
        aggregated = jax.ops.segment_sum(messages, tgt_idx, num_segments=NUM_NODES)
        node_input = jnp.concatenate([node_features, aggregated], axis=-1)
        g = jax.nn.relu(node_input @ W3 + b3)
        node_update = g @ W4 + b4
        return node_features + node_update

    def _L1_gnn_ref(x, W, attn_src, attn_dst, edge_index, edge_type):
        import jax, jax.numpy as jnp
        import numpy as np
        N, E, R, H, D = (3750, 37500, 8, 8, 32)
        IN_F = 256
        NEG_SLOPE = 0.2
        n = x.shape[0]
        r = W.shape[0]
        h, d = attn_src.shape
        h_all = jnp.einsum('nf,rof->rno', x, W).reshape(r, n, h, d)
        src, dst = (edge_index[0], edge_index[1])
        h_src = h_all[edge_type, src]
        h_dst = h_all[edge_type, dst]
        scores = jnp.einsum('ehd,hd->eh', h_src, attn_src) + jnp.einsum('ehd,hd->eh', h_dst, attn_dst)
        scores = jnp.where(scores > 0, scores, NEG_SLOPE * scores)
        amax = jnp.maximum(jax.ops.segment_max(scores, dst, num_segments=n), 0.0)
        w = jnp.exp(scores - amax[dst])
        denom = jax.ops.segment_sum(w, dst, num_segments=n) + 1e-12
        w = w / denom[dst]
        msg = h_src * w[..., None]
        out = jax.ops.segment_sum(msg, dst, num_segments=n)
        return out.reshape(n, h * d)
    edge_index = jnp.stack([src, dst])
    x = _layernorm(x + _L0_gnn_ref(x, edge_index, edge_attr_64, L0_gnn_W1, L0_gnn_b1, L0_gnn_W2, L0_gnn_b2, L0_gnn_W3, L0_gnn_b3, L0_gnn_W4, L0_gnn_b4), axis=-1)
    x = _layernorm(x + _L1_gnn_ref(x, L1_gnn_W, L1_gnn_attn_src, L1_gnn_attn_dst, edge_index, edge_type_8), axis=-1)
    return x

_drawn_inputs = setup_inputs


def setup_inputs(seed=0):
    import zlib

    import numpy as np

    out = dict(_drawn_inputs(seed))
    spreads = {}
    factors = {'L0_gnn_b1': 4.193, 'L0_gnn_b3': 8.0, 'L0_gnn_b4': 3.038}
    for name, (base, spread) in spreads.items():
        noise = np.random.default_rng([zlib.crc32(name.encode()), seed]).standard_normal(out[name].shape)
        drawn = base * np.exp(spread * noise) if base else spread * noise
        out[name] = jnp.asarray(drawn.astype(out[name].dtype))
    for name, factor in factors.items():
        out[name] = (out[name] * factor).astype(out[name].dtype)
    return out
```

```python
from contextlib import ExitStack

import concourse.bass as bass
from concourse import mybir

F32 = mybir.dt.float32
I32 = mybir.dt.int32
U32 = mybir.dt.uint32
ALU = mybir.AluOpType
ACT = mybir.ActivationFunctionType
AX = mybir.AxisListType

P = 128
N, E, D, ED, HID, R, H = 2500, 40000, 256, 64, 512, 8, 8
HD = D // H
HW = HD + 1
ROW = H * HW
NT = -(-N // P)
NP = NT * P
U = 8
GU = 16
STEPS = -(-(-(-E // P) + NT) // GU) * GU
ITERS = STEPS // U
GROUPS = STEPS // GU
EP = E + 192
CNT = -(-E // P)
PAD_DST = 4095
EPS_LN = 1e-5
EPS_DEN = 1e-12
AGW = HID + 1


class Chain:

    def __init__(self, eng, sem):
        self.eng, self.sem, self.n = eng, sem, 0

    def __call__(self, ins):
        self.n += 1
        ins.then_inc(self.sem, 1)
        self.eng.wait_ge(self.sem, self.n)


def wait_step(eng, sem, it, j, ago=0):
    v = it * U + (j + 1 - ago)
    if not isinstance(v, int) or v > 0:
        eng.wait_ge(sem, v)


def run_skewed(eng, stages):
    def body(it):
        for j in range(U):
            for f, lag in stages:
                if j >= lag:
                    f(it, j - lag)
                elif not isinstance(it, int):
                    f(it - 1, j - lag + U)
    body(0)
    with eng.Fori(1, ITERS) as it:
        body(it)
    for j in range(max(lag for _, lag in stages)):
        for f, lag in stages:
            if j < lag:
                f(ITERS - 1, j - lag + U)


def load_row(eng, regs, row, it, top):
    eng.load(regs, row[0:1, bass.ds(it * U, U)])


def gnn_kernel(nc, x, xT, dst, meta, efT, W1, b1, W2, b2, W3, b3, W4, b4, WT, Wn, attn, out):
    A_dram = nc.dram_tensor("A_table", (NP, HID), F32, kind="Internal").ap()
    T_dram = nc.dram_tensor("L1_table", (R * NP, ROW), F32, kind="Internal").ap()
    mm = nc.tensor.matmul

    class Mem:
        pass

    m = Mem()
    with ExitStack() as whole:
        def sb(ctx, name, shape, dt=F32):
            return ctx.enter_context(nc.sbuf_tensor(name, shape, dt))

        def psum(ctx, name, shape):
            return ctx.enter_context(nc.psum_tensor(name, shape, F32))

        def sem(ctx, name):
            return ctx.enter_context(nc.semaphore(name))

        m.ident = sb(whole, "ident", [P, P])
        m.iota = sb(whole, "iota", [P, P])
        m.ones = sb(whole, "ones", [P, P])
        m.xs = sb(whole, "xs", [P, NT, D])
        m.xTs = sb(whole, "xTs", [P, 2, NP])
        m.dl = sb(whole, "dl", [P, STEPS])
        m.src_ix = sb(whole, "src_ix", [P, STEPS], U32)
        m.tab_ix = sb(whole, "tab_ix", [P, STEPS], U32)
        m.emask = sb(whole, "emask", [P, STEPS, R])
        m.cont = sb(whole, "cont", [P, STEPS])
        m.nt_i = sb(whole, "nt_i", [1, STEPS], I32)
        m.start_i = sb(whole, "start_i", [1, STEPS], I32)

        l0 = whole.enter_context(ExitStack())
        m.w1e = sb(l0, "w1e", [ED, HID])
        m.w2 = sb(l0, "w2", [P, 4, HID])
        m.w3 = sb(l0, "w3", [P, 6, HID])
        m.w4 = sb(l0, "w4", [P, 4, D])
        m.b2 = sb(l0, "b2b", [P, HID])
        m.b3 = sb(l0, "b3b", [P, HID])
        m.b4 = sb(l0, "b4b", [P, D])
        m.agg = sb(l0, "agg", [P, NT, AGW])
        m.B = sb(l0, "B", [P, NT, HID])

        with ExitStack() as ctx:
            w1 = sb(ctx, "w1", [P, 4, HID])
            b1b = sb(ctx, "b1b", [P, HID])
            Ab = sb(ctx, "Ab", [P, 2, HID])
            dsti = sb(ctx, "dsti", [P, CNT], I32)
            dstf = sb(ctx, "dstf", [P, CNT])
            below = sb(ctx, "below", [P, CNT])
            cnt = sb(ctx, "cnt", [P, NT + 1])
            upper = sb(ctx, "upper", [P, P])
            n128 = sb(ctx, "n128", [P, P])
            steps_f = sb(ctx, "steps_f", [P, STEPS])
            col = sb(ctx, "col", [NT, 8])
            coli = sb(ctx, "coli", [NT, 2], I32)
            sel = sb(ctx, "sel", [NT, 2, STEPS])
            sval = sb(ctx, "sval", [NT, STEPS])
            metab = sb(ctx, "metab", [P, STEPS, 4], I32)
            ntb = sb(ctx, "ntb", [P, STEPS])
            iota_r = sb(ctx, "iota_r", [P, R])
            tf = sb(ctx, "tf", [P, 2, STEPS])
            pa = psum(ctx, "pa", [P, 2, HID])
            pb = psum(ctx, "pb", [P, 2, HID])
            pc = psum(ctx, "pc", [P, HID])
            pn = psum(ctx, "pn", [P, HID])
            in_dst = sem(ctx, "in_dst")
            in_x = sem(ctx, "in_x")
            in_rest = sem(ctx, "in_rest")
            set0 = sem(ctx, "set0")
            consts = sem(ctx, "consts")
            dve_done = sem(ctx, "dve_done")
            counted = sem(ctx, "counted")
            tiles_in = sem(ctx, "tiles_in")
            sel_in = sem(ctx, "sel_in")
            pe_step = sem(ctx, "pe_step")
            tables = sem(ctx, "tables")
            meta_in = [sem(ctx, f"meta_in{j}") for j in range(U)]
            A_mm, A_out, B_mm, B_out = (sem(ctx, n) for n in ("A_mm", "A_out", "B_mm", "B_out"))
            A_wr = [sem(ctx, f"A_wr{k}") for k in range(2)]

            with nc.Block() as block:
                @block.sync
                def _(sp):
                    sp.dma_start(dsti[:, :], dst).then_inc(in_dst, 16)
                    sp.dma_start(m.xTs[:, :, :], xT.rearrange("(c p) n -> p c n", p=P)).then_inc(in_x, 16)
                    sp.dma_start(w1[:, :, :], W1[0:2 * D, :].rearrange("(c p) n -> p c n", p=P)).then_inc(in_x, 16)
                    sp.dma_start(b1b[:, :], b1.partition_broadcast(P)).then_inc(in_x, 16)
                    sp.dma_start(m.w1e[:, :], W1[2 * D:2 * D + ED, :]).then_inc(in_rest, 16)
                    sp.dma_start(m.w2[:, :, :], W2.rearrange("(c p) n -> p c n", p=P)).then_inc(in_rest, 16)
                    sp.dma_start(m.w3[:, :, :], W3.rearrange("(c p) n -> p c n", p=P)).then_inc(in_rest, 16)
                    sp.dma_start(m.w4[:, :, :], W4.rearrange("(c p) n -> p c n", p=P)).then_inc(in_rest, 16)
                    sp.dma_start(m.b2[:, :], b2.partition_broadcast(P)).then_inc(in_rest, 16)
                    sp.dma_start(m.b3[:, :], b3.partition_broadcast(P)).then_inc(in_rest, 16)
                    sp.dma_start(m.b4[:, :], b4.partition_broadcast(P)).then_inc(in_rest, 16)
                    sp.dma_start(m.xs[:, :, :], x.rearrange("(t p) n -> p t n", p=P)).then_inc(in_rest, 16)
                    sp.wait_ge(tables, 1)
                    regs = [sp.alloc_register(f"start{j}") for j in range(U)]

                    def load_meta(it):
                        load_row(sp, regs, m.start_i, it, E)
                        for j in range(U):
                            if not isinstance(it, int):
                                sp.wait_ge(meta_in[j], it * 16)
                            first = sp.snap(regs[j], min_val=0, max_val=E)
                            sp.dma_start(metab[:, bass.ds(it * U + j, 1), :].rearrange("p o f -> p (o f)"),
                                         meta[bass.ds(first, P), :]).then_inc(meta_in[j], 16)

                    load_meta(0)
                    with sp.Fori(1, ITERS) as it:
                        load_meta(it)
                    sp.wait_ge(in_rest, 16 * 8)

                @block.gpsimd
                def _(pool):
                    pool.memset(m.ident[:, :], 0.0).then_inc(set0, 1)
                    pool.memset(upper[:, :], 1.0).then_inc(set0, 1)
                    for t, pattern, mult in ((m.iota, [[1, P]], 0), (n128, [[0, P]], P), (steps_f, [[1, STEPS]], 0),
                                             (iota_r, [[1, R]], 0)):
                        pool.iota(t[:, :], pattern, base=0, channel_multiplier=mult,
                                  allow_small_or_imprecise_dtypes=True).then_inc(consts, 1)
                    pool.memset(m.ones[:, :], 1.0).then_inc(consts, 1)
                    pool.wait_ge(set0, 2)
                    pool.affine_select(out=m.ident[:, :], in_=m.ident[:, :], compare_op=ALU.not_equal, fill=1.0,
                                       base=0, pattern=[[-1, P]], channel_multiplier=1).then_inc(consts, 1)
                    pool.affine_select(out=upper[:, :], in_=upper[:, :], compare_op=ALU.is_gt, fill=0.0,
                                       base=0, pattern=[[1, P]], channel_multiplier=-1).then_inc(consts, 1)
                    pool.memset(m.agg[:, :, :], 0.0).then_inc(consts, 1)

                @block.vector
                def _(dve):
                    do = Chain(dve, dve_done)
                    dve.wait_ge(in_dst, 16)
                    do(dve.tensor_copy(dstf[:, :], dsti[:, :]))
                    do(dve.memset(cnt[:, 0:1], 0.0))
                    for n in range(1, NT + 1):
                        do(dve.tensor_scalar(below[:, :], dstf[:, :], float(P * n), None, ALU.is_lt, ALU.add,
                                             accum_out=cnt[:, n:n + 1]))
                    dve.sem_inc(counted, 1)
                    dve.wait_ge(pe_step, 1)
                    do(dve.tensor_copy(col[:, 0:2], pn[0:NT, 0:2]))
                    do(dve.tensor_tensor(col[:, 2:3], col[:, 1:2], col[:, 0:1], ALU.subtract))
                    do(dve.tensor_scalar(coli[:, 0:1], col[:, 2:3], float(P - 1), None, ALU.add))
                    do(dve.tensor_scalar(coli[:, 1:2], coli[:, 0:1], 7, None, ALU.arith_shift_right))
                    do(dve.tensor_copy(col[:, 3:4], coli[:, 1:2]))
                    dve.sem_inc(tiles_in, 1)
                    dve.wait_ge(pe_step, 2)
                    do(dve.tensor_copy(col[:, 4:5], pn[0:NT, 2:3]))
                    do(dve.tensor_tensor(col[:, 5:6], col[:, 4:5], col[:, 3:4], ALU.add))
                    do(dve.tensor_scalar(col[:, 6:7], col[:, 4:5], float(-P), float(-E), ALU.mult, ALU.add))
                    do(dve.tensor_tensor(col[:, 7:8], col[:, 6:7], col[:, 0:1], ALU.add))
                    dve.wait_ge(consts, 8)
                    do(dve.tensor_scalar(sel[:, 0, :], steps_f[0:NT, :], col[:, 4:5], None, ALU.is_ge))
                    do(dve.scalar_tensor_tensor(sel[:, 1, :], steps_f[0:NT, :], col[:, 5:6], sel[:, 0, :], ALU.is_lt, ALU.mult))
                    do(dve.tensor_scalar(sval[:, :], steps_f[0:NT, :], float(P), col[:, 7:8], ALU.mult, ALU.add))
                    do(dve.tensor_tensor(sval[:, :], sval[:, :], sel[:, 1, :], ALU.mult))
                    dve.sem_inc(sel_in, 1)
                    dve.wait_ge(pe_step, 3)
                    do(dve.tensor_copy(ntb[:, :], pn[:, 0:STEPS]))
                    do(dve.tensor_scalar(m.nt_i[:, :], ntb[0:1, :], 1.0 / P, None, ALU.mult))
                    do(dve.tensor_scalar(m.start_i[:, :], pc[0:1, 0:STEPS], float(E), None, ALU.add))
                    dve.sem_inc(tables, 1)
                    do(dve.memset(m.cont[:, 0:1], 0.0))
                    do(dve.tensor_tensor(m.cont[:, 1:STEPS], ntb[:, 1:STEPS], ntb[:, 0:STEPS - 1], ALU.is_equal))
                    dve.wait_ge(in_x, 48)
                    for t in range(NT):
                        dve.wait_ge(B_mm, t + 1)
                        dve.tensor_tensor(m.B[:, t, :], pb[:, t % 2, :], b1b[:, :], ALU.add).then_inc(B_out, 1)
                    for j in range(U):
                        dve.wait_ge(meta_in[j], 16 * ITERS)
                    do(dve.tensor_copy(tf[:, 0, :], metab[:, :, 1]))
                    do(dve.tensor_tensor(m.dl[:, :], tf[:, 0, :], ntb[:, :], ALU.subtract))
                    do(dve.tensor_copy(m.src_ix[:, :], metab[:, :, 0]))
                    do(dve.tensor_copy(tf[:, 0, :], metab[:, :, 2]))
                    do(dve.tensor_copy(tf[:, 1, :], metab[:, :, 0]))
                    do(dve.scalar_tensor_tensor(m.tab_ix[:, :], tf[:, 0, :], float(NP), tf[:, 1, :], ALU.mult, ALU.add))
                    do(dve.tensor_tensor(m.emask[:, :, :], tf[:, 0, :].unsqueeze(2).to_broadcast([P, STEPS, R]),
                                         iota_r[:, :].unsqueeze(1).to_broadcast([P, STEPS, R]), ALU.is_equal))

                @block.tensor
                def _(pe):
                    pe.wait_ge(consts, 8)
                    pe.wait_ge(counted, 1)
                    mm(pn[0:NT, 0:1], cnt[:, 0:NT], m.ones[:, 0:1], start=True, stop=True)
                    mm(pn[0:NT, 1:2], cnt[:, 1:NT + 1], m.ones[:, 0:1], start=True, stop=True).then_inc(pe_step, 1)
                    pe.wait_ge(tiles_in, 1)
                    mm(pn[0:NT, 2:3], upper[0:NT, 0:NT], col[:, 3:4], start=True, stop=True).then_inc(pe_step, 1)
                    pe.wait_ge(sel_in, 1)
                    mm(pn[:, 0:STEPS], n128[0:NT, :], sel[:, 1, :], start=True, stop=True)
                    mm(pc[0:1, 0:STEPS], m.ones[0:NT, 0:1], sval[:, :], start=True, stop=True).then_inc(pe_step, 1)
                    pe.wait_ge(in_x, 48)
                    for t in range(NT):
                        for k, (ps, done, free) in enumerate(((pa, A_mm, A_out), (pb, B_mm, B_out))):
                            if t >= 2:
                                pe.wait_ge(free, t - 1)
                            for c in range(2):
                                last = mm(ps[:, t % 2, :], m.xTs[:, c, t * P:(t + 1) * P], w1[:, 2 * k + c, :],
                                          start=(c == 0), stop=(c == 1))
                            last.then_inc(done, 1)

                @block.scalar
                def _(act):
                    for t in range(NT):
                        act.wait_ge(A_mm, t + 1)
                        if t >= 2:
                            act.wait_ge(A_wr[t % 2], 16 * (t // 2))
                        nc.scalar.activation(Ab[:, t % 2, :], pa[:, t % 2, :], ACT.Copy).then_inc(A_out, 1)
                        act.wait_ge(A_out, t + 1)
                        act.dma_start(A_dram[t * P:(t + 1) * P, :], Ab[:, t % 2, :]).then_inc(A_wr[t % 2], 16)
                    for k in range(2):
                        act.wait_ge(A_wr[k], 16 * (NT // 2))

        with ExitStack() as ctx:
            G = sb(ctx, "G0", [P, U, HID])
            ixr = sb(ctx, "ixr0", [P, U], U32)
            ef = sb(ctx, "ef", [ED, U, P])
            oh = sb(ctx, "oh0", [P, 4, P])
            ohT = sb(ctx, "ohT0", [P, 4, P])
            hb = sb(ctx, "hb", [P, 4, HID])
            pt = psum(ctx, "pt", [P, 2, 512])
            pz = psum(ctx, "pz", [P, 2, HID])
            pp = psum(ctx, "pp", [P, 2, 2 * HID])
            ef_in = [sem(ctx, f"ef_in{j}") for j in range(U)]
            g_in = [sem(ctx, f"g_in{j}") for j in range(U)]
            (ix_copied, gate, oh_made, turned, ohT_made, z_made, z_summed, h_made, p_made, p_added) = (
                sem(ctx, n) for n in ("ix_copied", "gate", "oh_made", "turned", "ohT_made", "z_made", "z_summed",
                                      "h_made", "p_made", "p_added"))

            with nc.Block() as block:
                @block.sync
                def _(sp):
                    regs = [sp.alloc_register(f"start_e{j}") for j in range(U)]

                    def load_ef(it):
                        load_row(sp, regs, m.start_i, it, E)
                        for j in range(U):
                            wait_step(sp, z_made, it, j, ago=U)
                            first = sp.snap(regs[j], min_val=0, max_val=E)
                            sp.dma_start(ef[:, j, :], efT[:, bass.ds(first, P)]).then_inc(ef_in[j], 16)

                    load_ef(0)
                    with sp.Fori(1, ITERS) as it:
                        load_ef(it)

                @block.gpsimd
                def _(pool):
                    def gather(it):
                        if not isinstance(it, int):
                            for j in range(U):
                                pool.wait_ge(g_in[j], it * 16)
                        pool.tensor_copy(ixr[:, :], m.src_ix[:, bass.ds(it * U, U)]).then_inc(ix_copied, 1)
                        pool.wait_ge(ix_copied, it + 1)
                        for j in range(U):
                            wait_step(pool, z_summed, it, j, ago=U)
                            pool.sem_inc(gate, 1)
                            pool.indirect_dma_start(G[:, j, :], None, A_dram,
                                                    bass.IndirectOffsetOnAxis(ap=ixr[:, j:j + 1], axis=0)
                                                    ).then_inc(g_in[j], 16)

                    gather(0)
                    with pool.Fori(1, ITERS) as it:
                        gather(it)

                @block.vector
                def _(dve):
                    regs = [dve.alloc_register(f"nt_v{j}") for j in range(U)]

                    def one_hot(it, j):
                        wait_step(dve, p_made, it, j, ago=4)
                        dve.tensor_scalar(oh[:, j % 4, :], m.iota[:, :], m.dl[:, bass.ds(it * U + j, 1)], None,
                                          ALU.is_equal).then_inc(oh_made, 1)

                    def add_rows(it, j):
                        wait_step(dve, z_made, it, j)
                        dve.wait_ge(g_in[j], (it + 1) * 16)
                        wait_step(dve, p_made, it, j, ago=4)
                        dve.tensor_tensor(hb[:, j % 4, :], pz[:, j % 2, :], G[:, j, :], ALU.add).then_inc(z_summed, 1)

                    def accumulate(it, j):
                        if j == 0:
                            load_row(dve, regs, m.nt_i, it, NT - 1)
                        nt = dve.snap(regs[j], min_val=0, max_val=NT - 1)
                        wait_step(dve, p_made, it, j)
                        wait_step(dve, p_added, it, j, ago=1)
                        a = m.agg[:, bass.ds(nt, 1), :].rearrange("p o n -> p (o n)")
                        dve.tensor_tensor(a, a, pp[:, j % 2, 0:AGW], ALU.add).then_inc(p_added, 1)

                    run_skewed(dve, [(one_hot, 0), (add_rows, 1), (accumulate, 3)])

                @block.scalar
                def _(act):
                    def copy_turned(it, j):
                        wait_step(act, turned, it, j)
                        wait_step(act, z_made, it, j, ago=4)
                        nc.scalar.activation(ohT[:, j % 4, :], pt[:, j % 2, 0:P], ACT.Copy).then_inc(ohT_made, 1)

                    def relu(it, j):
                        wait_step(act, z_summed, it, j)
                        nc.scalar.activation(hb[:, j % 4, :], hb[:, j % 4, :], ACT.Relu).then_inc(h_made, 1)

                    run_skewed(act, [(copy_turned, 0), (relu, 2)])

                @block.tensor
                def _(pe):
                    regs = [pe.alloc_register(f"nt_p{j}") for j in range(U)]

                    def turn(it, j):
                        wait_step(pe, oh_made, it, j)
                        wait_step(pe, ohT_made, it, j, ago=2)
                        pe.transpose(pt[:, j % 2, 0:P], oh[:, j % 4, :], m.ident[:, :]).then_inc(turned, 1)

                    def preact(it, j):
                        if j == 0:
                            load_row(pe, regs, m.nt_i, it, NT - 1)
                        nt = pe.snap(regs[j], min_val=0, max_val=NT - 1)
                        wait_step(pe, ohT_made, it, j)
                        wait_step(pe, z_summed, it, j, ago=2)
                        pe.wait_ge(ef_in[j], (it + 1) * 16)
                        mm(pz[:, j % 2, :], ef[:, j, :], m.w1e[:, :], start=True, stop=False)
                        mm(pz[:, j % 2, :], ohT[:, j % 4, :], m.B[:, bass.ds(nt, 1), :].rearrange("p o n -> p (o n)"),
                           start=False, stop=True).then_inc(z_made, 1)

                    def segsum(it, j):
                        wait_step(pe, h_made, it, j)
                        wait_step(pe, p_added, it, j, ago=2)
                        mm(pp[:, j % 2, 0:HID], oh[:, j % 4, :], hb[:, j % 4, :], start=True, stop=True)
                        mm(pp[:, j % 2, HID:AGW], oh[:, j % 4, :], m.ones[:, 0:1], start=True, stop=True).then_inc(p_made, 1)

                    run_skewed(pe, [(turn, 0), (preact, 1), (segsum, 2)])

        with ExitStack() as ctx:
            aT = sb(ctx, "aT", [P, 4, P])
            msg = sb(ctx, "msg", [P, HID])
            mT = sb(ctx, "mT", [P, 4, P])
            g = sb(ctx, "g", [P, HID])
            gT = sb(ctx, "gT", [P, 4, P])
            y = sb(ctx, "y", [P, D])
            st = sb(ctx, "st", [P, 16])
            eps = sb(ctx, "eps", [P, 1])
            q = [psum(ctx, f"q{k}", [P, HID]) for k in range(6)]
            pe_s, act_s, dve_s = (sem(ctx, n) for n in ("pe_s", "act_s", "dve_s"))
            PE_N, ACT_N, DVE_N = 7, 5, 10

            with nc.Block() as block:
                @block.tensor
                def _(pe):
                    def turn4(out_ps, src):
                        for c in range(4):
                            last = pe.transpose(out_ps[:, c * P:(c + 1) * P], src[:, c * P:(c + 1) * P], m.ident[:, :])
                        last.then_inc(pe_s, 1)

                    for t in range(NT):
                        if t:
                            pe.wait_ge(act_s, ACT_N * t)
                        turn4(q[0], m.agg[:, t, :])
                        pe.wait_ge(act_s, ACT_N * t + 1)
                        for c in range(4):
                            last = mm(q[1][:, :], aT[:, c, :], m.w2[:, c, :], start=(c == 0), stop=(c == 3))
                        last.then_inc(pe_s, 1)
                        pe.wait_ge(dve_s, DVE_N * t + 2)
                        turn4(q[2], msg)
                        pe.wait_ge(act_s, ACT_N * t + 2)
                        for c in range(6):
                            lhs = m.xTs[:, c, t * P:(t + 1) * P] if c < 2 else mT[:, c - 2, :]
                            last = mm(q[3][:, :], lhs, m.w3[:, c, :], start=(c == 0), stop=(c == 5))
                        last.then_inc(pe_s, 1)
                        pe.wait_ge(act_s, ACT_N * t + 3)
                        turn4(q[4], g)
                        pe.wait_ge(act_s, ACT_N * t + 4)
                        for c in range(4):
                            last = mm(q[5][:, 0:D], gT[:, c, :], m.w4[:, c, :], start=(c == 0), stop=(c == 3))
                        last.then_inc(pe_s, 1)
                        pe.wait_ge(dve_s, DVE_N * (t + 1))
                        for c in range(2):
                            last = pe.transpose(q[5][:, c * P:(c + 1) * P], m.xs[:, t, c * P:(c + 1) * P], m.ident[:, :])
                        last.then_inc(pe_s, 1)

                @block.scalar
                def _(act):
                    for t in range(NT):
                        def copy(o, i, n):
                            act.wait_ge(pe_s, PE_N * t + n)
                            nc.scalar.activation(o, i, ACT.Copy).then_inc(act_s, 1)

                        copy(aT[:, :, :].rearrange("p c n -> p (c n)"), q[0][:, :], 1)
                        copy(mT[:, :, :].rearrange("p c n -> p (c n)"), q[2][:, :], 3)
                        act.wait_ge(dve_s, DVE_N * t + 3)
                        nc.scalar.activation(g[:, :], g[:, :], ACT.Relu).then_inc(act_s, 1)
                        copy(gT[:, :, :].rearrange("p c n -> p (c n)"), q[4][:, :], 5)
                        act.wait_ge(dve_s, DVE_N * t + 8)
                        nc.scalar.activation(st[:, 9:10], st[:, 7:8], ACT.Sqrt, bias=eps[:, 0:1]).then_inc(act_s, 1)


                @block.vector
                def _(dve):
                    do = Chain(dve, dve_s)
                    do.n = 0
                    dve.memset(eps[:, :], EPS_LN)
                    for t in range(NT):
                        dve.wait_ge(pe_s, PE_N * t + 2)
                        do(dve.tensor_scalar(msg[:, :], m.b2[:, :], m.agg[:, t, HID:AGW], None, ALU.mult))
                        do(dve.tensor_tensor(msg[:, :], msg[:, :], q[1][:, :], ALU.add))
                        dve.wait_ge(pe_s, PE_N * t + 4)
                        do(dve.tensor_tensor(g[:, :], q[3][:, :], m.b3[:, :], ALU.add))
                        dve.wait_ge(pe_s, PE_N * t + 6)
                        do(dve.tensor_tensor(y[:, :], q[5][:, 0:D], m.b4[:, :], ALU.add))
                        do(dve.scalar_tensor_tensor(y[:, :], m.xs[:, t, :], 2.0, y[:, :], ALU.mult, ALU.add))
                        do(dve.bn_stats(st[:, 0:6], y[:, :]))
                        do(dve.bn_aggr(st[:, 6:8], st[:, 0:6]))
                        do(dve.memset(st[:, 8:9], 0.0))
                        dve.wait_ge(act_s, ACT_N * t + 5)
                        do(dve.reciprocal(st[:, 10:11], st[:, 9:10]))
                        do(dve.tensor_scalar(m.xs[:, t, :], y[:, :], st[:, 6:7], st[:, 10:11], ALU.subtract, ALU.mult))
                        dve.wait_ge(pe_s, PE_N * t + 7)
                        dve.tensor_copy(m.xTs[:, :, t * P:(t + 1) * P], q[5][:, 0:D].rearrange("p (c n) -> p c n", c=2))
        l0.close()

        l1 = whole.enter_context(ExitStack())
        m.acc = sb(l1, "acc", [P, NT, ROW])
        m.sdt = sb(l1, "sdt", [P, NT, R * H])
        with ExitStack() as ctx:
            wt = sb(ctx, "wt", [P, 2, R * ROW])
            wtd = sb(ctx, "wtd", [P, 2, R * H])
            wn = sb(ctx, "wn", [P, R, 2, D])
            at = sb(ctx, "at", [P, 2, 2])
            blk = sb(ctx, "blk", [P, 2, 2 * H])
            row = sb(ctx, "row", [P, 2, R * ROW])
            pr = psum(ctx, "pr", [P, 6, 512])
            pv = psum(ctx, "pv", [P, 512])
            pd = psum(ctx, "pd", [P, 512])
            w_in, blk_made, v_made, v_copied, row_mm, row_dve, row_act, d_mm, d_out, dve_c = (
                sem(ctx, n) for n in ("w_in", "blk_made", "v_made", "v_copied", "row_mm", "row_dve", "row_act", "d_mm",
                                      "d_out", "dve_c"))
            row_wr = [sem(ctx, f"row_wr{k}") for k in range(2)]
            blk0 = sem(ctx, "blk0")
            with nc.Block() as block:
                @block.sync
                def _(sp):
                    sp.dma_start(wt[:, :, :], WT.rearrange("(c p) n -> p c n", p=P)).then_inc(w_in, 16)
                    sp.dma_start(wn[:, :, :, :], Wn.rearrange("r (c p) n -> p r c n", p=P)).then_inc(w_in, 16)
                    sp.dma_start(at[:, :, :], attn).then_inc(w_in, 16)
                    for t in range(NT):
                        sp.wait_ge(row_dve, R // 2 * (t + 1))
                        sp.wait_ge(row_act, R // 2 * (t + 1))
                        sp.dma_start(T_dram.rearrange("(r t p) n -> t p r n", r=R, p=P)[t],
                                     row[:, t % 2, :].rearrange("p (r n) -> p r n", r=R)).then_inc(row_wr[t % 2], 16)
                    for k in range(2):
                        sp.wait_ge(row_wr[k], 16 * (NT // 2))

                @block.gpsimd
                def _(pool):
                    pool.memset(blk[:, :, :], 1.0).then_inc(blk0, 1)
                    v = blk[:, :, :].rearrange("p c (s h) -> p c s h", s=2)
                    pool.wait_ge(blk0, 1)
                    pool.affine_select(out=v, in_=v, compare_op=ALU.is_ge, fill=0.0, base=0,
                                       pattern=[[P, 2], [0, 2], [-HD, H]], channel_multiplier=1).then_inc(blk0, 1)
                    pool.wait_ge(blk0, 2)
                    pool.affine_select(out=v, in_=v, compare_op=ALU.is_gt, fill=0.0, base=HD,
                                       pattern=[[-P, 2], [0, 2], [HD, H]], channel_multiplier=-1).then_inc(blk0, 1)
                    pool.memset(m.acc[:, :, :], 0.0)

                @block.vector
                def _(dve):
                    do = Chain(dve, dve_c)
                    dve.wait_ge(w_in, 48)
                    dve.wait_ge(blk0, 3)
                    for c in range(2):
                        for s in range(2):
                            do(dve.tensor_scalar(blk[:, c, s * H:(s + 1) * H], blk[:, c, s * H:(s + 1) * H],
                                                 at[:, s, c:c + 1], None, ALU.mult))
                    dve.sem_inc(blk_made, 1)
                    dve.wait_ge(v_made, 1)
                    v = pv[:, 0:2 * R * 16].rearrange("p (f r n) -> p f r n", f=2, r=R)
                    do(dve.tensor_copy(wt[:, :, :].rearrange("p f (r h w) -> p f r h w", r=R, h=H)[:, 0, :, :, HD], v[:, 0, :, 0:H]))
                    do(dve.tensor_copy(wt[:, :, :].rearrange("p f (r h w) -> p f r h w", r=R, h=H)[:, 1, :, :, HD], v[:, 1, :, 0:H]))
                    do(dve.tensor_copy(wtd[:, 0, :].rearrange("p (r h) -> p r h", r=R), v[:, 0, :, H:2 * H]))
                    do(dve.tensor_copy(wtd[:, 1, :].rearrange("p (r h) -> p r h", r=R), v[:, 1, :, H:2 * H]))
                    dve.sem_inc(v_copied, 1)
                    for t in range(NT):
                        for r in range(0, R, 2):
                            n = t * R + r
                            dve.wait_ge(row_mm, n + 1)
                            if t >= 2:
                                dve.wait_ge(row_wr[t % 2], 16 * (t // 2))
                            dve.tensor_copy(row[:, t % 2, r * ROW:(r + 1) * ROW], pr[:, n % 6, 0:ROW]).then_inc(row_dve, 1)
                        dve.wait_ge(d_mm, t + 1)
                        dve.tensor_copy(m.sdt[:, t, :], pd[:, 0:R * H]).then_inc(d_out, 1)

                @block.scalar
                def _(act):
                    for t in range(NT):
                        for r in range(1, R, 2):
                            n = t * R + r
                            act.wait_ge(row_mm, n + 1)
                            if t >= 2:
                                act.wait_ge(row_wr[t % 2], 16 * (t // 2))
                            nc.scalar.activation(row[:, t % 2, r * ROW:(r + 1) * ROW], pr[:, n % 6, 0:ROW], ACT.Copy
                                                 ).then_inc(row_act, 1)

                @block.tensor
                def _(pe):
                    pe.wait_ge(w_in, 48)
                    pe.wait_ge(blk_made, 1)
                    for f in range(2):
                        for r in range(R):
                            for c in range(2):
                                last = mm(pv[:, (f * R + r) * 16:(f * R + r + 1) * 16], wn[:, r, c, f * P:(f + 1) * P],
                                          blk[:, c, :], start=(c == 0), stop=(c == 1))
                    last.then_inc(v_made, 1)
                    pe.wait_ge(v_copied, 1)
                    for t in range(NT):
                        for r in range(R):
                            n = t * R + r
                            if n >= 6:
                                pe.wait_ge((row_dve, row_act)[n % 2], (n - 6) // 2 + 1)
                            for c in range(2):
                                last = mm(pr[:, n % 6, 0:ROW], m.xTs[:, c, t * P:(t + 1) * P], wt[:, c, r * ROW:(r + 1) * ROW],
                                          start=(c == 0), stop=(c == 1))
                            last.then_inc(row_mm, 1)
                        if t:
                            pe.wait_ge(d_out, t)
                        for c in range(2):
                            last = mm(pd[:, 0:R * H], m.xTs[:, c, t * P:(t + 1) * P], wtd[:, c, :], start=(c == 0), stop=(c == 1))
                        last.then_inc(d_mm, 1)

        with ExitStack() as ctx:
            G = sb(ctx, "G1", [P, 2, GU, ROW])
            ixr = sb(ctx, "ixr1", [P, 2, GU], U32)
            oh = sb(ctx, "oh1", [P, 2, GU, P])
            ohT = sb(ctx, "ohT1", [P, 2, GU, P])
            sd8 = sb(ctx, "sd8", [P, GU, R * H])
            sc = sb(ctx, "sc", [P, 2, GU * H])
            raw = sb(ctx, "raw", [P, 2, GU * H])
            dT = sb(ctx, "dT", [P, P])
            eq = sb(ctx, "eq", [P, P + 1])
            run = sb(ctx, "run", [P, 2, P])
            rl = sb(ctx, "rl", [P, GU * H])
            cb = sb(ctx, "cb", [P, H, GU + 1])
            mb = sb(ctx, "mb", [P, H, GU + 1])
            mx = sb(ctx, "mx", [P, 2, H, GU + 1])
            av = sb(ctx, "av", [P, 2, H, GU])
            w8 = sb(ctx, "w8", [P, 2, GU * H])
            pt = psum(ctx, "pt1", [P, 2, 4, P])
            psd = psum(ctx, "psd", [P, GU, R * H])
            pq = psum(ctx, "pq", [P, 2, P])
            pm = psum(ctx, "pm", [P, 3, GU * H])
            pw = psum(ctx, "pw", [P, 2, 512])
            s = {k: sem(ctx, "s_" + k) for k in ("ixc", "gate", "oh", "turn", "ohT", "sd", "dve", "sc", "scT", "dT", "rl",
                                                 "rlT", "rlc", "mt", "mx", "mbc", "a", "ea", "sm", "w", "msg", "p",
                                                 "resc", "acc")}
            g_in = [[sem(ctx, f"g1_in{b}_{j}") for j in range(GU)] for b in range(2)]

            def run_groups(eng, group):
                group(0, 0, 0)
                with eng.Fori(0, (GROUPS - 1) // 2) as i:
                    group(i * 2 + 1, 1, i)
                    group(i * 2 + 2, 0, i + 1)

            def step_of(gi, j):
                return gi * GU + j

            def wait_count(eng, sm, v):
                if not isinstance(v, int) or v > 0:
                    eng.wait_ge(sm, v)

            def load_tiles(eng, regs, gi):
                for k in range(0, GU, U):
                    eng.load(regs[k:k + U], m.nt_i[0:1, bass.ds(gi * GU + k, U)])

            with nc.Block() as block:
                @block.gpsimd
                def _(pool):
                    def gather(gi, b, n, first):
                        if not first:
                            pool.wait_ge(s["acc"], (gi - 1) * GU)
                        pool.tensor_copy(ixr[:, b, :], m.tab_ix[:, bass.ds(gi * GU, GU)]).then_inc(s["ixc"], 1)
                        pool.wait_ge(s["ixc"], gi + 1)
                        pool.sem_inc(s["gate"], 1)
                        for j in range(GU):
                            pool.indirect_dma_start(G[:, b, j, :], None, T_dram,
                                                    bass.IndirectOffsetOnAxis(ap=ixr[:, b, j:j + 1], axis=0)
                                                    ).then_inc(g_in[b][j], 16)

                    gather(0, 0, 0, True)
                    gather(1, 1, 0, True)
                    gather(2, 0, 1, False)
                    with pool.Fori(1, (GROUPS - 1) // 2) as i:
                        gather(i * 2 + 1, 1, i, False)
                        gather(i * 2 + 2, 0, i + 1, False)

                @block.vector
                def _(dve):
                    regs = [dve.alloc_register(f"nt_w{j}") for j in range(GU)]
                    dve.memset(eq[:, :], 0.0).then_inc(s["dve"], 1)
                    dve.memset(cb[:, :, :], 0.0).then_inc(s["dve"], 1)
                    dve.memset(mx[:, :, :, :], 0.0).then_inc(s["dve"], 1)
                    dve.wait_ge(s["dve"], 3)
                    K = 11

                    def group(gi, b, n):
                        c = [3]

                        def do(ins):
                            c[0] += 1
                            ins.then_inc(s["dve"], 1)
                            dve.wait_ge(s["dve"], gi * K + c[0])

                        for j in range(GU):
                            last = dve.tensor_scalar(oh[:, b, j, :], m.iota[:, :], m.dl[:, bass.ds(step_of(gi, j), 1)], None, ALU.is_equal)
                        last.then_inc(s["oh"], 1)
                        dve.wait_ge(s["sd"], gi + 1)
                        do(dve.tensor_tensor(sd8[:, :, :].rearrange("p u (r h) -> p u r h", r=R),
                                             psd[:, :, :].rearrange("p u (r h) -> p u r h", r=R),
                                             m.emask[:, bass.ds(gi * GU, GU), :].unsqueeze(3).to_broadcast([P, GU, R, H]), ALU.mult))
                        do(dve.tensor_reduce(raw[:, 0, :].rearrange("p (u h) -> p u h", u=GU),
                                             sd8[:, :, :].rearrange("p u (r h) -> p u h r", r=R), AX.X, ALU.add))
                        for j in range(GU):
                            dve.wait_ge(g_in[b][j], (n + 1) * 16)
                        Gv = G[:, b, :, :].rearrange("p u (h w) -> p u h w", h=H)
                        do(dve.tensor_tensor(raw[:, 1, :].rearrange("p (u h) -> p u h", u=GU), Gv[:, :, :, HD],
                                             raw[:, 0, :].rearrange("p (u h) -> p u h", u=GU), ALU.add))
                        do(dve.scalar_tensor_tensor(sc[:, 0, :], raw[:, 1, :], 0.2, raw[:, 1, :], ALU.mult, ALU.max))
                        dve.tensor_scalar(sc[:, 1, :].rearrange("p (u h) -> p u h", u=GU),
                                          m.dl[:, bass.ds(gi * GU, GU)].unsqueeze(2).to_broadcast([P, GU, H]), 0.0, None, ALU.add
                                          ).then_inc(s["sc"], 1)
                        dve.wait_ge(s["dT"], gi + 1)
                        do(dve.tensor_tensor(eq[:, 1:P], dT[:, 1:P], dT[:, 0:P - 1], ALU.is_equal))
                        do(dve.tensor_tensor_scan(run[:, 0, :], eq[:, 0:P], pq[:, 0, :], 0.0, ALU.mult, ALU.max))
                        dve.scalar_tensor_tensor(run[:, 1, :], eq[:, 1:P + 1], 0.0, run[:, 0, :], ALU.is_equal, ALU.mult
                                                 ).then_inc(s["rl"], 1)
                        do(dve.tensor_scalar(cb[:, :, 1:GU + 1],
                                             m.cont[:, bass.ds(gi * GU, GU)].unsqueeze(1).to_broadcast([P, H, GU]), 0.0, None, ALU.add))
                        do(dve.tensor_copy(mb[:, :, 0:1], mx[:, 1 - b, :, GU:GU + 1]))
                        dve.wait_ge(s["mt"], gi + 1)
                        do(dve.tensor_copy(mb[:, :, 1:GU + 1], pm[:, 1, :].rearrange("p (u h) -> p h u", u=GU)))
                        dve.tensor_tensor_scan(mx[:, b, :, :].rearrange("p h u -> p (h u)"),
                                               cb[:, :, :].rearrange("p h u -> p (h u)"),
                                               mb[:, :, :].rearrange("p h u -> p (h u)"), 0.0, ALU.mult, ALU.max
                                               ).then_inc(s["mx"], 1)
                        dve.wait_ge(s["mx"], gi + 1)
                        do(dve.tensor_tensor(av[:, 0, :, :], mx[:, b, :, 0:GU], cb[:, :, 1:GU + 1], ALU.mult))
                        dve.tensor_tensor(av[:, 0, :, :], av[:, 0, :, :], mx[:, b, :, 1:GU + 1], ALU.subtract).then_inc(s["a"], 1)
                        dve.wait_ge(s["mbc"], gi + 1)
                        dve.tensor_tensor(w8[:, 0, :], sc[:, 0, :], pm[:, 2, :], ALU.subtract).then_inc(s["sm"], 1)
                        dve.wait_ge(s["w"], gi + 1)
                        do(dve.tensor_scalar(Gv[:, :, :, HD], w8[:, 1, :].rearrange("p (u h) -> p u h", u=GU), 1.0, None, ALU.min))
                        dve.tensor_tensor(Gv[:, :, :, 0:HD], Gv[:, :, :, 0:HD],
                                          Gv[:, :, :, HD:HD + 1].to_broadcast([P, GU, H, HD]), ALU.mult).then_inc(s["msg"], 1)
                        assert c[0] == K + 3
                        dve.wait_ge(s["ea"], gi + 1)
                        load_tiles(dve, regs, gi)
                        for j in range(GU):
                            nt = dve.snap(regs[j], min_val=0, max_val=NT - 1)
                            a = m.acc[:, bass.ds(nt, 1), :].rearrange("p o n -> p (o n)")
                            ah = a.rearrange("p (h w) -> p h w", h=H)
                            wait_count(dve, s["acc"], step_of(gi, j))
                            dve.tensor_tensor(ah, ah, av[:, 1, :, j:j + 1].to_broadcast([P, H, HW]), ALU.mult).then_inc(s["resc"], 1)
                            dve.wait_ge(s["resc"], step_of(gi, j) + 1)
                            dve.wait_ge(s["p"], step_of(gi, j) + 1)
                            dve.tensor_tensor(a, a, pw[:, j % 2, 0:ROW], ALU.add).then_inc(s["acc"], 1)

                    run_groups(dve, group)

                @block.scalar
                def _(act):
                    def group(gi, b, n):
                        for k in range(4):
                            act.wait_ge(s["turn"], gi * 4 + k + 1)
                            nc.scalar.activation(ohT[:, b, 4 * k:4 * k + 4, :], pt[:, k % 2, :, :], ACT.Copy).then_inc(s["ohT"], 1)
                        act.wait_ge(s["scT"], gi + 1)
                        nc.scalar.activation(dT[:, :], pq[:, 1, :], ACT.Copy).then_inc(s["dT"], 1)
                        act.wait_ge(s["rlT"], gi + 1)
                        nc.scalar.activation(rl[:, :], pm[:, 0, :], ACT.Copy).then_inc(s["rlc"], 1)
                        act.wait_ge(s["a"], gi + 1)
                        nc.scalar.activation(av[:, 1, :, :], av[:, 0, :, :], ACT.Exp).then_inc(s["ea"], 1)
                        act.wait_ge(s["sm"], gi + 1)
                        nc.scalar.activation(w8[:, 1, :], w8[:, 0, :], ACT.Exp).then_inc(s["w"], 1)

                    run_groups(act, group)

                @block.tensor
                def _(pe):
                    regs = [pe.alloc_register(f"nt_q{j}") for j in range(GU)]

                    def group(gi, b, n):
                        load_tiles(pe, regs, gi)
                        pe.wait_ge(s["oh"], gi + 1)
                        for k in range(4):
                            wait_count(pe, s["ohT"], gi * 4 + k - 1)
                            for j in range(4):
                                last = pe.transpose(pt[:, k % 2, j, :], oh[:, b, 4 * k + j, :], m.ident[:, :])
                            last.then_inc(s["turn"], 1)
                        for j in range(GU):
                            if j % 4 == 0:
                                pe.wait_ge(s["ohT"], gi * 4 + j // 4 + 1)
                            nt = pe.snap(regs[j], min_val=0, max_val=NT - 1)
                            last = mm(psd[:, j, :], ohT[:, b, j, :], m.sdt[:, bass.ds(nt, 1), :].rearrange("p o n -> p (o n)"),
                                      start=True, stop=True)
                        last.then_inc(s["sd"], 1)
                        pe.wait_ge(s["sc"], gi + 1)
                        pe.transpose(pq[:, 0, :], sc[:, 0, :], m.ident[:, :])
                        pe.transpose(pq[:, 1, :], sc[:, 1, :], m.ident[:, :]).then_inc(s["scT"], 1)
                        pe.wait_ge(s["rl"], gi + 1)
                        pe.transpose(pm[:, 0, :], run[:, 1, :], m.ident[:, :]).then_inc(s["rlT"], 1)
                        pe.wait_ge(s["rlc"], gi + 1)
                        for j in range(GU):
                            last = mm(pm[:, 1, j * H:(j + 1) * H], oh[:, b, j, :], rl[:, j * H:(j + 1) * H], start=True, stop=True)
                        last.then_inc(s["mt"], 1)
                        pe.wait_ge(s["mx"], gi + 1)
                        for j in range(GU):
                            last = mm(pm[:, 2, j * H:(j + 1) * H], ohT[:, b, j, :], mx[:, b, :, j + 1], start=True, stop=True)
                        last.then_inc(s["mbc"], 1)
                        pe.wait_ge(s["msg"], gi + 1)
                        for j in range(GU):
                            wait_count(pe, s["acc"], step_of(gi, j) - 1)
                            mm(pw[:, j % 2, 0:ROW], oh[:, b, j, :], G[:, b, j, :], start=True, stop=True).then_inc(s["p"], 1)

                    run_groups(pe, group)

        with ExitStack() as ctx:
            den = sb(ctx, "den", [P, 2, NT, H])
            y = sb(ctx, "yf", [P, NT, D])
            st = sb(ctx, "stf", [P, NT, 6])
            mv = sb(ctx, "mv", [P, NT, 2])
            eps = sb(ctx, "epsf", [P, 1])
            std = sb(ctx, "std", [P, 2, NT])
            f_dve, f_act, f_out, ready, sq = (sem(ctx, n) for n in ("f_dve", "f_act", "f_out", "ready", "sq"))
            with nc.Block() as block:
                @block.vector
                def _(dve):
                    do = Chain(dve, f_dve)
                    av = m.acc[:, :, :].rearrange("p t (h w) -> p t h w", h=H)
                    do(dve.memset(eps[:, :], EPS_LN))
                    do(dve.tensor_scalar(den[:, 0, :, :], av[:, :, :, HD], EPS_DEN, None, ALU.add))
                    do(dve.reciprocal(den[:, 1, :, :], den[:, 0, :, :]))
                    for t in range(NT):
                        do(dve.tensor_tensor(y[:, t, :].rearrange("p (h w) -> p h w", h=H), av[:, t, :, 0:HD],
                                             den[:, 1, t, :].unsqueeze(2).to_broadcast([P, H, HD]), ALU.mult))
                        do(dve.tensor_tensor(y[:, t, :], y[:, t, :], m.xs[:, t, :], ALU.add))
                        do(dve.bn_stats(st[:, t, :], y[:, t, :]))
                        do(dve.bn_aggr(mv[:, t, :], st[:, t, :]))
                    dve.sem_inc(ready, 1)
                    dve.wait_ge(sq, 1)
                    do(dve.reciprocal(std[:, 1, :], std[:, 0, :]))
                    for t in range(NT):
                        dve.tensor_scalar(y[:, t, :], y[:, t, :], mv[:, t, 0:1], std[:, 1, t:t + 1], ALU.subtract, ALU.mult
                                          ).then_inc(f_act, 1)

                @block.scalar
                def _(act):
                    act.wait_ge(ready, 1)
                    nc.scalar.activation(std[:, 0, :], mv[:, :, 1], ACT.Sqrt, bias=eps[:, 0:1]).then_inc(sq, 1)

                @block.sync
                def _(sp):
                    sp.wait_ge(f_act, NT)
                    sp.dma_start(out[0:(NT - 1) * P, :].rearrange("(t p) n -> p t n", p=P), y[:, 0:NT - 1, :]).then_inc(f_out, 16)
                    sp.dma_start(out[(NT - 1) * P:N, :], y[0:N - (NT - 1) * P, NT - 1, :]).then_inc(f_out, 16)
                    sp.wait_ge(f_out, 32)


def kernel(**inputs):
    import numpy as np
    import concourse.bacc as bacc
    from concourse.bass_utils import run_bass_kernel_spmd

    a = {k: np.asarray(v) for k, v in inputs.items()}
    pad_e = EP - E
    x = np.pad(a["x"], ((0, NP - N), (0, 0)))
    src, dst, typ = (a[k].astype(np.int32) for k in ("src", "dst", "edge_type_8"))
    dst = np.concatenate([dst, np.full(pad_e, PAD_DST, np.int32)])
    meta = np.stack([np.pad(src, (0, pad_e)), dst, np.pad(typ, (0, pad_e)), np.zeros(EP, np.int32)], axis=1)
    W = a["L1_gnn_W"]
    WT = np.pad(W.reshape(R, H, HD, D).transpose(3, 0, 1, 2), ((0, 0), (0, 0), (0, 0), (0, 1))).reshape(D, R * ROW)
    attn = np.stack([a["L1_gnn_attn_src"].reshape(2, P), a["L1_gnn_attn_dst"].reshape(2, P)]).transpose(2, 0, 1)
    arrays = {
        "x": x, "xT": x.T, "dst": dst[:P * CNT].reshape(P, CNT), "meta": meta,
        "efT": np.pad(a["edge_attr_64"].T, ((0, 0), (0, pad_e))),
        "W1": a["L0_gnn_W1"], "b1": a["L0_gnn_b1"], "W2": a["L0_gnn_W2"], "b2": a["L0_gnn_b2"],
        "W3": a["L0_gnn_W3"], "b3": a["L0_gnn_b3"], "W4": a["L0_gnn_W4"], "b4": a["L0_gnn_b4"],
        "WT": WT, "Wn": W, "attn": attn,
    }
    arrays = {f"in_{k}": np.ascontiguousarray(v) for k, v in arrays.items()}
    nc = bacc.Bacc("TRN2", target_bir_lowering=False, num_devices=1)
    args = [nc.dram_tensor(k, v.shape, mybir.dt.from_np(v.dtype), kind="ExternalInput").ap() for k, v in arrays.items()]
    out = nc.dram_tensor("out", (N, D), F32, kind="ExternalOutput").ap()
    gnn_kernel(nc, *args, out)
    return run_bass_kernel_spmd(nc, [arrays], core_ids=[0]).results[0]["out"]
```

```python
from contextlib import ExitStack

import concourse.bass as bass
from concourse import mybir

F32 = mybir.dt.float32
I32 = mybir.dt.int32
U32 = mybir.dt.uint32
BF16 = mybir.dt.bfloat16
ALU = mybir.AluOpType
ACT = mybir.ActivationFunctionType
AX = mybir.AxisListType

P = 128
N, E, D, ED, HID, R, H = 2500, 40000, 256, 64, 512, 8, 8
HD = D // H
HW = HD + 1
ROW = H * HW
NT = -(-N // P)
NP = NT * P
U = 16
GU = 16
STEPS = -(-(-(-E // P) + NT) // GU) * GU
ITERS = STEPS // U
GROUPS = STEPS // GU
TSTEPS = STEPS + U
GR = 8
CE = 4
EP = E + 192
CNT = -(-E // P)
TILES_E = EP // P
SC = 8
PAD_DST = 4095
EPS_LN = 1e-5
EPS_DEN = 1e-12


class Chain:

    def __init__(self, eng, sem):
        self.eng, self.sem, self.n = eng, sem, 0

    def __call__(self, ins):
        self.n += 1
        ins.then_inc(self.sem, 1)
        self.eng.wait_ge(self.sem, self.n)


def wait_step(eng, sem, it, j, ago=0):
    v = it * U + (j + 1 - ago)
    if not isinstance(v, int) or v > 0:
        eng.wait_ge(sem, v)


def run_skewed(eng, stages):
    def body(it):
        for j in range(U):
            for f, lag in stages:
                if j >= lag:
                    f(it, j - lag)
                elif not isinstance(it, int):
                    f(it - 1, j - lag + U)
    body(0)
    with eng.Fori(1, ITERS) as it:
        body(it)
    for j in range(max(lag for _, lag in stages)):
        for f, lag in stages:
            if j < lag:
                f(ITERS - 1, j - lag + U)


def load_row(eng, regs, row, it, top):
    eng.load(regs, row[0:1, bass.ds(it * U, U)])


def over_tiles(eng, tile):
    tile(0)
    with eng.Fori(1, TILES_E) as t:
        tile(t)


def edge_order(nc, m, sb, psum, sem, whole, dst, dst_tiles, meta, ef, efT, meta_s, ef_s):
    flag = sb(whole, "flag", [1, 1], I32)
    with ExitStack() as ctx:
        pair = sb(ctx, "pair", [P, 2, CNT], I32)
        fall = sb(ctx, "fall", [P, CNT])
        falls = sb(ctx, "falls", [P, 1])
        ones = sb(ctx, "ones_s", [P, 1])
        fs = psum(ctx, "fs", [1, 1])
        pair_in, falls_in, summed = (sem(whole, n) for n in ("pair_in", "falls_in", "falls_summed"))
        with nc.Block() as block:
            @block.sync
            def _(sp):
                for k in range(2):
                    sp.dma_start(pair[:, k, :], dst[k:P * CNT + k, :].rearrange("(p c) o -> p (c o)", p=P)).then_inc(pair_in, 16)

            @block.vector
            def _(dve):
                dve.memset(ones[:, :], 1.0).then_inc(falls_in, 1)
                dve.wait_ge(pair_in, 32)
                dve.scalar_tensor_tensor(fall[:, :], pair[:, 0, :], 1.0, pair[:, 1, :], ALU.mult, ALU.is_gt,
                                         accum_out=falls[:, :]).then_inc(falls_in, 1)
                dve.wait_ge(summed, 1)
                dve.tensor_scalar(flag[:, :], fs[:, :], 0.0, None, ALU.is_gt)

            @block.tensor
            def _(pe):
                pe.wait_ge(falls_in, 2)
                nc.tensor.matmul(fs[:, :], falls[:, :], ones[:, :], start=True, stop=True).then_inc(summed, 1)

    with ExitStack() as ctx:
        key_i = sb(ctx, "key_i", [P, TILES_E], I32)
        key = sb(ctx, "key", [P, 2, TILES_E])
        wide = sb(ctx, "wide", [P, EP])
        stage = sb(ctx, "stage", [P, EP // SC], I32)
        hit = sb(ctx, "hit", [P, EP // SC], BF16)
        lower = sb(ctx, "lower", [P, P])
        part = sb(ctx, "part", [P, SC + 1])
        place = sb(ctx, "place", [P, TILES_E])
        place_i = sb(ctx, "place_i", [P, TILES_E], U32)
        place_now = sb(ctx, "place_now", [P, 1], U32)
        meta_t = sb(ctx, "meta_t", [P, 4], I32)
        (keys_in, stage_in, staged, lower_in, ranked, places, m_in, m_ix, m_out, e_in, e_ix, e_rows, e_turned, e_col, e_out, sgate) = (
            sem(whole, "so_" + n) for n in ("keys_in", "stage_in", "staged", "lower_in", "ranked", "places", "m_in", "m_ix",
                                   "m_out", "e_in", "e_ix", "e_rows", "e_turned", "e_col", "e_out", "gate"))
        ef_rows = sb(ctx, "ef_rows", [P, P])
        ef_cols = sb(ctx, "ef_cols", [P, P])
        identS = sb(ctx, "identS", [P, P])
        pe_t = psum(ctx, "pe_t", [P, 512])
        W = EP // SC
        RK = SC + 4

        with nc.Block() as block:
            @block.sync
            def _(sp):
                unsorted = sp.value_load(flag[0:1, 0:1], min_val=0, max_val=1)
                with sp.If(unsorted > 0):
                    sp.dma_start(key_i[:, :], dst_tiles).then_inc(keys_in, 16)
                    for c in range(SC):
                        if c:
                            sp.wait_ge(staged, c)
                        sp.dma_start(stage[:, :], dst[c * W:(c + 1) * W, :].rearrange("w o -> (w o)").partition_broadcast(P)
                                     ).then_inc(stage_in, 16)
                    sp.wait_ge(places, 1)
                    def tile(t):
                        if not isinstance(t, int):
                            sp.wait_ge(m_out, t * 16)
                        sp.sem_inc(sgate, 1)
                        sp.dma_start(meta_t[:, :], meta[bass.ds(t * P, P), :]).then_inc(m_in, 16)
                    over_tiles(sp, tile)
                    def tile(t):
                        if not isinstance(t, int):
                            sp.wait_ge(e_ix, t)
                        sp.sem_inc(sgate, 1)
                        sp.wait_ge(m_out, TILES_E * 16)
                        sp.dma_start(meta_t[:, :], meta_s[bass.ds(t * P, P), :]).then_inc(e_in, 16)
                        sp.wait_ge(e_col, t + 1)
                        sp.sem_inc(sgate, 1)
                        for half in range(2):
                            sp.dma_start(ef_s[half * ED:(half + 1) * ED, bass.ds(t * P, P)], ef_cols[0:ED, :]).then_inc(e_out, 16)
                    over_tiles(sp, tile)
                    sp.wait_ge(e_out, TILES_E * 32)

            @block.vector
            def _(dve):
                unsorted = dve.value_load(flag[0:1, 0:1], min_val=0, max_val=1)
                with dve.If(unsorted > 0):
                    dve.wait_ge(keys_in, 16)
                    dve.tensor_copy(key[:, 0, :], key_i[:, :]).then_inc(ranked, 1)
                    dve.tensor_scalar(key[:, 1, :], key_i[:, :], 0.25, None, ALU.add).then_inc(ranked, 1)
                    for c in range(SC):
                        dve.wait_ge(stage_in, (c + 1) * 16)
                        dve.tensor_scalar(wide[:, c * W:(c + 1) * W], stage[:, :], 0.25, None, ALU.add).then_inc(staged, 1)
                    dve.wait_ge(lower_in, 4)
                    dve.wait_ge(staged, SC)
                    dve.wait_ge(ranked, 2)
                    dve.memset(ef_rows[:, :], 0.0).then_inc(ranked, 1)
                    def tile(t):
                        own = wide[:, bass.ds(t * P, P)]
                        for c in range(SC):
                            dve.wait_ge(ranked, t * RK + (c + 3))
                            dve.tensor_scalar(hit[:, :], wide[:, c * W:(c + 1) * W], key[:, 0, bass.ds(t, 1)], None,
                                              ALU.is_lt, ALU.add, accum_out=part[:, c:c + 1]).then_inc(ranked, 1)
                        dve.wait_ge(ranked, t * RK + (SC + 3))
                        dve.scalar_tensor_tensor(hit[:, 0:P], own, key[:, 1, bass.ds(t, 1)], lower[:, :],
                                                 ALU.is_equal, ALU.mult, accum_out=part[:, SC:SC + 1]).then_inc(ranked, 1)
                        dve.wait_ge(ranked, t * RK + (SC + 4))
                        dve.tensor_scalar(own, own, -0.5, None, ALU.add).then_inc(ranked, 1)
                        dve.wait_ge(ranked, t * RK + (SC + 5))
                        dve.tensor_reduce(place[:, bass.ds(t, 1)], part[:, :], AX.X, ALU.add).then_inc(ranked, 1)
                        dve.wait_ge(ranked, t * RK + (SC + 6))
                        dve.sem_inc(ranked, 1)
                    over_tiles(dve, tile)
                    dve.wait_ge(ranked, TILES_E * RK + 3)
                    dve.tensor_copy(place_i[:, :], place[:, :]).then_inc(places, 1)

            @block.gpsimd
            def _(pool):
                unsorted = pool.value_load(flag[0:1, 0:1], min_val=0, max_val=1)
                with pool.If(unsorted > 0):
                    pool.memset(lower[:, :], 1.0).then_inc(lower_in, 1)
                    pool.memset(identS[:, :], 0.0).then_inc(lower_in, 1)
                    pool.wait_ge(lower_in, 2)
                    pool.affine_select(out=lower[:, :], in_=lower[:, :], compare_op=ALU.is_gt, fill=0.0,
                                       base=0, pattern=[[-1, P]], channel_multiplier=1).then_inc(lower_in, 1)
                    pool.affine_select(out=identS[:, :], in_=identS[:, :], compare_op=ALU.not_equal, fill=1.0,
                                       base=0, pattern=[[-1, P]], channel_multiplier=1).then_inc(lower_in, 1)
                    pool.wait_ge(places, 1)
                    def tile(t):
                        pool.wait_ge(m_in, (t + 1) * 16)
                        pool.sem_inc(sgate, 1)
                        if not isinstance(t, int):
                            pool.wait_ge(m_out, t * 16)
                        pool.sem_inc(sgate, 1)
                        pool.tensor_copy(place_now[:, :], place_i[:, bass.ds(t, 1)]).then_inc(m_ix, 1)
                        pool.wait_ge(m_ix, t + 1)
                        pool.sem_inc(sgate, 1)
                        pool.indirect_dma_start(meta_s, bass.IndirectOffsetOnAxis(ap=place_now[:, 0:1], axis=0),
                                                meta_t[:, :], None).then_inc(m_out, 16)
                    over_tiles(pool, tile)
                    pool.wait_ge(m_out, TILES_E * 16)
                    def tile(t):
                        pool.wait_ge(e_in, (t + 1) * 16)
                        pool.sem_inc(sgate, 1)
                        if not isinstance(t, int):
                            pool.wait_ge(e_turned, t)
                        pool.sem_inc(sgate, 1)
                        pool.tensor_copy(place_now[:, :], meta_t[:, 3:4]).then_inc(e_ix, 1)
                        pool.wait_ge(e_ix, t + 1)
                        pool.sem_inc(sgate, 1)
                        pool.indirect_dma_start(ef_rows[:, 0:ED], None, ef,
                                                bass.IndirectOffsetOnAxis(ap=place_now[:, 0:1], axis=0)).then_inc(e_rows, 16)
                    over_tiles(pool, tile)

            @block.tensor
            def _(pe):
                unsorted = pe.value_load(flag[0:1, 0:1], min_val=0, max_val=1)
                with pe.If(unsorted > 0):
                    pe.wait_ge(lower_in, 4)
                    pe.wait_ge(ranked, 3)
                    def tile(t):
                        pe.wait_ge(e_rows, (t + 1) * 16)
                        if not isinstance(t, int):
                            pe.wait_ge(e_col, t)
                        pe.transpose(pe_t[:, 0:P], ef_rows[:, :], identS[:, :]).then_inc(e_turned, 1)
                    over_tiles(pe, tile)

            @block.scalar
            def _(act):
                unsorted = act.value_load(flag[0:1, 0:1], min_val=0, max_val=1)
                with act.If(unsorted > 0):
                    def tile(t):
                        act.wait_ge(e_turned, t + 1)
                        if not isinstance(t, int):
                            act.wait_ge(e_out, t * 32)
                        nc.scalar.activation(ef_cols[:, :], pe_t[:, 0:P], ACT.Copy).then_inc(e_col, 1)
                    over_tiles(act, tile)
    return flag


def gnn_kernel(nc, x, xT, dst, dst_tiles, meta, ef_rows, efT, W1, b1, W2T, b2, W3, b3, W4, b4, WT, Wn, attn, out):
    A_dram = nc.dram_tensor("A_table", (NP, HID), F32, kind="Internal").ap()
    T_dram = nc.dram_tensor("L1_table", (R * NP, ROW), F32, kind="Internal").ap()
    mm = nc.tensor.matmul

    class Mem:
        pass

    m = Mem()
    with ExitStack() as whole:
        def sb(ctx, name, shape, dt=F32):
            return ctx.enter_context(nc.sbuf_tensor(name, shape, dt))

        def psum(ctx, name, shape):
            return ctx.enter_context(nc.psum_tensor(name, shape, F32))

        done_with = []

        def sem(ctx, name):
            handle = ctx.enter_context(nc.semaphore(name))
            done_with.append(handle)
            return handle

        meta_s = nc.dram_tensor("meta_sorted", (EP, 4), I32, kind="Internal").ap()
        efT_s = nc.dram_tensor("efT_sorted", (2 * ED, EP), F32, kind="Internal").ap()
        flag = edge_order(nc, m, sb, psum, lambda ctx, name: ctx.enter_context(nc.semaphore(name)), whole, dst, dst_tiles, meta, ef_rows, efT, meta_s, efT_s)

        def gather_sem(name):
            return whole.enter_context(nc.semaphore(name))

        m.ident = sb(whole, "ident", [P, P])
        m.iota = sb(whole, "iota", [P, P])
        m.ones = sb(whole, "ones", [P, P])
        m.xs = sb(whole, "xs", [P, NT, D])
        m.xTs = sb(whole, "xTs", [P, 2, NP])
        m.dl = sb(whole, "dl", [P, TSTEPS])
        m.tab_ix = sb(whole, "tab_ix", [P, TSTEPS], U32)
        m.emask = sb(whole, "emask", [P, TSTEPS, R], BF16)
        m.cont = sb(whole, "cont", [P, TSTEPS])
        m.nt_i = sb(whole, "nt_i", [1, TSTEPS], I32)
        m.start_i = sb(whole, "start_i", [1, TSTEPS], I32)

        m.ntb = sb(whole, "ntb", [P, TSTEPS])
        m.iota_r = sb(whole, "iota_r", [P, R])
        m.degs = sb(whole, "degs", [P, TSTEPS])
        m.deg = sb(whole, "deg", [P, NT])

        l0 = whole.enter_context(ExitStack())
        m.agg = sb(l0, "agg", [P, NT, HID])
        l0_edges = l0.enter_context(ExitStack())
        m.w1e = sb(l0_edges, "w1e", [P, 2, HID], BF16)
        m.B = sb(l0_edges, "B", [P, NT, 3, HID], BF16)

        with ExitStack() as ctx:
            w1 = sb(ctx, "w1", [P, 4, HID])
            b1b = sb(ctx, "b1b", [P, HID])
            w1f = sb(ctx, "w1f", [P, 2, HID])
            w1p = sb(ctx, "w1p", [P, 3, HID], BF16)
            Ab = sb(ctx, "Ab", [P, 2, HID])
            dsti = sb(ctx, "dsti", [P, CNT], I32)
            dstf = sb(ctx, "dstf", [P, CNT])
            below = sb(ctx, "below", [P, CNT])
            cnt = sb(ctx, "cnt", [P, NT + 1])
            upper = sb(ctx, "upper", [P, P])
            n128 = sb(ctx, "n128", [P, P])
            steps_f = sb(ctx, "steps_f", [P, TSTEPS])
            col = sb(ctx, "col", [NT, 8])
            coli = sb(ctx, "coli", [NT, 2], I32)
            sel = sb(ctx, "sel", [NT, 2, TSTEPS])
            sval = sb(ctx, "sval", [NT, TSTEPS])
            Bf = sb(ctx, "Bf", [P, 2, 2, HID])
            pa = psum(ctx, "pa", [P, 2, HID])
            pb = psum(ctx, "pb", [P, 2, HID])
            pc = psum(ctx, "pc", [P, HID])
            pn = psum(ctx, "pn", [P, HID])
            in_dst = sem(ctx, "in_dst")
            in_x = sem(ctx, "in_x")
            in_rest = sem(ctx, "in_rest")
            in_w1e = sem(ctx, "in_w1e")
            w1_parts = sem(ctx, "w1_parts")
            set0 = sem(ctx, "set0")
            consts = sem(ctx, "consts")
            dve_done = sem(ctx, "dve_done")
            counted = sem(ctx, "counted")
            tiles_in = sem(ctx, "tiles_in")
            sel_in = sem(ctx, "sel_in")
            pe_step = sem(ctx, "pe_step")
            split = [sem(ctx, f"split{k}") for k in range(4)]
            A_mm, A_out, B_mm, B_out = (sem(ctx, n) for n in ("A_mm", "A_out", "B_mm", "B_out"))
            A_wr = [sem(ctx, f"A_wr{k}") for k in range(2)]

            with nc.Block() as block:
                @block.sync
                def _(sp):
                    sp.dma_start(dsti[:, :], dst[0:P * CNT, :].rearrange("(p c) o -> p (c o)", p=P)).then_inc(in_dst, 16)
                    sp.dma_start(m.xTs[:, :, :], xT.rearrange("(c p) n -> p c n", p=P)).then_inc(in_x, 16)
                    sp.dma_start(w1[:, :, :], W1[0:2 * D, :].rearrange("(c p) n -> p c n", p=P)).then_inc(in_x, 16)
                    sp.dma_start(b1b[:, :], b1.partition_broadcast(P)).then_inc(in_x, 16)
                    for half in range(2):
                        sp.dma_start(w1f[half * ED:(half + 1) * ED, 0, :], W1[2 * D:2 * D + ED, :]).then_inc(in_w1e, 16)
                    sp.dma_start(m.xs[:, :, :], x.rearrange("(t p) n -> p t n", p=P)).then_inc(in_rest, 16)
                    sp.wait_ge(in_rest, 16)

                @block.gpsimd
                def _(pool):
                    pool.memset(m.ident[:, :], 0.0).then_inc(set0, 1)
                    pool.memset(upper[:, :], 1.0).then_inc(set0, 1)
                    for t, pattern, mult in ((m.iota, [[1, P]], 0), (n128, [[0, P]], P), (steps_f, [[1, TSTEPS]], 0),
                                             (m.iota_r, [[1, R]], 0)):
                        pool.iota(t[:, :], pattern, base=0, channel_multiplier=mult,
                                  allow_small_or_imprecise_dtypes=True).then_inc(consts, 1)
                    pool.memset(m.ones[:, :], 1.0).then_inc(consts, 1)
                    pool.wait_ge(set0, 2)
                    pool.affine_select(out=m.ident[:, :], in_=m.ident[:, :], compare_op=ALU.not_equal, fill=1.0,
                                       base=0, pattern=[[-1, P]], channel_multiplier=1).then_inc(consts, 1)
                    pool.affine_select(out=upper[:, :], in_=upper[:, :], compare_op=ALU.is_gt, fill=0.0,
                                       base=0, pattern=[[1, P]], channel_multiplier=-1).then_inc(consts, 1)
                    pool.memset(m.agg[:, :, :], 0.0).then_inc(consts, 1)

                @block.vector
                def _(dve):
                    do = Chain(dve, dve_done)
                    dve.wait_ge(in_dst, 16)
                    do(dve.tensor_copy(dstf[:, :], dsti[:, :]))
                    do(dve.memset(cnt[:, 0:1], 0.0))
                    for n in range(1, NT + 1):
                        do(dve.tensor_scalar(below[:, :], dstf[:, :], float(P * n), None, ALU.is_lt, ALU.add,
                                             accum_out=cnt[:, n:n + 1]))
                    dve.sem_inc(counted, 1)
                    dve.wait_ge(pe_step, 1)
                    do(dve.tensor_copy(col[:, 0:2], pn[0:NT, 0:2]))
                    do(dve.tensor_tensor(col[:, 2:3], col[:, 1:2], col[:, 0:1], ALU.subtract))
                    do(dve.tensor_scalar(coli[:, 0:1], col[:, 2:3], float(P - 1), None, ALU.add))
                    do(dve.tensor_scalar(coli[:, 1:2], coli[:, 0:1], 7, None, ALU.arith_shift_right))
                    do(dve.tensor_copy(col[:, 3:4], coli[:, 1:2]))
                    dve.sem_inc(tiles_in, 1)
                    dve.wait_ge(pe_step, 2)
                    do(dve.tensor_copy(col[:, 4:5], pn[0:NT, 2:3]))
                    do(dve.tensor_tensor(col[:, 5:6], col[:, 4:5], col[:, 3:4], ALU.add))
                    do(dve.tensor_scalar(col[:, 6:7], col[:, 4:5], float(-P), float(-E), ALU.mult, ALU.add))
                    do(dve.tensor_tensor(col[:, 7:8], col[:, 6:7], col[:, 0:1], ALU.add))
                    dve.wait_ge(consts, 8)
                    do(dve.tensor_scalar(sel[:, 0, :], steps_f[0:NT, :], col[:, 4:5], None, ALU.is_ge))
                    do(dve.scalar_tensor_tensor(sel[:, 1, :], steps_f[0:NT, :], col[:, 5:6], sel[:, 0, :], ALU.is_lt, ALU.mult))
                    do(dve.tensor_scalar(sval[:, :], steps_f[0:NT, :], float(P), col[:, 7:8], ALU.mult, ALU.add))
                    do(dve.tensor_tensor(sval[:, :], sval[:, :], sel[:, 1, :], ALU.mult))
                    dve.sem_inc(sel_in, 1)
                    dve.wait_ge(pe_step, 3)
                    do(dve.tensor_copy(m.ntb[:, :], pn[:, 0:TSTEPS]))
                    do(dve.tensor_scalar(m.nt_i[:, :], m.ntb[0:1, :], 1.0 / P, None, ALU.mult))
                    do(dve.tensor_scalar(m.start_i[:, :], pc[0:1, 0:TSTEPS], float(E), None, ALU.add))
                    do(dve.memset(m.cont[:, 0:1], 0.0))
                    do(dve.tensor_tensor(m.cont[:, 1:TSTEPS], m.ntb[:, 1:TSTEPS], m.ntb[:, 0:TSTEPS - 1], ALU.is_equal))
                    dve.wait_ge(in_x, 48)
                    for t in range(NT):
                        dve.wait_ge(B_mm, t + 1)
                        dve.tensor_tensor(Bf[:, t % 2, 0, :], pb[:, t % 2, :], b1b[:, :], ALU.add).then_inc(B_out, 1)
                        dve.wait_ge(split[0], t + 1)
                        dve.tensor_tensor(Bf[:, t % 2, 1, :], Bf[:, t % 2, 0, :], m.B[:, t, 0, :], ALU.subtract).then_inc(split[1], 1)
                        dve.wait_ge(split[2], t + 1)
                        dve.tensor_tensor(m.B[:, t, 2, :], Bf[:, t % 2, 1, :], m.B[:, t, 1, :], ALU.subtract)
                    wp = Chain(dve, w1_parts)
                    dve.wait_ge(in_w1e, 32)
                    wp(dve.tensor_copy(w1p[:, 0, :], w1f[:, 0, :]))
                    wp(dve.tensor_tensor(w1f[:, 1, :], w1f[:, 0, :], w1p[:, 0, :], ALU.subtract))
                    wp(dve.tensor_copy(w1p[:, 1, :], w1f[:, 1, :]))
                    wp(dve.tensor_tensor(w1p[:, 2, :], w1f[:, 1, :], w1p[:, 1, :], ALU.subtract))
                    for half, (a, b) in enumerate(((0, 2), (1, 0))):
                        ps = slice(half * ED, (half + 1) * ED)
                        dve.tensor_copy(m.w1e[ps, 0, :], w1p[ps, a, :])
                        dve.tensor_copy(m.w1e[ps, 1, :], w1p[ps, b, :])

                @block.tensor
                def _(pe):
                    pe.wait_ge(consts, 8)
                    pe.wait_ge(counted, 1)
                    mm(pn[0:NT, 0:1], cnt[:, 0:NT], m.ones[:, 0:1], start=True, stop=True)
                    mm(pn[0:NT, 1:2], cnt[:, 1:NT + 1], m.ones[:, 0:1], start=True, stop=True).then_inc(pe_step, 1)
                    pe.wait_ge(tiles_in, 1)
                    mm(pn[0:NT, 2:3], upper[0:NT, 0:NT], col[:, 3:4], start=True, stop=True).then_inc(pe_step, 1)
                    pe.wait_ge(sel_in, 1)
                    mm(pn[:, 0:TSTEPS], n128[0:NT, :], sel[:, 1, :], start=True, stop=True)
                    mm(pc[0:1, 0:TSTEPS], m.ones[0:NT, 0:1], sval[:, :], start=True, stop=True).then_inc(pe_step, 1)
                    pe.wait_ge(in_x, 48)
                    for t in range(NT):
                        for k, (ps, done, free) in enumerate(((pa, A_mm, A_out), (pb, B_mm, B_out))):
                            if t >= 2:
                                pe.wait_ge(free, t - 1)
                            for c in range(2):
                                last = mm(ps[:, t % 2, :], m.xTs[:, c, t * P:(t + 1) * P], w1[:, 2 * k + c, :],
                                          start=(c == 0), stop=(c == 1))
                            last.then_inc(done, 1)

                @block.scalar
                def _(act):
                    for t in range(NT):
                        act.wait_ge(A_mm, t + 1)
                        if t >= 2:
                            act.wait_ge(A_wr[t % 2], 16 * (t // 2))
                        nc.scalar.activation(Ab[:, t % 2, :], pa[:, t % 2, :], ACT.Copy).then_inc(A_out, 1)
                        act.wait_ge(A_out, t + 1)
                        act.dma_start(A_dram[t * P:(t + 1) * P, :], Ab[:, t % 2, :]).then_inc(A_wr[t % 2], 16)
                        act.wait_ge(B_out, t + 1)
                        nc.scalar.activation(m.B[:, t, 0, :], Bf[:, t % 2, 0, :], ACT.Copy).then_inc(split[0], 1)
                        act.wait_ge(split[1], t + 1)
                        nc.scalar.activation(m.B[:, t, 1, :], Bf[:, t % 2, 1, :], ACT.Copy).then_inc(split[2], 1)
                    for k in range(2):
                        act.wait_ge(A_wr[k], 16 * (NT // 2))

        with ExitStack() as ctx:
            meta_b = sb(ctx, "meta_b", [P, U, 4], I32)
            G = sb(ctx, "G0", [P, GR, HID])
            ixr = sb(ctx, "ixr0", [P, U], U32)
            ef = sb(ctx, "ef", [P, U, P])
            ep = sb(ctx, "ep", [P, 3, 2, CE * P], BF16)
            er = sb(ctx, "er", [P, CE * P])
            oh = sb(ctx, "oh0", [P, 8, P])
            ohT = sb(ctx, "ohT0", [P, 4, P], BF16)
            hb = sb(ctx, "hb", [P, 4, HID])
            pt = psum(ctx, "pt", [P, 2, 512])
            pz = psum(ctx, "pz", [P, 2, HID])
            pp = psum(ctx, "pp", [P, 2, HID])
            sum_deg = sem(ctx, "sum_deg")
            meta_in = [sem(ctx, f"meta_in{j}") for j in range(U)]
            ef_in = [sem(ctx, f"ef_in{j}") for j in range(U)]
            g_in = [gather_sem(f"g_in{j}") for j in range(GR)]
            e0_made, e_rest, e1_made, e_split, e_low = (sem(ctx, n) for n in ("e0_made", "e_rest", "e1_made", "e_split", "e_low"))
            (ix_copied, gate, prepared, prep, oh_made, turned, ohT_made, z_made, z_summed, h_made, p_made, p_added) = (
                sem(ctx, n) for n in ("ix_copied", "gate", "prepared", "prep", "oh_made", "turned", "ohT_made", "z_made",
                                      "z_summed", "h_made", "p_made", "p_added"))

            def chunk_of(c):
                at = c * CE % U
                return ef[:, at:at + CE, :].rearrange("p u n -> p (u n)")

            with nc.Block() as block:
                @block.sync
                def _(sp):
                    regs = [sp.alloc_register(f"start_e{j}") for j in range(U)]
                    mregs = [sp.alloc_register(f"start_m{j}") for j in range(U)]

                    def load_meta(meta, it, j):
                        if j == 0:
                            load_row(sp, mregs, m.start_i, it, E)
                            if not isinstance(it, int) or it > 0:
                                sp.wait_ge(prepared, it)
                                sp.sem_inc(gate, 1)
                                sp.wait_ge(ix_copied, 2 * it)
                                sp.sem_inc(gate, 1)
                        first = sp.snap(mregs[j], min_val=0, max_val=E)
                        sp.dma_start(meta_b[:, j, :], meta[bass.ds(first, P), :]).then_inc(meta_in[j], 16)

                    def load_ef(efT, it, j):
                        if j == 0:
                            load_row(sp, regs, m.start_i, it, E)
                        if j % CE == 0 and (not isinstance(it, int) or it > 0):
                            sp.wait_ge(e_split, (it - 1) * (U // CE) + (j // CE + 1))
                            sp.sem_inc(gate, 1)
                        first = sp.snap(regs[j], min_val=0, max_val=E)
                        sp.dma_start(ef[:, j, :], efT[:, bass.ds(first, P)]).then_inc(ef_in[j], 16)

                    def iteration(meta, efT, it):
                        for j in range(U):
                            load_ef(efT, it, j)
                        for j in range(U):
                            load_meta(meta, it + 1, j)

                    def program(meta, efT):
                        for j in range(U):
                            load_meta(meta, 0, j)
                        iteration(meta, efT, 0)
                        with sp.Fori(1, ITERS) as it:
                            iteration(meta, efT, it)
                        for j in range(CE):
                            load_ef(efT, ITERS, j)
                        for j in range(U):
                            sp.wait_ge(meta_in[j], 16 * (ITERS + 1))

                    unsorted = sp.value_load(flag[0:1, 0:1], min_val=0, max_val=1)
                    with sp.If(unsorted > 0):
                        program(meta_s, efT_s)
                    with sp.Else():
                        program(meta, efT)

                @block.gpsimd
                def _(pool):
                    def gather(it):
                        for half in range(2):
                            js = range(half * GR, (half + 1) * GR)
                            for j in js:
                                pool.wait_ge(meta_in[j], (it + 1) * 16)
                                if not isinstance(it, int):
                                    pool.wait_ge(g_in[j % GR], (it * 2 - 1 + half) * 16)
                            pool.sem_inc(gate, 1)
                            pool.tensor_copy(ixr[:, js.start:js.stop], meta_b[:, js.start:js.stop, 0]).then_inc(ix_copied, 1)
                            pool.wait_ge(ix_copied, it * 2 + half + 1)
                            for j in js:
                                pool.sem_inc(gate, 1)
                                wait_step(pool, z_summed, it, j, ago=GR)
                                pool.sem_inc(gate, 1)
                                pool.indirect_dma_start(G[:, j % GR, :], None, A_dram,
                                                        bass.IndirectOffsetOnAxis(ap=ixr[:, j:j + 1], axis=0)
                                                        ).then_inc(g_in[j % GR], 16)

                    gather(0)
                    with pool.Fori(1, ITERS) as it:
                        gather(it)

                @block.vector
                def _(dve):
                    regs = [dve.alloc_register(f"nt_v{j}") for j in range(U)]

                    def prepare(it):
                        for j in range(U):
                            dve.wait_ge(meta_in[j], (it + 1) * 16)
                        at = bass.ds(it * U, U)
                        dve.tensor_tensor(m.dl[:, at], meta_b[:, :, 1], m.ntb[:, at], ALU.subtract).then_inc(prep, 1)
                        dve.scalar_tensor_tensor(m.tab_ix[:, at], meta_b[:, :, 2], float(NP), meta_b[:, :, 0], ALU.mult, ALU.add
                                                 ).then_inc(prep, 1)
                        dve.tensor_tensor(m.emask[:, at, :], meta_b[:, :, 2].unsqueeze(2).to_broadcast([P, U, R]),
                                          m.iota_r[:, :].unsqueeze(1).to_broadcast([P, U, R]), ALU.is_equal).then_inc(prep, 1)
                        dve.wait_ge(prep, (it + 1) * 3)
                        dve.sem_inc(prepared, 1)

                    def one_hot(it, j):
                        if j == 11:
                            prepare(it + 1)
                        wait_step(dve, p_made, it, j, ago=8)
                        dve.tensor_scalar(oh[:, j % 8, :], m.iota[:, :], m.dl[:, bass.ds(it * U + j, 1)], None,
                                          ALU.is_equal).then_inc(oh_made, 1)

                    def add_rows(it, j):
                        wait_step(dve, z_made, it, j)
                        dve.wait_ge(g_in[j % GR], (it * 2 + j // GR + 1) * 16)
                        wait_step(dve, p_made, it, j, ago=4)
                        dve.tensor_tensor(hb[:, j % 4, :], pz[:, j % 2, :], G[:, j % GR, :], ALU.add).then_inc(z_summed, 1)

                    def accumulate(it, j):
                        if j == 0:
                            load_row(dve, regs, m.nt_i, it, NT - 1)
                        nt = dve.snap(regs[j], min_val=0, max_val=NT - 1)
                        wait_step(dve, p_made, it, j)
                        wait_step(dve, p_added, it, j, ago=1)
                        a = m.agg[:, bass.ds(nt, 1), :].rearrange("p o n -> p (o n)")
                        dve.tensor_tensor(a, a, pp[:, j % 2, :], ALU.add).then_inc(p_added, 1)

                    def less_e0(it, c):
                        dve.wait_ge(e0_made, it * (U // CE) + (c + 1))
                        if not isinstance(it, int) or it + c > 0:
                            dve.wait_ge(e_split, it * (U // CE) + c)
                        dve.tensor_tensor(er[:, :], chunk_of(c), ep[:, 0, c % 2, :], ALU.subtract).then_inc(e_rest, 1)

                    def copy_low(it, c):
                        dve.tensor_copy(ep[0:ED, 2, c % 2, :], ep[0:ED, 0, c % 2, :]).then_inc(e_low, 1)

                    def last_parts(it, c):
                        dve.wait_ge(e_low, it * (U // CE) + (c + 1))
                        dve.wait_ge(e1_made, it * (U // CE) + (c + 1))
                        dve.tensor_tensor(ep[ED:P, 2, c % 2, :], er[ED:P, :], ep[ED:P, 1, c % 2, :], ALU.subtract
                                          ).then_inc(e_split, 1)

                    def split_next(it, j):
                        if j % CE == 1:
                            less_e0(it, j // CE + 1)
                        if j % CE == 2:
                            copy_low(it, j // CE + 1)
                        if j % CE == 3:
                            last_parts(it, j // CE + 1)

                    prepare(0)
                    less_e0(0, 0)
                    copy_low(0, 0)
                    last_parts(0, 0)
                    run_skewed(dve, [(one_hot, 0), (accumulate, 5), (add_rows, 2), (split_next, 0)])
                    dve.wait_ge(ohT_made, STEPS)
                    do = Chain(dve, sum_deg)
                    for t in range(NT):
                        do(dve.scalar_tensor_tensor(hb[:, 0, 0:STEPS], m.ntb[:, 0:STEPS], float(t * P), m.degs[:, 0:STEPS],
                                                    ALU.is_equal, ALU.mult, accum_out=m.deg[:, t:t + 1]))

                @block.scalar
                def _(act):
                    def copy_turned(it, j):
                        wait_step(act, turned, it, j)
                        wait_step(act, z_made, it, j, ago=4)
                        nc.scalar.activation(ohT[:, j % 4, :], pt[:, j % 2, 0:P], ACT.Copy,
                                             accum_out=m.degs[:, bass.ds(it * U + j, 1)]).then_inc(ohT_made, 1)

                    def relu(it, j):
                        wait_step(act, z_summed, it, j)
                        nc.scalar.activation(hb[:, j % 4, :], hb[:, j % 4, :], ACT.Relu).then_inc(h_made, 1)

                    def first_part(it, c):
                        for j in range(CE):
                            if c < U // CE:
                                act.wait_ge(ef_in[c * CE + j], (it + 1) * 16)
                            else:
                                act.wait_ge(ef_in[j], (it + 2) * 16)
                        if not isinstance(it, int) or it * U + (c - 1) * CE > 0:
                            act.wait_ge(z_made, it * U + (c - 1) * CE)
                        nc.scalar.activation(ep[:, 0, c % 2, :], chunk_of(c), ACT.Copy).then_inc(e0_made, 1)

                    def second_part(it, c):
                        act.wait_ge(e_rest, it * (U // CE) + (c + 1))
                        nc.scalar.activation(ep[:, 1, c % 2, :], er[:, :], ACT.Copy).then_inc(e1_made, 1)

                    def split_next(it, j):
                        if j % CE == 0:
                            first_part(it, j // CE + 1)
                        if j % CE == 2:
                            second_part(it, j // CE + 1)

                    first_part(0, 0)
                    second_part(0, 0)
                    run_skewed(act, [(copy_turned, 1), (relu, 3), (split_next, 0)])

                @block.tensor
                def _(pe):
                    regs = [pe.alloc_register(f"nt_p{j}") for j in range(U)]

                    def turn(it, j):
                        wait_step(pe, oh_made, it, j)
                        wait_step(pe, ohT_made, it, j, ago=2)
                        pe.transpose(pt[:, j % 2, 0:P], oh[:, j % 8, :], m.ident[:, :]).then_inc(turned, 1)

                    def preact(it, j):
                        if j == 0:
                            load_row(pe, regs, m.nt_i, it, NT - 1)
                        nt = pe.snap(regs[j], min_val=0, max_val=NT - 1)
                        wait_step(pe, z_summed, it, j, ago=2)
                        pe.wait_ge(e_split, it * (U // CE) + (j // CE + 1))
                        for k, w in ((0, 0), (1, 0), (2, 1)):
                            mm(pz[:, j % 2, :], ep[:, k, j // CE % 2, j % CE * P:(j % CE + 1) * P], m.w1e[:, w, :],
                               start=(k == 0), stop=False)
                        wait_step(pe, ohT_made, it, j)
                        Bn = m.B[:, bass.ds(nt, 1), :, :].rearrange("p o k n -> p (o k) n")
                        for k in range(3):
                            last = mm(pz[:, j % 2, :], ohT[:, j % 4, :], Bn[:, k, :], start=False, stop=(k == 2))
                        last.then_inc(z_made, 1)

                    def segsum(it, j):
                        wait_step(pe, h_made, it, j)
                        wait_step(pe, p_added, it, j, ago=2)
                        mm(pp[:, j % 2, :], oh[:, j % 8, :], hb[:, j % 4, :], start=True, stop=True).then_inc(p_made, 1)

                    run_skewed(pe, [(turn, 1), (preact, 2), (segsum, 4)])

        l0_edges.close()
        finished = list(done_with)
        with ExitStack() as ctx:
            w2T = sb(ctx, "w2T", [P, 4, HID])
            w3 = sb(ctx, "w3", [P, 6, HID])
            w23 = sb(ctx, "w23", [P, 4, HID])
            w4 = sb(ctx, "w4", [P, 4, D])
            b2c = sb(ctx, "b2c", [P, 4])
            b2w = sb(ctx, "b2w", [P, 4, P])
            b23 = sb(ctx, "b23", [P, HID])
            b3b = sb(ctx, "b3b", [P, HID])
            b4b = sb(ctx, "b4b", [P, D])
            aT = sb(ctx, "aT", [P, 2, HID])
            base = sb(ctx, "base", [P, 2, HID])
            g = sb(ctx, "g", [P, 2, HID])
            gT = sb(ctx, "gT", [P, 2, HID])
            y = sb(ctx, "y", [P, 2, D])
            st = sb(ctx, "st", [P, 2, 12])
            eps = sb(ctx, "eps", [P, 1])
            q_aT = psum(ctx, "q_aT", [P, 2, HID])
            q_g = psum(ctx, "q_g", [P, 2, HID])
            q_gT = psum(ctx, "q_gT", [P, 2, HID])
            q_y = psum(ctx, "q_y", [P, 512])
            q_xT = psum(ctx, "q_xT", [P, 512])
            (w23_in, w_in0, bw_made, w23_mm, w23_made, b23_made, agg_turned, aT_made, g_mm, base_made, g_made, g_turned,
             gT_made, y_mm, y_bias, y_made, stats, var_made, std_made, rstd, x1_made, x1_turned, xT_made) = (
                sem(ctx, "n_" + n) for n in (
                    "w23_in", "w_in", "bw_made", "w23_mm", "w23_made", "b23_made", "agg_turned", "aT_made", "g_mm",
                    "base_made", "g_made", "g_turned", "gT_made", "y_mm", "y_bias", "y_made", "stats", "var_made",
                    "std_made", "rstd", "x1_made", "x1_turned", "xT_made"))

            def run_tiles(stages):
                for i in range(NT + max(lag for _, lag in stages)):
                    for f, lag in stages:
                        if 0 <= i - lag < NT:
                            f(i - lag)

            def ago(eng, sm, t, n):
                if t - n >= 0:
                    eng.wait_ge(sm, t - n + 1)

            with nc.Block() as block:
                @block.sync
                def _(sp):
                    sp.dma_start(w3[:, :, :], W3.rearrange("(c p) n -> p c n", p=P)).then_inc(w23_in, 16)
                    sp.dma_start(b2c[:, :], b2).then_inc(w23_in, 16)
                    sp.dma_start(b3b[:, :], b3.partition_broadcast(P)).then_inc(w_in0, 16)
                    sp.dma_start(b4b[:, :], b4.partition_broadcast(P)).then_inc(w_in0, 16)
                    sp.dma_start(w4[:, :, :], W4.rearrange("(c p) n -> p c n", p=P)).then_inc(w_in0, 16)

                @block.gpsimd
                def _(pool):
                    for handle in finished:
                        pool.sem_clear(handle)

                @block.tensor
                def _(pe):
                    def turn_agg(t):
                        ago(pe, aT_made, t, 2)
                        for c in range(4):
                            last = pe.transpose(q_aT[:, t % 2, c * P:(c + 1) * P], m.agg[:, t, c * P:(c + 1) * P], m.ident[:, :])
                        last.then_inc(agg_turned, 1)

                    def hidden(t):
                        if t == 0:
                            pe.wait_ge(w23_in, 48)
                            pe.wait_ge(bw_made, 1)
                            for k in range(4):
                                last = mm(q_y[:, :], b2w[:, k, :], w3[:, 2 + k, :], start=(k == 0), stop=(k == 3))
                            last.then_inc(b23_made, 1)
                            for c in range(4):
                                out_q = (q_g, q_gT)[c // 2][:, c % 2, :]
                                for k in range(4):
                                    last = mm(out_q, w2T[:, k, c * P:(c + 1) * P], w3[:, 2 + k, :], start=(k == 0), stop=(k == 3))
                                last.then_inc(w23_mm, 1)
                            pe.wait_ge(w23_made, 4)
                        ago(pe, g_made, t, 2)
                        pe.wait_ge(aT_made, t + 1)
                        for c in range(2):
                            mm(q_g[:, t % 2, :], m.xTs[:, c, t * P:(t + 1) * P], w3[:, c, :], start=(c == 0), stop=False)
                        for c in range(4):
                            last = mm(q_g[:, t % 2, :], aT[:, t % 2, c * P:(c + 1) * P], w23[:, c, :], start=False, stop=(c == 3))
                        last.then_inc(g_mm, 1)

                    def turn_g(t):
                        pe.wait_ge(g_made, t + 1)
                        ago(pe, gT_made, t, 2)
                        for c in range(4):
                            last = pe.transpose(q_gT[:, t % 2, c * P:(c + 1) * P], g[:, t % 2, c * P:(c + 1) * P], m.ident[:, :])
                        last.then_inc(g_turned, 1)

                    def update(t):
                        if t == 0:
                            pe.wait_ge(w_in0, 48)
                            pe.wait_ge(b23_made, 2)
                        pe.wait_ge(gT_made, t + 1)
                        ago(pe, y_bias, t, 1)
                        for c in range(4):
                            last = mm(q_y[:, 0:D], gT[:, t % 2, c * P:(c + 1) * P], w4[:, c, :], start=(c == 0), stop=(c == 3))
                        last.then_inc(y_mm, 1)

                    def turn_x1(t):
                        pe.wait_ge(x1_made, t + 1)
                        ago(pe, xT_made, t, 1)
                        for c in range(2):
                            last = pe.transpose(q_xT[:, c * P:(c + 1) * P], m.xs[:, t, c * P:(c + 1) * P], m.ident[:, :])
                        last.then_inc(x1_turned, 1)

                    run_tiles([(turn_agg, 0), (hidden, 1), (turn_g, 3), (update, 4), (turn_x1, 6)])

                @block.scalar
                def _(act):
                    act.dma_start(w2T[:, :, :], W2T.rearrange("(c p) n -> p c n", p=P)).then_inc(w23_in, 16)

                    def copy_aT(t):
                        act.wait_ge(agg_turned, t + 1)
                        ago(act, g_mm, t, 2)
                        nc.scalar.activation(aT[:, t % 2, :], q_aT[:, t % 2, :], ACT.Copy).then_inc(aT_made, 1)
                        if t == 1:
                            for c in (1, 3):
                                act.wait_ge(w23_mm, c + 1)
                                nc.scalar.activation(w23[:, c, :], (q_g, q_gT)[c // 2][:, 1, :], ACT.Copy).then_inc(w23_made, 1)

                    def relu_gT(t):
                        act.wait_ge(g_turned, t + 1)
                        ago(act, y_mm, t, 2)
                        nc.scalar.activation(gT[:, t % 2, :], q_gT[:, t % 2, :], ACT.Relu).then_inc(gT_made, 1)

                    def std(t):
                        act.wait_ge(var_made, t + 1)
                        ago(act, rstd, t, 2)
                        nc.scalar.activation(st[:, t % 2, 8:9], st[:, t % 2, 7:8], ACT.Sqrt, bias=eps[:, 0:1]).then_inc(std_made, 1)

                    def copy_xT(t):
                        act.wait_ge(x1_turned, t + 1)
                        nc.scalar.activation(m.xTs[:, :, t * P:(t + 1) * P], q_xT[:, 0:D].rearrange("p (c n) -> p c n", c=2),
                                             ACT.Copy).then_inc(xT_made, 1)

                    run_tiles([(copy_aT, 0), (relu_gT, 3), (std, 4), (copy_xT, 6)])

                @block.vector
                def _(dve):
                    dve.memset(eps[:, :], EPS_LN)
                    dve.wait_ge(w23_in, 48)
                    dve.tensor_copy(b2w[:, :, :], b2c[:, :].unsqueeze(2).to_broadcast([P, 4, P])).then_inc(bw_made, 1)
                    dve.wait_ge(b23_made, 1)
                    dve.tensor_copy(b23[:, :], q_y[:, :]).then_inc(b23_made, 1)
                    for c in (0, 2):
                        dve.wait_ge(w23_mm, c + 1)
                        dve.tensor_copy(w23[:, c, :], (q_g, q_gT)[c // 2][:, 0, :]).then_inc(w23_made, 1)
                    dve.wait_ge(w_in0, 48)
                    dve.wait_ge(b23_made, 2)

                    def bias(t):
                        ago(dve, g_made, t, 2)
                        dve.scalar_tensor_tensor(base[:, t % 2, :], b23[:, :], m.deg[:, t:t + 1], b3b[:, :], ALU.mult, ALU.add
                                                 ).then_inc(base_made, 1)

                    def add_bias(t):
                        dve.wait_ge(g_mm, t + 1)
                        dve.wait_ge(base_made, t + 1)
                        ago(dve, g_turned, t, 2)
                        dve.tensor_tensor(g[:, t % 2, :], q_g[:, t % 2, :], base[:, t % 2, :], ALU.add).then_inc(g_made, 1)

                    def residual(t):
                        yt, s6 = y[:, t % 2, :], st[:, t % 2, :]
                        dve.wait_ge(y_mm, t + 1)
                        ago(dve, x1_made, t, 2)
                        dve.tensor_tensor(yt, q_y[:, 0:D], b4b[:, :], ALU.add).then_inc(y_bias, 1)
                        dve.wait_ge(y_bias, t + 1)
                        dve.scalar_tensor_tensor(yt, m.xs[:, t, :], 2.0, yt, ALU.mult, ALU.add).then_inc(y_made, 1)
                        dve.wait_ge(y_made, t + 1)
                        dve.bn_stats(s6[:, 0:6], yt).then_inc(stats, 1)
                        dve.wait_ge(stats, t + 1)
                        dve.bn_aggr(s6[:, 6:8], s6[:, 0:6]).then_inc(var_made, 1)

                    def normalise(t):
                        s6 = st[:, t % 2, :]
                        dve.wait_ge(std_made, t + 1)
                        dve.reciprocal(s6[:, 9:10], s6[:, 8:9]).then_inc(rstd, 1)
                        dve.wait_ge(rstd, t + 1)
                        dve.tensor_scalar(m.xs[:, t, :], y[:, t % 2, :], s6[:, 6:7], s6[:, 9:10], ALU.subtract, ALU.mult
                                          ).then_inc(x1_made, 1)

                    run_tiles([(bias, 0), (normalise, 5), (residual, 4), (add_bias, 1)])
        l0.close()

        l1 = whole.enter_context(ExitStack())
        m.acc = sb(l1, "acc", [P, NT, ROW])
        m.sdt = sb(l1, "sdt", [P, NT, 3, R * H], BF16)
        with ExitStack() as ctx:
            wt = sb(ctx, "wt", [P, 2, R * ROW])
            wtd = sb(ctx, "wtd", [P, 2, R * H])
            wn = sb(ctx, "wn", [P, R, 2, D])
            at = sb(ctx, "at", [P, 2, 2])
            blk = sb(ctx, "blk", [P, 2, 2 * H])
            row = sb(ctx, "row", [P, 2, R * ROW])
            pr = psum(ctx, "pr", [P, 6, 512])
            pv = psum(ctx, "pv", [P, 512])
            pd = psum(ctx, "pd", [P, 512])
            w_in, blk_made, v_made, v_copied, row_mm, row_dve, row_act, d_mm, d_out, dve_c = (
                sem(ctx, n) for n in ("w_in", "blk_made", "v_made", "v_copied", "row_mm", "row_dve", "row_act", "d_mm",
                                      "d_out", "dve_c"))
            row_wr = [sem(ctx, f"row_wr{k}") for k in range(2)]
            blk0 = sem(ctx, "blk0")
            sdf = sb(ctx, "sdf", [P, 2, NT, R * H])
            s0, s1_, s2_ = (sem(ctx, f"split_s{k}") for k in range(3))
            with nc.Block() as block:
                @block.sync
                def _(sp):
                    sp.dma_start(wt[:, :, :], WT.rearrange("(c p) n -> p c n", p=P)).then_inc(w_in, 16)
                    sp.dma_start(wn[:, :, :, :], Wn.rearrange("r (c p) n -> p r c n", p=P)).then_inc(w_in, 16)
                    sp.dma_start(at[:, :, :], attn).then_inc(w_in, 16)
                    for t in range(NT):
                        sp.wait_ge(row_dve, R // 2 * (t + 1))
                        sp.wait_ge(row_act, R // 2 * (t + 1))
                        sp.dma_start(T_dram.rearrange("(r t p) n -> t p r n", r=R, p=P)[t],
                                     row[:, t % 2, :].rearrange("p (r n) -> p r n", r=R)).then_inc(row_wr[t % 2], 16)
                    for k in range(2):
                        sp.wait_ge(row_wr[k], 16 * (NT // 2))

                @block.gpsimd
                def _(pool):
                    pool.memset(blk[:, :, :], 1.0).then_inc(blk0, 1)
                    v = blk[:, :, :].rearrange("p c (s h) -> p c s h", s=2)
                    pool.wait_ge(blk0, 1)
                    pool.affine_select(out=v, in_=v, compare_op=ALU.is_ge, fill=0.0, base=0,
                                       pattern=[[P, 2], [0, 2], [-HD, H]], channel_multiplier=1).then_inc(blk0, 1)
                    pool.wait_ge(blk0, 2)
                    pool.affine_select(out=v, in_=v, compare_op=ALU.is_gt, fill=0.0, base=HD,
                                       pattern=[[-P, 2], [0, 2], [HD, H]], channel_multiplier=-1).then_inc(blk0, 1)
                    pool.memset(m.acc[:, :, :], 0.0)

                @block.vector
                def _(dve):
                    do = Chain(dve, dve_c)
                    dve.wait_ge(w_in, 48)
                    dve.wait_ge(blk0, 3)
                    for c in range(2):
                        for s in range(2):
                            do(dve.tensor_scalar(blk[:, c, s * H:(s + 1) * H], blk[:, c, s * H:(s + 1) * H],
                                                 at[:, s, c:c + 1], None, ALU.mult))
                    dve.sem_inc(blk_made, 1)
                    dve.wait_ge(v_made, 1)
                    v = pv[:, 0:2 * R * 16].rearrange("p (f r n) -> p f r n", f=2, r=R)
                    do(dve.tensor_copy(wt[:, :, :].rearrange("p f (r h w) -> p f r h w", r=R, h=H)[:, 0, :, :, HD], v[:, 0, :, 0:H]))
                    do(dve.tensor_copy(wt[:, :, :].rearrange("p f (r h w) -> p f r h w", r=R, h=H)[:, 1, :, :, HD], v[:, 1, :, 0:H]))
                    do(dve.tensor_copy(wtd[:, 0, :].rearrange("p (r h) -> p r h", r=R), v[:, 0, :, H:2 * H]))
                    do(dve.tensor_copy(wtd[:, 1, :].rearrange("p (r h) -> p r h", r=R), v[:, 1, :, H:2 * H]))
                    dve.sem_inc(v_copied, 1)
                    for t in range(NT):
                        for r in range(0, R, 2):
                            n = t * R + r
                            dve.wait_ge(row_mm, n + 1)
                            if t >= 2:
                                dve.wait_ge(row_wr[t % 2], 16 * (t // 2))
                            dve.tensor_copy(row[:, t % 2, r * ROW:(r + 1) * ROW], pr[:, n % 6, 0:ROW]).then_inc(row_dve, 1)
                        dve.wait_ge(d_mm, t + 1)
                        dve.tensor_copy(sdf[:, 0, t, :], pd[:, 0:R * H]).then_inc(d_out, 1)
                    dve.wait_ge(s0, 1)
                    dve.tensor_tensor(sdf[:, 1, :, :], sdf[:, 0, :, :], m.sdt[:, :, 0, :], ALU.subtract).then_inc(s1_, 1)
                    dve.wait_ge(s2_, 1)
                    dve.tensor_tensor(m.sdt[:, :, 2, :], sdf[:, 1, :, :], m.sdt[:, :, 1, :], ALU.subtract)

                @block.scalar
                def _(act):
                    for t in range(NT):
                        for r in range(1, R, 2):
                            n = t * R + r
                            act.wait_ge(row_mm, n + 1)
                            if t >= 2:
                                act.wait_ge(row_wr[t % 2], 16 * (t // 2))
                            nc.scalar.activation(row[:, t % 2, r * ROW:(r + 1) * ROW], pr[:, n % 6, 0:ROW], ACT.Copy
                                                 ).then_inc(row_act, 1)
                    act.wait_ge(d_out, NT)
                    nc.scalar.activation(m.sdt[:, :, 0, :], sdf[:, 0, :, :], ACT.Copy).then_inc(s0, 1)
                    act.wait_ge(s1_, 1)
                    nc.scalar.activation(m.sdt[:, :, 1, :], sdf[:, 1, :, :], ACT.Copy).then_inc(s2_, 1)

                @block.tensor
                def _(pe):
                    pe.wait_ge(w_in, 48)
                    pe.wait_ge(blk_made, 1)
                    for f in range(2):
                        for r in range(R):
                            for c in range(2):
                                last = mm(pv[:, (f * R + r) * 16:(f * R + r + 1) * 16], wn[:, r, c, f * P:(f + 1) * P],
                                          blk[:, c, :], start=(c == 0), stop=(c == 1))
                    last.then_inc(v_made, 1)
                    pe.wait_ge(v_copied, 1)
                    for t in range(NT):
                        for r in range(R):
                            n = t * R + r
                            if n >= 6:
                                pe.wait_ge((row_dve, row_act)[n % 2], (n - 6) // 2 + 1)
                            for c in range(2):
                                last = mm(pr[:, n % 6, 0:ROW], m.xTs[:, c, t * P:(t + 1) * P], wt[:, c, r * ROW:(r + 1) * ROW],
                                          start=(c == 0), stop=(c == 1))
                            last.then_inc(row_mm, 1)
                        if t:
                            pe.wait_ge(d_out, t)
                        for c in range(2):
                            last = mm(pd[:, 0:R * H], m.xTs[:, c, t * P:(t + 1) * P], wtd[:, c, :], start=(c == 0), stop=(c == 1))
                        last.then_inc(d_mm, 1)

        with ExitStack() as ctx:
            G = sb(ctx, "G1", [P, 2, GU, ROW])
            ixr = sb(ctx, "ixr1", [P, 2, GU], U32)
            oh = sb(ctx, "oh1", [P, 2, GU, P], BF16)
            ohf = sb(ctx, "ohf", [P, 2, GU, P])
            ohT = sb(ctx, "ohT1", [P, 2, GU, P], BF16)
            sd8 = sb(ctx, "sd8", [P, GU, R * H])
            sc = sb(ctx, "sc", [P, 2, GU * H])
            raw = sb(ctx, "raw", [P, 2, GU * H])
            dT = sb(ctx, "dT", [P, P])
            eq = sb(ctx, "eq", [P, P + 1])
            run = sb(ctx, "run", [P, 2, P])
            rl = sb(ctx, "rl", [P, 3, GU * H], BF16)
            rlf = sb(ctx, "rlf", [P, GU * H])
            cb = sb(ctx, "cb", [P, H * (GU + 1) + 1])
            mb = sb(ctx, "mb", [P, H, GU + 1])
            fw = sb(ctx, "fw", [P, 2, H, GU + 1])
            bw = sb(ctx, "bw", [P, H, GU + 1])
            mx = sb(ctx, "mx", [P, 3, H, GU + 1], BF16)
            mxf = sb(ctx, "mxf", [P, H, GU + 1])
            av = sb(ctx, "av", [P, 2, H, 1])
            w8 = sb(ctx, "w8", [P, 2, GU * H])
            iota_b = sb(ctx, "iota_b", [P, P], BF16)
            ident_b = sb(ctx, "ident_b", [P, P], BF16)
            pt = ctx.enter_context(nc.psum_tensor("pt1", [P, 2, 8, P], BF16))
            psd = psum(ctx, "psd", [P, GU, R * H])
            pq = psum(ctx, "pq", [P, 4, P])
            pm = psum(ctx, "pm", [P, 4, GU * H])
            pw = psum(ctx, "pw", [P, 2, 512])
            s = {k: sem(ctx, "s_" + k) for k in (
                "ixc", "gate", "oh", "ohf", "turn", "ohT", "sd", "sdm", "dve", "sc", "scT", "dT", "rl", "rlT", "r0", "r1",
                "rb", "r2", "mt", "mx", "m0", "m1", "mbb", "m2", "mbc", "a", "ea", "sm", "w", "wcap", "msg", "p", "resc", "acc")}
            g_in = [[gather_sem(f"g1_in{b}_{j}") for j in range(GU)] for b in range(2)]
            set1 = sem(ctx, "set1")
            CH = 2

            def wait_count(eng, sm, v):
                if not isinstance(v, int) or v > 0:
                    eng.wait_ge(sm, v)

            def load_tiles(eng, regs, gi):
                eng.load(regs, m.nt_i[0:1, bass.ds(gi * GU, GU)])

            def over_groups(eng, body):
                body(-1, 1, None, False, False, True)
                body(0, 0, 0, False, True, True)
                body(1, 1, 0, True, True, True)
                body(2, 0, 1, True, True, True)
                with eng.Fori(1, (GROUPS - 3) // 2) as i:
                    body(i * 2 + 1, 1, i, True, True, True)
                    body(i * 2 + 2, 0, i + 1, True, True, True)
                n = GROUPS - 2
                body(n, n % 2, n // 2, True, True, True)
                body(n + 1, (n + 1) % 2, (n + 1) // 2, True, True, False)
                body(n + 2, (n + 2) % 2, None, True, False, False)

            assert GROUPS % 2 == 1

            with nc.Block() as block:
                @block.gpsimd
                def _(pool):
                    def gather(gi, b, first):
                        if not first:
                            for j in range(GU):
                                pool.wait_ge(g_in[b][j], first_use(gi) * 16)
                        pool.sem_inc(s["gate"], 1)
                        pool.tensor_copy(ixr[:, b, :], m.tab_ix[:, bass.ds(gi * GU, GU)]).then_inc(s["ixc"], 1)
                        pool.wait_ge(s["ixc"], gi + 1)
                        pool.sem_inc(s["gate"], 1)
                        for j in range(GU):
                            if not first:
                                pool.wait_ge(s["p"], (gi - 2) * GU + j + 1)
                                pool.sem_inc(s["gate"], 1)
                            pool.indirect_dma_start(G[:, b, j, :], None, T_dram,
                                                    bass.IndirectOffsetOnAxis(ap=ixr[:, b, j:j + 1], axis=0)
                                                    ).then_inc(g_in[b][j], 16)

                    def first_use(gi):
                        return gi_uses[0]

                    gi_uses = [0]
                    gather(0, 0, True)
                    gather(1, 1, True)
                    gi_uses[0] = 1
                    gather(2, 0, False)
                    with pool.Fori(1, (GROUPS - 1) // 2) as i:
                        gi_uses[0] = i
                        gather(i * 2 + 1, 1, False)
                        gi_uses[0] = i + 1
                        gather(i * 2 + 2, 0, False)

                @block.vector
                def _(dve):
                    regs = [dve.alloc_register(f"nt_w{j}") for j in range(GU)]
                    dve.tensor_copy(iota_b[:, :], m.iota[:, :]).then_inc(s["dve"], 1)
                    dve.tensor_copy(ident_b[:, :], m.ident[:, :]).then_inc(set1, 1)
                    dve.memset(eq[:, :], 0.0).then_inc(s["dve"], 1)
                    dve.memset(cb[:, :], 0.0).then_inc(s["dve"], 1)
                    dve.memset(fw[:, :, :, :], 0.0).then_inc(s["dve"], 1)
                    dve.wait_ge(s["dve"], 4)
                    K = 10

                    def body(n, b, u, prev, now, nxt):
                        c = [4]

                        def do(ins):
                            c[0] += 1
                            ins.then_inc(s["dve"], 1)
                            dve.wait_ge(s["dve"], n * K + c[0])

                        def one_hot(j):
                            if j == 0 and (now or prev):
                                wait_count(dve, s["ohf"], n * 4)
                                dve.wait_ge(s["mt"], n) if prev else None
                            dve.tensor_scalar(oh[:, 1 - b, j, :], iota_b[:, :], m.dl[:, bass.ds((n + 1) * GU + j, 1)], None,
                                              ALU.is_equal).then_inc(s["oh"], 1)

                        def largest_weight():
                            dve.wait_ge(s["w"], n)
                            dve.tensor_scalar(G[:, 1 - b, :, :].rearrange("p u (h w) -> p u h w", h=H)[:, :, :, HD],
                                              w8[:, 1, :].rearrange("p (u h) -> p u h", u=GU), 1.0, None, ALU.min
                                              ).then_inc(s["wcap"], 1)
                            dve.wait_ge(s["wcap"], n)

                        def messages(k):
                            Gv = G[:, 1 - b, k * CH:(k + 1) * CH, :].rearrange("p u (h w) -> p (u h) w", h=H)
                            dve.tensor_tensor(Gv[:, :, 0:HD], Gv[:, :, 0:HD], Gv[:, :, HD:HD + 1].to_broadcast([P, CH * H, HD]),
                                              ALU.mult).then_inc(s["msg"], 1)

                        def accumulate(j):
                            t = (n - 1) * GU + j
                            nt = dve.snap(regs[j], min_val=0, max_val=NT - 1)
                            a = m.acc[:, bass.ds(nt, 1), :].rearrange("p o n -> p (o n)")
                            if j == 0:
                                ah = a.rearrange("p (h w) -> p h w", h=H)
                                dve.wait_ge(s["ea"], n)
                                wait_count(dve, s["acc"], t)
                                dve.tensor_tensor(ah, ah, av[:, 1, :, :].to_broadcast([P, H, HW]), ALU.mult).then_inc(s["resc"], 1)
                                dve.wait_ge(s["resc"], n)
                            wait_count(dve, s["acc"], t)
                            dve.wait_ge(s["p"], t + 1)
                            dve.tensor_tensor(a, a, pw[:, j % 2, 0:ROW], ALU.add).then_inc(s["acc"], 1)

                        def target_scores(k):
                            js = slice(k % 2 * (GU // 2), (k % 2 + 1) * (GU // 2))
                            if k < 2:
                                dve.wait_ge(s["sd"], n * 2 + k + 1)
                                dve.tensor_tensor(sd8[:, js, :].rearrange("p u (r h) -> p u r h", r=R),
                                                  psd[:, js, :].rearrange("p u (r h) -> p u r h", r=R),
                                                  m.emask[:, bass.ds(n * GU + js.start, GU // 2), :].unsqueeze(3).to_broadcast(
                                                      [P, GU // 2, R, H]), ALU.mult).then_inc(s["sdm"], 1)
                            else:
                                dve.wait_ge(s["sdm"], n * 2 + (k - 1))
                                do(dve.tensor_reduce(raw[:, 0, :].rearrange("p (u h) -> p u h", u=GU)[:, js, :],
                                                     sd8[:, js, :].rearrange("p u (r h) -> p u h r", r=R), AX.X, ALU.add))

                        def scores():
                            for j in range(GU):
                                dve.wait_ge(g_in[b][j], (u + 1) * 16)
                            Gv = G[:, b, :, :].rearrange("p u (h w) -> p u h w", h=H)
                            do(dve.tensor_tensor(raw[:, 1, :].rearrange("p (u h) -> p u h", u=GU), Gv[:, :, :, HD],
                                                 raw[:, 0, :].rearrange("p (u h) -> p u h", u=GU), ALU.add))
                            do(dve.scalar_tensor_tensor(sc[:, 0, :], raw[:, 1, :], 0.2, raw[:, 1, :], ALU.mult, ALU.max))
                            dve.tensor_scalar(sc[:, 1, :].rearrange("p (u h) -> p u h", u=GU),
                                              m.dl[:, bass.ds(n * GU, GU)].unsqueeze(2).to_broadcast([P, GU, H]), 0.0, None,
                                              ALU.add).then_inc(s["sc"], 1)

                        def step_max():
                            dve.wait_ge(s["dT"], n + 1)
                            do(dve.tensor_tensor(eq[:, 1:P], dT[:, 1:P], dT[:, 0:P - 1], ALU.is_equal))
                            do(dve.tensor_tensor_scan(run[:, 0, :], eq[:, 0:P], pq[:, 0, :], 0.0, ALU.mult, ALU.max))
                            dve.scalar_tensor_tensor(run[:, 1, :], eq[:, 1:P + 1], 0.0, run[:, 0, :], ALU.is_equal, ALU.mult
                                                     ).then_inc(s["rl"], 1)

                        def node_max():
                            cv = cb[:, 0:H * (GU + 1)]
                            do(dve.tensor_scalar(cv.rearrange("p (h u) -> p h u", h=H)[:, :, 1:GU + 1],
                                                 m.cont[:, bass.ds(n * GU, GU)].unsqueeze(1).to_broadcast([P, H, GU]), 0.0, None,
                                                 ALU.add))
                            dve.tensor_copy(mb[:, :, 0:1], fw[:, 1 - b, :, GU:GU + 1])
                            dve.wait_ge(s["mt"], n + 1)
                            do(dve.tensor_copy(mb[:, :, 1:GU + 1], pm[:, 1, :].rearrange("p (u h) -> p h u", u=GU)))
                            f = fw[:, b, :, :].rearrange("p h u -> p (h u)")
                            do(dve.tensor_tensor_scan(f, cv, mb[:, :, :].rearrange("p h u -> p (h u)"), 0.0, ALU.mult, ALU.max))
                            dve.tensor_tensor_scan(bw[:, :, :].rearrange("p h u -> p (h u)")[:, ::-1],
                                                   cb[:, 1:H * (GU + 1) + 1][:, ::-1], f[:, ::-1], 0.0, ALU.mult, ALU.max
                                                   ).then_inc(s["mx"], 1)
                            wait_count(dve, s["ea"], n)
                            do(dve.tensor_tensor(av[:, 0, :, :], fw[:, b, :, 0:1],
                                                 cv.rearrange("p (h u) -> p h u", h=H)[:, :, 1:2], ALU.mult))
                            dve.wait_ge(s["mx"], n + 1)
                            dve.tensor_tensor(av[:, 0, :, :], av[:, 0, :, :], bw[:, :, 1:2], ALU.subtract).then_inc(s["a"], 1)

                        def part(k, whole_, first, rest, waits, done, last=None):
                            dve.wait_ge(waits, n + 1)
                            dve.tensor_tensor(rest, whole_, first, ALU.subtract).then_inc(done, 1)

                        if prev:
                            load_tiles(dve, regs, n - 1)
                        for j in range(GU):
                            if nxt:
                                one_hot(j)
                            if prev and j == 0:
                                largest_weight()
                                messages(0)
                            if prev and j % CH == CH - 1 and j + 1 < GU:
                                messages((j + 1) // CH)
                            if prev and j:
                                accumulate(j - 1)
                            if now:
                                if 1 <= j <= 4:
                                    target_scores((0, 2, 1, 3)[j - 1])
                                if j == SCO:
                                    scores()
                                if j == SCO + 2:
                                    step_max()
                                if j == SCO + 4:
                                    part(0, pm[:, 0, :], rl[:, 0, :], rlf[:, :], s["r0"], s["r1"])
                                if j == SCO + 5:
                                    part(0, rlf[:, :], rl[:, 1, :], rl[:, 2, :], s["rb"], s["r2"])
                                if j == SCO + 7:
                                    node_max()
                                if j == SCO + 8:
                                    part(0, bw[:, :, :], mx[:, 0, :, :], mxf[:, :, :], s["m0"], s["m1"])
                                if j == SCO + 9:
                                    part(0, mxf[:, :, :], mx[:, 1, :, :], mx[:, 2, :, :], s["mbb"], s["m2"])
                        if prev:
                            accumulate(GU - 1)
                        if now:
                            dve.wait_ge(s["mbc"], n + 1)
                            dve.tensor_tensor(w8[:, 0, :], sc[:, 0, :], pm[:, 2, :], ALU.subtract).then_inc(s["sm"], 1)
                            assert c[0] == K + 4, c

                    SCO = 5
                    over_groups(dve, body)

                @block.scalar
                def _(act):
                    def body(n, b, u, prev, now, nxt):
                        def copy(o, i, waits, done, func=ACT.Copy):
                            act.wait_ge(waits, n + 1)
                            nc.scalar.activation(o, i, func).then_inc(done, 1)

                        def turned(k, n, b):
                            act.wait_ge(s["turn"], n * 2 + k + 1)
                            wait_count(act, s["mbc"], n - 1)
                            nc.scalar.activation(ohT[:, b, 8 * k:8 * k + 8, :], pt[:, k, :, :], ACT.Copy).then_inc(s["ohT"], 1)

                        def widen(k):
                            act.wait_ge(s["oh"], n * GU + 4 * k + 4)
                            wait_count(act, s["p"], (n - 2) * GU + 4 * k + 4)
                            nc.scalar.activation(ohf[:, b, 4 * k:4 * k + 4, :], oh[:, b, 4 * k:4 * k + 4, :], ACT.Copy
                                                 ).then_inc(s["ohf"], 1)

                        if now:
                            turned(1, n, b)
                            for k in range(4):
                                widen(k)
                            copy(dT[:, :], pq[:, 1, :], s["scT"], s["dT"])
                            copy(rl[:, 0, :], pm[:, 0, :], s["rlT"], s["r0"])
                            copy(rl[:, 1, :], rlf[:, :], s["r1"], s["rb"])
                        if nxt:
                            turned(0, n + 1, 1 - b)
                        if now:
                            copy(mx[:, 0, :, :], bw[:, :, :], s["mx"], s["m0"])
                            copy(mx[:, 1, :, :], mxf[:, :, :], s["m1"], s["mbb"])
                            wait_count(act, s["resc"], n)
                            copy(av[:, 1, :, :], av[:, 0, :, :], s["a"], s["ea"], ACT.Exp)
                            copy(w8[:, 1, :], w8[:, 0, :], s["sm"], s["w"], ACT.Exp)

                    over_groups(act, body)

                @block.tensor
                def _(pe):
                    regs = [pe.alloc_register(f"nt_q{j}") for j in range(GU)]
                    pe.wait_ge(set1, 1)

                    def body(n, b, u, prev, now, nxt):
                        def turn(j):
                            pe.wait_ge(s["oh"], (n + 1) * GU + j + 1)
                            if j == 0:
                                wait_count(pe, s["ohT"], (n + 1) * 2)
                            last = pe.transpose(pt[:, j // 8, j % 8, :], oh[:, 1 - b, j, :], ident_b[:, :])
                            if j % 8 == 7:
                                last.then_inc(s["turn"], 1)

                        def target_scores(n, b, k):
                            if k % 4 == 0:
                                if k == 0:
                                    load_tiles(pe, regs, n)
                                wait_count(pe, s["sdm"], n * 2 - (1 - k // 4))
                                pe.wait_ge(s["ohT"], n * 2 + k // 4 + 1)
                            for j in range(2 * k, 2 * k + 2):
                                nt = pe.snap(regs[j], min_val=0, max_val=NT - 1)
                                tab = m.sdt[:, bass.ds(nt, 1), :, :].rearrange("p o k n -> p (o k) n")
                                for q in range(3):
                                    last = mm(psd[:, j, :], ohT[:, b, j, :], tab[:, q, :], start=(q == 0), stop=(q == 2))
                            if k % 4 == 3:
                                last.then_inc(s["sd"], 1)

                        def messages(j):
                            t = (n - 1) * GU + j
                            if j % CH == 0:
                                pe.wait_ge(s["msg"], (n - 1) * (GU // CH) + j // CH + 1)
                            if j == 0:
                                pe.wait_ge(s["ohf"], n * 4)
                            wait_count(pe, s["acc"], t - 1)
                            mm(pw[:, j % 2, 0:ROW], ohf[:, 1 - b, j, :], G[:, 1 - b, j, :], start=True, stop=True).then_inc(s["p"], 1)

                        def turn_scores():
                            pe.wait_ge(s["sc"], n + 1)
                            pe.transpose(pq[:, 0, :], sc[:, 0, :], m.ident[:, :])
                            pe.transpose(pq[:, 1, :], sc[:, 1, :], m.ident[:, :]).then_inc(s["scT"], 1)

                        def turn_max():
                            pe.wait_ge(s["rl"], n + 1)
                            pe.transpose(pm[:, 0, :], run[:, 1, :], m.ident[:, :]).then_inc(s["rlT"], 1)

                        def node_max():
                            pe.wait_ge(s["r2"], n + 1)
                            for j in range(GU):
                                for q in range(3):
                                    last = mm(pm[:, 1, j * H:(j + 1) * H], oh[:, b, j, :], rl[:, q, j * H:(j + 1) * H],
                                              start=(q == 0), stop=(q == 2))
                            last.then_inc(s["mt"], 1)

                        def edge_max():
                            pe.wait_ge(s["m2"], n + 1)
                            for j in range(GU):
                                for q in range(3):
                                    last = mm(pm[:, 2, j * H:(j + 1) * H], ohT[:, b, j, :], mx[:, q, :, j + 1],
                                              start=(q == 0), stop=(q == 2))
                            last.then_inc(s["mbc"], 1)

                        for j in range(GU):
                            if nxt and j:
                                turn(j - 1)
                            if prev:
                                messages(j)
                            if now and j in (1, 2):
                                for k in (0, 1):
                                    target_scores(n, b, 2 + 2 * j + k)
                            if now:
                                if j == SCO + 1:
                                    turn_scores()
                                if j == SCO + 3:
                                    turn_max()
                                if j == SCO + 6:
                                    node_max()
                                if j == SCO + 10:
                                    edge_max()
                            if nxt and j >= GU - 4:
                                target_scores(n + 1, 1 - b, j - (GU - 4))
                        if nxt:
                            turn(GU - 1)

                    SCO = 5
                    over_groups(pe, body)

        with ExitStack() as ctx:
            den = sb(ctx, "den", [P, 2, NT, H])
            y = sb(ctx, "yf", [P, NT, D])
            st = sb(ctx, "stf", [P, NT, 6])
            mv = sb(ctx, "mv", [P, NT, 2])
            eps = sb(ctx, "epsf", [P, 1])
            std = sb(ctx, "std", [P, 2, NT])
            f_dve, f_act, f_out, ready, sq = (sem(ctx, n) for n in ("f_dve", "f_act", "f_out", "ready", "sq"))
            with nc.Block() as block:
                @block.vector
                def _(dve):
                    do = Chain(dve, f_dve)
                    av = m.acc[:, :, :].rearrange("p t (h w) -> p t h w", h=H)
                    do(dve.memset(eps[:, :], EPS_LN))
                    do(dve.tensor_scalar(den[:, 0, :, :], av[:, :, :, HD], EPS_DEN, None, ALU.add))
                    do(dve.reciprocal(den[:, 1, :, :], den[:, 0, :, :]))
                    for t in range(NT):
                        do(dve.tensor_tensor(y[:, t, :].rearrange("p (h w) -> p h w", h=H), av[:, t, :, 0:HD],
                                             den[:, 1, t, :].unsqueeze(2).to_broadcast([P, H, HD]), ALU.mult))
                        do(dve.tensor_tensor(y[:, t, :], y[:, t, :], m.xs[:, t, :], ALU.add))
                        do(dve.bn_stats(st[:, t, :], y[:, t, :]))
                        do(dve.bn_aggr(mv[:, t, :], st[:, t, :]))
                    dve.sem_inc(ready, 1)
                    dve.wait_ge(sq, 1)
                    do(dve.reciprocal(std[:, 1, :], std[:, 0, :]))
                    for t in range(NT):
                        dve.tensor_scalar(y[:, t, :], y[:, t, :], mv[:, t, 0:1], std[:, 1, t:t + 1], ALU.subtract, ALU.mult
                                          ).then_inc(f_act, 1)

                @block.scalar
                def _(act):
                    act.wait_ge(ready, 1)
                    nc.scalar.activation(std[:, 0, :], mv[:, :, 1], ACT.Sqrt, bias=eps[:, 0:1]).then_inc(sq, 1)

                @block.sync
                def _(sp):
                    sp.wait_ge(f_act, NT)
                    sp.dma_start(out[0:(NT - 1) * P, :].rearrange("(t p) n -> p t n", p=P), y[:, 0:NT - 1, :]).then_inc(f_out, 16)
                    sp.dma_start(out[(NT - 1) * P:N, :], y[0:N - (NT - 1) * P, NT - 1, :]).then_inc(f_out, 16)
                    sp.wait_ge(f_out, 32)


def kernel(**inputs):
    import numpy as np
    import concourse.bacc as bacc
    from concourse.bass_utils import run_bass_kernel_spmd

    a = {k: np.asarray(v) for k, v in inputs.items()}
    pad_e = EP - E
    x = np.pad(a["x"], ((0, NP - N), (0, 0)))
    src, dst, typ = (a[k].astype(np.int32) for k in ("src", "dst", "edge_type_8"))
    dst = np.concatenate([dst, np.full(pad_e, PAD_DST, np.int32)])
    meta = np.stack([np.pad(src, (0, pad_e)), dst, np.pad(typ, (0, pad_e)), np.arange(EP, dtype=np.int32)], axis=1)
    W = a["L1_gnn_W"]
    WT = np.pad(W.reshape(R, H, HD, D).transpose(3, 0, 1, 2), ((0, 0), (0, 0), (0, 0), (0, 1))).reshape(D, R * ROW)
    attn = np.stack([a["L1_gnn_attn_src"].reshape(2, P), a["L1_gnn_attn_dst"].reshape(2, P)]).transpose(2, 0, 1)
    arrays = {
        "x": x, "xT": x.T, "dst": dst.reshape(EP, 1), "dst_tiles": dst.reshape(TILES_E, P).T, "meta": meta,
        "ef": np.pad(a["edge_attr_64"], ((0, pad_e), (0, 0))),
        "efT": np.tile(np.pad(a["edge_attr_64"].T, ((0, 0), (0, pad_e))), (2, 1)),
        "W1": a["L0_gnn_W1"], "b1": a["L0_gnn_b1"], "W2T": a["L0_gnn_W2"].T, "b2": a["L0_gnn_b2"].reshape(4, P).T,
        "W3": a["L0_gnn_W3"], "b3": a["L0_gnn_b3"], "W4": a["L0_gnn_W4"], "b4": a["L0_gnn_b4"],
        "WT": WT, "Wn": W, "attn": attn,
    }
    arrays = {f"in_{k}": np.ascontiguousarray(v) for k, v in arrays.items()}
    nc = bacc.Bacc("TRN2", target_bir_lowering=False, num_devices=1)
    args = [nc.dram_tensor(k, v.shape, mybir.dt.from_np(v.dtype), kind="ExternalInput").ap() for k, v in arrays.items()]
    out = nc.dram_tensor("out", (N, D), F32, kind="ExternalOutput").ap()
    gnn_kernel(nc, *args, out)
    return run_bass_kernel_spmd(nc, [arrays], core_ids=[0]).results[0]["out"]
```

```python
from contextlib import ExitStack

import concourse.bass as bass
from concourse import mybir

F32 = mybir.dt.float32
I32 = mybir.dt.int32
U32 = mybir.dt.uint32
BF16 = mybir.dt.bfloat16
ALU = mybir.AluOpType
ACT = mybir.ActivationFunctionType
AX = mybir.AxisListType

P = 128
N, E, D, ED, HID, R, H = 2500, 40000, 256, 64, 512, 8, 8
HD = D // H
HW = HD + 1
ROW = H * HW
NT = -(-N // P)
NP = NT * P
U = 16
GU = 16
STEPS = -(-(-(-E // P) + NT) // GU) * GU
ITERS = STEPS // U
GROUPS = STEPS // GU
TSTEPS = STEPS + U
GR = 8
CE = 4
EP = E + 192
CNT = -(-E // P)
TILES_E = EP // P
SC = 8
PAD_DST = 4095
EPS_LN = 1e-5
EPS_DEN = 1e-12


class Chain:

    def __init__(self, eng, sem):
        self.eng, self.sem, self.n = eng, sem, 0

    def __call__(self, ins):
        self.n += 1
        ins.then_inc(self.sem, 1)
        self.eng.wait_ge(self.sem, self.n)


class Mem:
    pass


def wait_step(eng, sem, it, j, ago=0):
    v = it * U + (j + 1 - ago)
    if not isinstance(v, int) or v > 0:
        eng.wait_ge(sem, v)


def run_skewed(eng, stages):
    def body(it):
        for j in range(U):
            for f, lag in stages:
                if j >= lag:
                    f(it, j - lag)
                elif not isinstance(it, int):
                    f(it - 1, j - lag + U)
    body(0)
    with eng.Fori(1, ITERS) as it:
        body(it)
    for j in range(max(lag for _, lag in stages)):
        for f, lag in stages:
            if j < lag:
                f(ITERS - 1, j - lag + U)


def load_row(eng, regs, row, it):
    eng.load(regs, row[0:1, bass.ds(it * U, U)])


def over_tiles(eng, tile):
    tile(0)
    with eng.Fori(1, TILES_E) as t:
        tile(t)


def edge_order(nc, sb, psum, whole, dst, dst_tiles, meta, ef, meta_s, ef_s):
    flag = sb(whole, "flag", [1, 1], I32)
    with ExitStack() as ctx:
        pair = sb(ctx, "pair", [P, 2, CNT], I32)
        fall = sb(ctx, "fall", [P, CNT])
        falls = sb(ctx, "falls", [P, 1])
        ones = sb(ctx, "ones_s", [P, 1])
        fs = psum(ctx, "fs", [1, 1])
        pair_in, falls_in, summed = (whole.enter_context(nc.semaphore(n)) for n in ("pair_in", "falls_in", "falls_summed"))
        with nc.Block() as block:
            @block.sync
            def _(sp):
                for k in range(2):
                    sp.dma_start(pair[:, k, :], dst[k:P * CNT + k, :].rearrange("(p c) o -> p (c o)", p=P)).then_inc(pair_in, 16)

            @block.vector
            def _(dve):
                dve.memset(ones[:, :], 1.0).then_inc(falls_in, 1)
                dve.wait_ge(pair_in, 32)
                dve.scalar_tensor_tensor(fall[:, :], pair[:, 0, :], 1.0, pair[:, 1, :], ALU.mult, ALU.is_gt,
                                         accum_out=falls[:, :]).then_inc(falls_in, 1)
                dve.wait_ge(summed, 1)
                dve.tensor_scalar(flag[:, :], fs[:, :], 0.0, None, ALU.is_gt)

            @block.tensor
            def _(pe):
                pe.wait_ge(falls_in, 2)
                nc.tensor.matmul(fs[:, :], falls[:, :], ones[:, :], start=True, stop=True).then_inc(summed, 1)

    with ExitStack() as ctx:
        key_i = sb(ctx, "key_i", [P, TILES_E], I32)
        key = sb(ctx, "key", [P, 2, TILES_E])
        wide = sb(ctx, "wide", [P, EP])
        stage = sb(ctx, "stage", [P, EP // SC], I32)
        hit = sb(ctx, "hit", [P, EP // SC], BF16)
        lower = sb(ctx, "lower", [P, P])
        part = sb(ctx, "part", [P, SC + 1])
        place = sb(ctx, "place", [P, TILES_E])
        place_i = sb(ctx, "place_i", [P, TILES_E], U32)
        place_now = sb(ctx, "place_now", [P, 1], U32)
        meta_t = sb(ctx, "meta_t", [P, 4], I32)
        (keys_in, stage_in, staged, lower_in, ranked, places, m_in, m_ix, m_out, e_in, e_ix, e_rows, e_turned, e_col,
         e_out, sgate) = (
            whole.enter_context(nc.semaphore("so_" + n)) for n in ("keys_in", "stage_in", "staged", "lower_in", "ranked", "places", "m_in", "m_ix",
                                   "m_out", "e_in", "e_ix", "e_rows", "e_turned", "e_col", "e_out", "gate"))
        ef_rows = sb(ctx, "ef_rows", [P, P])
        ef_cols = sb(ctx, "ef_cols", [P, P])
        identS = sb(ctx, "identS", [P, P])
        pe_t = psum(ctx, "pe_t", [P, 512])
        W = EP // SC
        RK = SC + 4

        with nc.Block() as block:
            @block.sync
            def _(sp):
                unsorted = sp.value_load(flag[0:1, 0:1], min_val=0, max_val=1)
                with sp.If(unsorted > 0):
                    sp.dma_start(key_i[:, :], dst_tiles).then_inc(keys_in, 16)
                    for c in range(SC):
                        if c:
                            sp.wait_ge(staged, c)
                        sp.dma_start(stage[:, :], dst[c * W:(c + 1) * W, :].rearrange("w o -> (w o)").partition_broadcast(P)
                                     ).then_inc(stage_in, 16)
                    sp.wait_ge(places, 1)
                    def tile(t):
                        if not isinstance(t, int):
                            sp.wait_ge(m_out, t * 16)
                        sp.sem_inc(sgate, 1)
                        sp.dma_start(meta_t[:, :], meta[bass.ds(t * P, P), :]).then_inc(m_in, 16)
                    over_tiles(sp, tile)
                    def tile(t):
                        if not isinstance(t, int):
                            sp.wait_ge(e_ix, t)
                        sp.sem_inc(sgate, 1)
                        sp.wait_ge(m_out, TILES_E * 16)
                        sp.dma_start(meta_t[:, :], meta_s[bass.ds(t * P, P), :]).then_inc(e_in, 16)
                        sp.wait_ge(e_col, t + 1)
                        sp.sem_inc(sgate, 1)
                        for half in range(2):
                            sp.dma_start(ef_s[half * ED:(half + 1) * ED, bass.ds(t * P, P)], ef_cols[0:ED, :]).then_inc(e_out, 16)
                    over_tiles(sp, tile)
                    sp.wait_ge(e_out, TILES_E * 32)

            @block.vector
            def _(dve):
                unsorted = dve.value_load(flag[0:1, 0:1], min_val=0, max_val=1)
                with dve.If(unsorted > 0):
                    dve.wait_ge(keys_in, 16)
                    dve.tensor_copy(key[:, 0, :], key_i[:, :]).then_inc(ranked, 1)
                    dve.tensor_scalar(key[:, 1, :], key_i[:, :], 0.25, None, ALU.add).then_inc(ranked, 1)
                    for c in range(SC):
                        dve.wait_ge(stage_in, (c + 1) * 16)
                        dve.tensor_scalar(wide[:, c * W:(c + 1) * W], stage[:, :], 0.25, None, ALU.add).then_inc(staged, 1)
                    dve.wait_ge(lower_in, 4)
                    dve.wait_ge(staged, SC)
                    dve.wait_ge(ranked, 2)
                    dve.memset(ef_rows[:, :], 0.0).then_inc(ranked, 1)
                    def tile(t):
                        own = wide[:, bass.ds(t * P, P)]
                        for c in range(SC):
                            dve.wait_ge(ranked, t * RK + (c + 3))
                            dve.tensor_scalar(hit[:, :], wide[:, c * W:(c + 1) * W], key[:, 0, bass.ds(t, 1)], None,
                                              ALU.is_lt, ALU.add, accum_out=part[:, c:c + 1]).then_inc(ranked, 1)
                        dve.wait_ge(ranked, t * RK + (SC + 3))
                        dve.scalar_tensor_tensor(hit[:, 0:P], own, key[:, 1, bass.ds(t, 1)], lower[:, :],
                                                 ALU.is_equal, ALU.mult, accum_out=part[:, SC:SC + 1]).then_inc(ranked, 1)
                        dve.wait_ge(ranked, t * RK + (SC + 4))
                        dve.tensor_scalar(own, own, -0.5, None, ALU.add).then_inc(ranked, 1)
                        dve.wait_ge(ranked, t * RK + (SC + 5))
                        dve.tensor_reduce(place[:, bass.ds(t, 1)], part[:, :], AX.X, ALU.add).then_inc(ranked, 1)
                        dve.wait_ge(ranked, t * RK + (SC + 6))
                        dve.sem_inc(ranked, 1)
                    over_tiles(dve, tile)
                    dve.wait_ge(ranked, TILES_E * RK + 3)
                    dve.tensor_copy(place_i[:, :], place[:, :]).then_inc(places, 1)

            @block.gpsimd
            def _(pool):
                unsorted = pool.value_load(flag[0:1, 0:1], min_val=0, max_val=1)
                with pool.If(unsorted > 0):
                    pool.memset(lower[:, :], 1.0).then_inc(lower_in, 1)
                    pool.memset(identS[:, :], 0.0).then_inc(lower_in, 1)
                    pool.wait_ge(lower_in, 2)
                    pool.affine_select(out=lower[:, :], in_=lower[:, :], compare_op=ALU.is_gt, fill=0.0,
                                       base=0, pattern=[[-1, P]], channel_multiplier=1).then_inc(lower_in, 1)
                    pool.affine_select(out=identS[:, :], in_=identS[:, :], compare_op=ALU.not_equal, fill=1.0,
                                       base=0, pattern=[[-1, P]], channel_multiplier=1).then_inc(lower_in, 1)
                    pool.wait_ge(places, 1)
                    def tile(t):
                        pool.wait_ge(m_in, (t + 1) * 16)
                        pool.sem_inc(sgate, 1)
                        if not isinstance(t, int):
                            pool.wait_ge(m_out, t * 16)
                        pool.sem_inc(sgate, 1)
                        pool.tensor_copy(place_now[:, :], place_i[:, bass.ds(t, 1)]).then_inc(m_ix, 1)
                        pool.wait_ge(m_ix, t + 1)
                        pool.sem_inc(sgate, 1)
                        pool.indirect_dma_start(meta_s, bass.IndirectOffsetOnAxis(ap=place_now[:, 0:1], axis=0),
                                                meta_t[:, :], None).then_inc(m_out, 16)
                    over_tiles(pool, tile)
                    pool.wait_ge(m_out, TILES_E * 16)
                    def tile(t):
                        pool.wait_ge(e_in, (t + 1) * 16)
                        pool.sem_inc(sgate, 1)
                        if not isinstance(t, int):
                            pool.wait_ge(e_turned, t)
                        pool.sem_inc(sgate, 1)
                        pool.tensor_copy(place_now[:, :], meta_t[:, 3:4]).then_inc(e_ix, 1)
                        pool.wait_ge(e_ix, t + 1)
                        pool.sem_inc(sgate, 1)
                        pool.indirect_dma_start(ef_rows[:, 0:ED], None, ef,
                                                bass.IndirectOffsetOnAxis(ap=place_now[:, 0:1], axis=0)).then_inc(e_rows, 16)
                    over_tiles(pool, tile)

            @block.tensor
            def _(pe):
                unsorted = pe.value_load(flag[0:1, 0:1], min_val=0, max_val=1)
                with pe.If(unsorted > 0):
                    pe.wait_ge(lower_in, 4)
                    pe.wait_ge(ranked, 3)
                    def tile(t):
                        pe.wait_ge(e_rows, (t + 1) * 16)
                        if not isinstance(t, int):
                            pe.wait_ge(e_col, t)
                        pe.transpose(pe_t[:, 0:P], ef_rows[:, :], identS[:, :]).then_inc(e_turned, 1)
                    over_tiles(pe, tile)

            @block.scalar
            def _(act):
                unsorted = act.value_load(flag[0:1, 0:1], min_val=0, max_val=1)
                with act.If(unsorted > 0):
                    def tile(t):
                        act.wait_ge(e_turned, t + 1)
                        if not isinstance(t, int):
                            act.wait_ge(e_out, t * 32)
                        nc.scalar.activation(ef_cols[:, :], pe_t[:, 0:P], ACT.Copy).then_inc(e_col, 1)
                    over_tiles(act, tile)
    return flag


def gnn_kernel(nc, x, xT, dst, dst_tiles, meta, ef_rows, efT, W1, b1, W2T, b2, W3, b3, W4, b4, WT, Wn, attn, out):
    A_dram = nc.dram_tensor("A_table", (NP, HID), F32, kind="Internal").ap()
    T_dram = nc.dram_tensor("L1_table", (R * NP, ROW), F32, kind="Internal").ap()
    mm = nc.tensor.matmul

    m = Mem()
    with ExitStack() as whole:
        def sb(ctx, name, shape, dt=F32):
            return ctx.enter_context(nc.sbuf_tensor(name, shape, dt))

        def psum(ctx, name, shape):
            return ctx.enter_context(nc.psum_tensor(name, shape, F32))

        done_with = []

        def sem(ctx, name):
            handle = ctx.enter_context(nc.semaphore(name))
            done_with.append(handle)
            return handle

        meta_s = nc.dram_tensor("meta_sorted", (EP, 4), I32, kind="Internal").ap()
        efT_s = nc.dram_tensor("efT_sorted", (2 * ED, EP), F32, kind="Internal").ap()
        flag = edge_order(nc, sb, psum, whole, dst, dst_tiles, meta, ef_rows, meta_s, efT_s)

        def gather_sem(name):
            return whole.enter_context(nc.semaphore(name))

        m.ident = sb(whole, "ident", [P, P])
        m.iota = sb(whole, "iota", [P, P])
        m.ones = sb(whole, "ones", [P, P])
        m.xs = sb(whole, "xs", [P, NT, D])
        m.xTs = sb(whole, "xTs", [P, 2, NP])
        m.dl = sb(whole, "dl", [P, TSTEPS])
        m.tab_ix = sb(whole, "tab_ix", [P, TSTEPS], U32)
        m.emask = sb(whole, "emask", [P, TSTEPS, R], BF16)
        m.cont = sb(whole, "cont", [P, TSTEPS])
        m.nt_i = sb(whole, "nt_i", [1, TSTEPS], I32)
        m.start_i = sb(whole, "start_i", [1, TSTEPS], I32)

        m.ntb = sb(whole, "ntb", [P, TSTEPS])
        m.iota_r = sb(whole, "iota_r", [P, R])
        m.degs = sb(whole, "degs", [P, TSTEPS])
        m.deg = sb(whole, "deg", [P, NT])

        m.agg = sb(whole, "agg", [P, NT, HID])
        m.acc = m.agg[:, :, 0:ROW]
        l0_edges = whole.enter_context(ExitStack())
        m.w1e = sb(l0_edges, "w1e", [P, 2, HID], BF16)
        m.B = sb(l0_edges, "B", [P, NT, 3, HID], BF16)

        meta_b = sb(l0_edges, "meta_b", [P, U, 4], I32)
        ef = sb(l0_edges, "ef", [P, U, P])
        meta_in = [sem(l0_edges, f"meta_in{j}") for j in range(U)]
        ef_in = [sem(l0_edges, f"ef_in{j}") for j in range(U)]

        with ExitStack() as ctx:
            w1 = sb(ctx, "w1", [P, 4, HID])
            b1b = sb(ctx, "b1b", [P, HID])
            w1f = sb(ctx, "w1f", [P, 2, HID])
            w1p = sb(ctx, "w1p", [P, 3, HID], BF16)
            Ab = sb(ctx, "Ab", [P, 2, HID])
            dsti = sb(ctx, "dsti", [P, CNT], I32)
            dstf = sb(ctx, "dstf", [P, CNT])
            below = sb(ctx, "below", [P, CNT])
            cnt = sb(ctx, "cnt", [P, NT + 1])
            upper = sb(ctx, "upper", [P, P])
            n128 = sb(ctx, "n128", [P, P])
            steps_f = sb(ctx, "steps_f", [P, TSTEPS])
            col = sb(ctx, "col", [NT, 8])
            coli = sb(ctx, "coli", [NT, 2], I32)
            sel = sb(ctx, "sel", [NT, 2, TSTEPS])
            sval = sb(ctx, "sval", [NT, TSTEPS])
            Bf = sb(ctx, "Bf", [P, 2, 2, HID])
            pa = psum(ctx, "pa", [P, 2, HID])
            pb = psum(ctx, "pb", [P, 2, HID])
            pc = psum(ctx, "pc", [P, HID])
            pn = psum(ctx, "pn", [P, HID])
            in_dst = sem(ctx, "in_dst")
            in_x = sem(ctx, "in_x")
            in_rest = sem(ctx, "in_rest")
            in_w1e = sem(ctx, "in_w1e")
            steps_in = sem(ctx, "steps_in")
            w1_parts = sem(ctx, "w1_parts")
            set0 = sem(ctx, "set0")
            consts = sem(ctx, "consts")
            dve_done = sem(ctx, "dve_done")
            counted = sem(ctx, "counted")
            tiles_in = sem(ctx, "tiles_in")
            sel_in = sem(ctx, "sel_in")
            pe_step = sem(ctx, "pe_step")
            split = [sem(ctx, f"split{k}") for k in range(4)]
            A_mm, A_out, B_mm, B_out = (sem(ctx, n) for n in ("A_mm", "A_out", "B_mm", "B_out"))
            A_wr = [sem(ctx, f"A_wr{k}") for k in range(2)]

            with nc.Block() as block:
                @block.sync
                def _(sp):
                    sp.dma_start(dsti[:, :], dst[0:P * CNT, :].rearrange("(p c) o -> p (c o)", p=P)).then_inc(in_dst, 16)
                    sp.dma_start(m.xTs[:, :, :], xT.rearrange("(c p) n -> p c n", p=P)).then_inc(in_x, 16)
                    sp.dma_start(w1[:, :, :], W1[0:2 * D, :].rearrange("(c p) n -> p c n", p=P)).then_inc(in_x, 16)
                    sp.dma_start(b1b[:, :], b1.partition_broadcast(P)).then_inc(in_x, 16)
                    for half in range(2):
                        sp.dma_start(w1f[half * ED:(half + 1) * ED, 0, :], W1[2 * D:2 * D + ED, :]).then_inc(in_w1e, 16)
                    sp.dma_start(m.xs[:, :, :], x.rearrange("(t p) n -> p t n", p=P)).then_inc(in_rest, 16)
                    regs = [sp.alloc_register(f"start_0_{j}") for j in range(U)]

                    def first_edges(meta, efT):
                        for j in range(U):
                            first = sp.snap(regs[j], min_val=0, max_val=E)
                            sp.dma_start(meta_b[:, j, :], meta[bass.ds(first, P), :]).then_inc(meta_in[j], 16)
                            sp.dma_start(ef[:, j, :], efT[:, bass.ds(first, P)]).then_inc(ef_in[j], 16)

                    sp.wait_ge(in_rest, 16)
                    sp.wait_ge(steps_in, 1)
                    sp.load(regs, m.start_i[0:1, 0:U])
                    unsorted = sp.value_load(flag[0:1, 0:1], min_val=0, max_val=1)
                    with sp.If(unsorted > 0):
                        first_edges(meta_s, efT_s)
                    with sp.Else():
                        first_edges(meta, efT)

                @block.gpsimd
                def _(pool):
                    pool.memset(m.ident[:, :], 0.0).then_inc(set0, 1)
                    pool.memset(upper[:, :], 1.0).then_inc(set0, 1)
                    for t, pattern, mult in ((m.iota, [[1, P]], 0), (n128, [[0, P]], P), (steps_f, [[1, TSTEPS]], 0),
                                             (m.iota_r, [[1, R]], 0)):
                        pool.iota(t[:, :], pattern, base=0, channel_multiplier=mult,
                                  allow_small_or_imprecise_dtypes=True).then_inc(consts, 1)
                    pool.memset(m.ones[:, :], 1.0).then_inc(consts, 1)
                    pool.wait_ge(set0, 2)
                    pool.affine_select(out=m.ident[:, :], in_=m.ident[:, :], compare_op=ALU.not_equal, fill=1.0,
                                       base=0, pattern=[[-1, P]], channel_multiplier=1).then_inc(consts, 1)
                    pool.affine_select(out=upper[:, :], in_=upper[:, :], compare_op=ALU.is_gt, fill=0.0,
                                       base=0, pattern=[[1, P]], channel_multiplier=-1).then_inc(consts, 1)
                    pool.memset(m.agg[:, :, :], 0.0).then_inc(consts, 1)

                @block.vector
                def _(dve):
                    do = Chain(dve, dve_done)
                    dve.wait_ge(in_dst, 16)
                    do(dve.tensor_copy(dstf[:, :], dsti[:, :]))
                    do(dve.memset(cnt[:, 0:1], 0.0))
                    for n in range(1, NT + 1):
                        do(dve.tensor_scalar(below[:, :], dstf[:, :], float(P * n), None, ALU.is_lt, ALU.add,
                                             accum_out=cnt[:, n:n + 1]))
                    dve.sem_inc(counted, 1)
                    dve.wait_ge(pe_step, 1)
                    do(dve.tensor_copy(col[:, 0:2], pn[0:NT, 0:2]))
                    do(dve.tensor_tensor(col[:, 2:3], col[:, 1:2], col[:, 0:1], ALU.subtract))
                    do(dve.tensor_scalar(coli[:, 0:1], col[:, 2:3], float(P - 1), None, ALU.add))
                    do(dve.tensor_scalar(coli[:, 1:2], coli[:, 0:1], 7, None, ALU.arith_shift_right))
                    do(dve.tensor_copy(col[:, 3:4], coli[:, 1:2]))
                    dve.sem_inc(tiles_in, 1)
                    dve.wait_ge(pe_step, 2)
                    do(dve.tensor_copy(col[:, 4:5], pn[0:NT, 2:3]))
                    do(dve.tensor_tensor(col[:, 5:6], col[:, 4:5], col[:, 3:4], ALU.add))
                    do(dve.tensor_scalar(col[:, 6:7], col[:, 4:5], float(-P), float(-E), ALU.mult, ALU.add))
                    do(dve.tensor_tensor(col[:, 7:8], col[:, 6:7], col[:, 0:1], ALU.add))
                    dve.wait_ge(consts, 8)
                    do(dve.tensor_scalar(sel[:, 0, :], steps_f[0:NT, :], col[:, 4:5], None, ALU.is_ge))
                    do(dve.scalar_tensor_tensor(sel[:, 1, :], steps_f[0:NT, :], col[:, 5:6], sel[:, 0, :], ALU.is_lt, ALU.mult))
                    do(dve.tensor_scalar(sval[:, :], steps_f[0:NT, :], float(P), col[:, 7:8], ALU.mult, ALU.add))
                    do(dve.tensor_tensor(sval[:, :], sval[:, :], sel[:, 1, :], ALU.mult))
                    dve.sem_inc(sel_in, 1)
                    dve.wait_ge(pe_step, 3)
                    do(dve.tensor_copy(m.ntb[:, :], pn[:, 0:TSTEPS]))
                    do(dve.tensor_scalar(m.nt_i[:, :], m.ntb[0:1, :], 1.0 / P, None, ALU.mult))
                    do(dve.tensor_scalar(m.start_i[:, :], pc[0:1, 0:TSTEPS], float(E), None, ALU.add))
                    dve.sem_inc(steps_in, 1)
                    do(dve.memset(m.cont[:, 0:1], 0.0))
                    do(dve.tensor_tensor(m.cont[:, 1:TSTEPS], m.ntb[:, 1:TSTEPS], m.ntb[:, 0:TSTEPS - 1], ALU.is_equal))
                    dve.wait_ge(in_x, 48)
                    for t in range(NT):
                        dve.wait_ge(B_mm, t + 1)
                        dve.tensor_tensor(Bf[:, t % 2, 0, :], pb[:, t % 2, :], b1b[:, :], ALU.add).then_inc(B_out, 1)
                        dve.wait_ge(split[0], t + 1)
                        dve.tensor_tensor(Bf[:, t % 2, 1, :], Bf[:, t % 2, 0, :], m.B[:, t, 0, :], ALU.subtract).then_inc(split[1], 1)
                        dve.wait_ge(split[2], t + 1)
                        dve.tensor_tensor(m.B[:, t, 2, :], Bf[:, t % 2, 1, :], m.B[:, t, 1, :], ALU.subtract)
                    wp = Chain(dve, w1_parts)
                    dve.wait_ge(in_w1e, 32)
                    wp(dve.tensor_copy(w1p[:, 0, :], w1f[:, 0, :]))
                    wp(dve.tensor_tensor(w1f[:, 1, :], w1f[:, 0, :], w1p[:, 0, :], ALU.subtract))
                    wp(dve.tensor_copy(w1p[:, 1, :], w1f[:, 1, :]))
                    wp(dve.tensor_tensor(w1p[:, 2, :], w1f[:, 1, :], w1p[:, 1, :], ALU.subtract))
                    for half, (a, b) in enumerate(((0, 2), (1, 0))):
                        ps = slice(half * ED, (half + 1) * ED)
                        dve.tensor_copy(m.w1e[ps, 0, :], w1p[ps, a, :])
                        dve.tensor_copy(m.w1e[ps, 1, :], w1p[ps, b, :])

                @block.tensor
                def _(pe):
                    pe.wait_ge(consts, 8)
                    pe.wait_ge(counted, 1)
                    mm(pn[0:NT, 0:1], cnt[:, 0:NT], m.ones[:, 0:1], start=True, stop=True)
                    mm(pn[0:NT, 1:2], cnt[:, 1:NT + 1], m.ones[:, 0:1], start=True, stop=True).then_inc(pe_step, 1)
                    pe.wait_ge(tiles_in, 1)
                    mm(pn[0:NT, 2:3], upper[0:NT, 0:NT], col[:, 3:4], start=True, stop=True).then_inc(pe_step, 1)
                    pe.wait_ge(sel_in, 1)
                    mm(pn[:, 0:TSTEPS], n128[0:NT, :], sel[:, 1, :], start=True, stop=True)
                    mm(pc[0:1, 0:TSTEPS], m.ones[0:NT, 0:1], sval[:, :], start=True, stop=True).then_inc(pe_step, 1)
                    pe.wait_ge(in_x, 48)
                    for t in range(NT):
                        for k, (ps, done, free) in enumerate(((pa, A_mm, A_out), (pb, B_mm, B_out))):
                            if t >= 2:
                                pe.wait_ge(free, t - 1)
                            for c in range(2):
                                last = mm(ps[:, t % 2, :], m.xTs[:, c, t * P:(t + 1) * P], w1[:, 2 * k + c, :],
                                          start=(c == 0), stop=(c == 1))
                            last.then_inc(done, 1)

                @block.scalar
                def _(act):
                    for t in range(NT):
                        act.wait_ge(A_mm, t + 1)
                        if t >= 2:
                            act.wait_ge(A_wr[t % 2], 16 * (t // 2))
                        nc.scalar.activation(Ab[:, t % 2, :], pa[:, t % 2, :], ACT.Copy).then_inc(A_out, 1)
                        act.wait_ge(A_out, t + 1)
                        act.dma_start(A_dram[t * P:(t + 1) * P, :], Ab[:, t % 2, :]).then_inc(A_wr[t % 2], 16)
                        act.wait_ge(B_out, t + 1)
                        nc.scalar.activation(m.B[:, t, 0, :], Bf[:, t % 2, 0, :], ACT.Copy).then_inc(split[0], 1)
                        act.wait_ge(split[1], t + 1)
                        nc.scalar.activation(m.B[:, t, 1, :], Bf[:, t % 2, 1, :], ACT.Copy).then_inc(split[2], 1)
                    for k in range(2):
                        act.wait_ge(A_wr[k], 16 * (NT // 2))

        with ExitStack() as ctx:
            G = sb(ctx, "G0", [P, GR, HID])
            ixr = sb(ctx, "ixr0", [P, U], U32)
            ep = sb(ctx, "ep", [P, 3, 2, CE * P], BF16)
            er = sb(ctx, "er", [P, CE * P])
            oh = sb(ctx, "oh0", [P, 8, P])
            ohT = sb(ctx, "ohT0", [P, 4, P], BF16)
            hb = sb(ctx, "hb", [P, 4, HID])
            pt = psum(ctx, "pt", [P, 2, 512])
            pz = psum(ctx, "pz", [P, 2, HID])
            pp = psum(ctx, "pp", [P, 2, HID])
            g_in = [gather_sem(f"g_in{j}") for j in range(GR)]
            e0_made, e_rest, e1_made, e_split, e_low = (sem(ctx, n) for n in ("e0_made", "e_rest", "e1_made", "e_split", "e_low"))
            (ix_copied, gate, prepared, prep, oh_made, turned, ohT_made, z_made, z_summed, h_made, p_made, p_added) = (
                sem(ctx, n) for n in ("ix_copied", "gate", "prepared", "prep", "oh_made", "turned", "ohT_made", "z_made",
                                      "z_summed", "h_made", "p_made", "p_added"))

            def chunk_of(c):
                at = c * CE % U
                return ef[:, at:at + CE, :].rearrange("p u n -> p (u n)")

            with nc.Block() as block:
                @block.sync
                def _(sp):
                    regs = [sp.alloc_register(f"start_e{j}") for j in range(U)]
                    mregs = [sp.alloc_register(f"start_m{j}") for j in range(U)]

                    def load_meta(meta, it, j):
                        if j == 0:
                            load_row(sp, mregs, m.start_i, it)
                            if not isinstance(it, int) or it > 0:
                                sp.wait_ge(prepared, it)
                                sp.sem_inc(gate, 1)
                                sp.wait_ge(ix_copied, 2 * it)
                                sp.sem_inc(gate, 1)
                        first = sp.snap(mregs[j], min_val=0, max_val=E)
                        sp.dma_start(meta_b[:, j, :], meta[bass.ds(first, P), :]).then_inc(meta_in[j], 16)

                    def load_ef(efT, it, j):
                        if j == 0:
                            load_row(sp, regs, m.start_i, it)
                        if j % CE == 0 and (not isinstance(it, int) or it > 0):
                            sp.wait_ge(e_split, (it - 1) * (U // CE) + (j // CE + 1))
                            sp.sem_inc(gate, 1)
                        first = sp.snap(regs[j], min_val=0, max_val=E)
                        sp.dma_start(ef[:, j, :], efT[:, bass.ds(first, P)]).then_inc(ef_in[j], 16)

                    def iteration(meta, efT, it):
                        if not isinstance(it, int) or it > 0:
                            for j in range(U):
                                load_ef(efT, it, j)
                        for j in range(U):
                            load_meta(meta, it + 1, j)

                    def program(meta, efT):
                        iteration(meta, efT, 0)
                        with sp.Fori(1, ITERS) as it:
                            iteration(meta, efT, it)
                        for j in range(CE):
                            load_ef(efT, ITERS, j)
                        for j in range(U):
                            sp.wait_ge(meta_in[j], 16 * (ITERS + 1))

                    unsorted = sp.value_load(flag[0:1, 0:1], min_val=0, max_val=1)
                    with sp.If(unsorted > 0):
                        program(meta_s, efT_s)
                    with sp.Else():
                        program(meta, efT)

                @block.gpsimd
                def _(pool):
                    def gather(it):
                        for half in range(2):
                            js = range(half * GR, (half + 1) * GR)
                            for j in js:
                                pool.wait_ge(meta_in[j], (it + 1) * 16)
                                if not isinstance(it, int):
                                    pool.wait_ge(g_in[j % GR], (it * 2 - 1 + half) * 16)
                            pool.sem_inc(gate, 1)
                            pool.tensor_copy(ixr[:, js.start:js.stop], meta_b[:, js.start:js.stop, 0]).then_inc(ix_copied, 1)
                            pool.wait_ge(ix_copied, it * 2 + half + 1)
                            for j in js:
                                pool.sem_inc(gate, 1)
                                wait_step(pool, z_summed, it, j, ago=GR)
                                pool.sem_inc(gate, 1)
                                pool.indirect_dma_start(G[:, j % GR, :], None, A_dram,
                                                        bass.IndirectOffsetOnAxis(ap=ixr[:, j:j + 1], axis=0)
                                                        ).then_inc(g_in[j % GR], 16)

                    gather(0)
                    with pool.Fori(1, ITERS) as it:
                        gather(it)

                @block.vector
                def _(dve):
                    regs = [dve.alloc_register(f"nt_v{j}") for j in range(U)]

                    def prepare(it):
                        for j in range(U):
                            dve.wait_ge(meta_in[j], (it + 1) * 16)
                        at = bass.ds(it * U, U)
                        dve.tensor_tensor(m.dl[:, at], meta_b[:, :, 1], m.ntb[:, at], ALU.subtract).then_inc(prep, 1)
                        dve.scalar_tensor_tensor(m.tab_ix[:, at], meta_b[:, :, 2], float(NP), meta_b[:, :, 0], ALU.mult, ALU.add
                                                 ).then_inc(prep, 1)
                        dve.tensor_tensor(m.emask[:, at, :], meta_b[:, :, 2].unsqueeze(2).to_broadcast([P, U, R]),
                                          m.iota_r[:, :].unsqueeze(1).to_broadcast([P, U, R]), ALU.is_equal).then_inc(prep, 1)
                        dve.wait_ge(prep, (it + 1) * 3)
                        dve.sem_inc(prepared, 1)

                    def one_hot(it, j):
                        if j == 11:
                            prepare(it + 1)
                        wait_step(dve, p_made, it, j, ago=8)
                        dve.tensor_scalar(oh[:, j % 8, :], m.iota[:, :], m.dl[:, bass.ds(it * U + j, 1)], None,
                                          ALU.is_equal).then_inc(oh_made, 1)

                    def add_rows(it, j):
                        wait_step(dve, z_made, it, j)
                        dve.wait_ge(g_in[j % GR], (it * 2 + j // GR + 1) * 16)
                        wait_step(dve, p_made, it, j, ago=4)
                        dve.tensor_tensor(hb[:, j % 4, :], pz[:, j % 2, :], G[:, j % GR, :], ALU.add).then_inc(z_summed, 1)

                    def accumulate(it, j):
                        if j == 0:
                            load_row(dve, regs, m.nt_i, it)
                        nt = dve.snap(regs[j], min_val=0, max_val=NT - 1)
                        wait_step(dve, p_made, it, j)
                        wait_step(dve, p_added, it, j, ago=1)
                        a = m.agg[:, bass.ds(nt, 1), :].rearrange("p o n -> p (o n)")
                        dve.tensor_tensor(a, a, pp[:, j % 2, :], ALU.add).then_inc(p_added, 1)

                    def less_e0(it, c):
                        dve.wait_ge(e0_made, it * (U // CE) + (c + 1))
                        if not isinstance(it, int) or it + c > 0:
                            dve.wait_ge(e_split, it * (U // CE) + c)
                        dve.tensor_tensor(er[:, :], chunk_of(c), ep[:, 0, c % 2, :], ALU.subtract).then_inc(e_rest, 1)

                    def copy_low(it, c):
                        dve.tensor_copy(ep[0:ED, 2, c % 2, :], ep[0:ED, 0, c % 2, :]).then_inc(e_low, 1)

                    def last_parts(it, c):
                        dve.wait_ge(e_low, it * (U // CE) + (c + 1))
                        dve.wait_ge(e1_made, it * (U // CE) + (c + 1))
                        dve.tensor_tensor(ep[ED:P, 2, c % 2, :], er[ED:P, :], ep[ED:P, 1, c % 2, :], ALU.subtract
                                          ).then_inc(e_split, 1)

                    def split_next(it, j):
                        if j % CE == 1:
                            less_e0(it, j // CE + 1)
                        if j % CE == 2:
                            copy_low(it, j // CE + 1)
                        if j % CE == 3:
                            last_parts(it, j // CE + 1)

                    prepare(0)
                    less_e0(0, 0)
                    copy_low(0, 0)
                    last_parts(0, 0)
                    run_skewed(dve, [(one_hot, 0), (accumulate, 5), (add_rows, 2), (split_next, 0)])

                @block.scalar
                def _(act):
                    def copy_turned(it, j):
                        wait_step(act, turned, it, j)
                        wait_step(act, z_made, it, j, ago=4)
                        nc.scalar.activation(ohT[:, j % 4, :], pt[:, j % 2, 0:P], ACT.Copy,
                                             accum_out=m.degs[:, bass.ds(it * U + j, 1)]).then_inc(ohT_made, 1)

                    def relu(it, j):
                        wait_step(act, z_summed, it, j)
                        nc.scalar.activation(hb[:, j % 4, :], hb[:, j % 4, :], ACT.Relu).then_inc(h_made, 1)

                    def first_part(it, c):
                        for j in range(CE):
                            if c < U // CE:
                                act.wait_ge(ef_in[c * CE + j], (it + 1) * 16)
                            else:
                                act.wait_ge(ef_in[j], (it + 2) * 16)
                        if not isinstance(it, int) or it * U + (c - 1) * CE > 0:
                            act.wait_ge(z_made, it * U + (c - 1) * CE)
                        nc.scalar.activation(ep[:, 0, c % 2, :], chunk_of(c), ACT.Copy).then_inc(e0_made, 1)

                    def second_part(it, c):
                        act.wait_ge(e_rest, it * (U // CE) + (c + 1))
                        nc.scalar.activation(ep[:, 1, c % 2, :], er[:, :], ACT.Copy).then_inc(e1_made, 1)

                    def split_next(it, j):
                        if j % CE == 0:
                            first_part(it, j // CE + 1)
                        if j % CE == 2:
                            second_part(it, j // CE + 1)

                    first_part(0, 0)
                    second_part(0, 0)
                    run_skewed(act, [(copy_turned, 1), (relu, 3), (split_next, 0)])

                @block.tensor
                def _(pe):
                    regs = [pe.alloc_register(f"nt_p{j}") for j in range(U)]

                    def turn(it, j):
                        wait_step(pe, oh_made, it, j)
                        wait_step(pe, ohT_made, it, j, ago=2)
                        pe.transpose(pt[:, j % 2, 0:P], oh[:, j % 8, :], m.ident[:, :]).then_inc(turned, 1)

                    def preact(it, j):
                        if j == 0:
                            load_row(pe, regs, m.nt_i, it)
                        nt = pe.snap(regs[j], min_val=0, max_val=NT - 1)
                        wait_step(pe, z_summed, it, j, ago=2)
                        pe.wait_ge(e_split, it * (U // CE) + (j // CE + 1))
                        for k, w in ((0, 0), (1, 0), (2, 1)):
                            mm(pz[:, j % 2, :], ep[:, k, j // CE % 2, j % CE * P:(j % CE + 1) * P], m.w1e[:, w, :],
                               start=(k == 0), stop=False)
                        wait_step(pe, ohT_made, it, j)
                        Bn = m.B[:, bass.ds(nt, 1), :, :].rearrange("p o k n -> p (o k) n")
                        for k in range(3):
                            last = mm(pz[:, j % 2, :], ohT[:, j % 4, :], Bn[:, k, :], start=False, stop=(k == 2))
                        last.then_inc(z_made, 1)

                    def segsum(it, j):
                        wait_step(pe, h_made, it, j)
                        wait_step(pe, p_added, it, j, ago=2)
                        mm(pp[:, j % 2, :], oh[:, j % 8, :], hb[:, j % 4, :], start=True, stop=True).then_inc(p_made, 1)

                    run_skewed(pe, [(turn, 1), (preact, 2), (segsum, 4)])

        l0_edges.close()
        m.sdt = sb(whole, "sdt", [P, NT, 3, R * H], BF16)
        l1_weights = whole.enter_context(ExitStack())
        wt = sb(l1_weights, "wt", [P, 2, R * ROW])
        wn = sb(l1_weights, "wn", [P, R, 2, D])
        at = sb(l1_weights, "at", [P, 2, 2])
        w_in = l1_weights.enter_context(nc.semaphore("w_in"))
        finished = list(done_with)
        with ExitStack() as ctx:
            w2T = sb(ctx, "w2T", [P, 4, HID])
            w3 = sb(ctx, "w3", [P, 6, HID])
            w23 = sb(ctx, "w23", [P, 4, HID])
            w4 = sb(ctx, "w4", [P, 4, D])
            b2c = sb(ctx, "b2c", [P, 4])
            b2w = sb(ctx, "b2w", [P, 4, P])
            b23 = sb(ctx, "b23", [P, HID])
            b3b = sb(ctx, "b3b", [P, HID])
            b4b = sb(ctx, "b4b", [P, D])
            aT = sb(ctx, "aT", [P, 2, HID])
            base = sb(ctx, "base", [P, 2, HID])
            g = sb(ctx, "g", [P, 2, HID])
            gT = sb(ctx, "gT", [P, 2, HID])
            y = sb(ctx, "y", [P, 2, D])
            st = sb(ctx, "st", [P, 2, 12])
            eps = sb(ctx, "eps", [P, 1])
            sum_deg = sem(ctx, "sum_deg")
            q_aT = psum(ctx, "q_aT", [P, 2, HID])
            q_g = psum(ctx, "q_g", [P, 2, HID])
            q_gT = psum(ctx, "q_gT", [P, 2, HID])
            q_y = psum(ctx, "q_y", [P, 512])
            q_xT = psum(ctx, "q_xT", [P, 512])
            (w23_in, w_in0, bw_made, w23_mm, w23_made, b23_made, agg_turned, aT_made, g_mm, base_made, g_made, g_turned,
             gT_made, y_mm, y_bias, y_made, stats, var_made, std_made, rstd, x1_made, x1_turned, xT_made) = (
                sem(ctx, "n_" + n) for n in (
                    "w23_in", "w_in", "bw_made", "w23_mm", "w23_made", "b23_made", "agg_turned", "aT_made", "g_mm",
                    "base_made", "g_made", "g_turned", "gT_made", "y_mm", "y_bias", "y_made", "stats", "var_made",
                    "std_made", "rstd", "x1_made", "x1_turned", "xT_made"))

            def run_tiles(stages):
                for i in range(NT + max(lag for _, lag in stages)):
                    for f, lag in stages:
                        if 0 <= i - lag < NT:
                            f(i - lag)

            def ago(eng, sm, t, n):
                if t - n >= 0:
                    eng.wait_ge(sm, t - n + 1)

            with nc.Block() as block:
                @block.sync
                def _(sp):
                    sp.dma_start(w3[:, :, :], W3.rearrange("(c p) n -> p c n", p=P)).then_inc(w23_in, 16)
                    sp.dma_start(b2c[:, :], b2).then_inc(w23_in, 16)
                    sp.dma_start(b3b[:, :], b3.partition_broadcast(P)).then_inc(w_in0, 16)
                    sp.dma_start(b4b[:, :], b4.partition_broadcast(P)).then_inc(w_in0, 16)
                    sp.dma_start(w4[:, :, :], W4.rearrange("(c p) n -> p c n", p=P)).then_inc(w_in0, 16)
                    sp.wait_ge(w_in0, 48)
                    sp.dma_start(wt[:, :, :], WT.rearrange("(c p) n -> p c n", p=P)).then_inc(w_in, 16)
                    sp.dma_start(wn[:, :, :, :], Wn.rearrange("r (c p) n -> p r c n", p=P)).then_inc(w_in, 16)
                    sp.dma_start(at[:, :, :], attn).then_inc(w_in, 16)

                @block.gpsimd
                def _(pool):
                    for handle in finished:
                        pool.sem_clear(handle)

                @block.tensor
                def _(pe):
                    def turn_agg(t):
                        ago(pe, aT_made, t, 2)
                        for c in range(4):
                            last = pe.transpose(q_aT[:, t % 2, c * P:(c + 1) * P], m.agg[:, t, c * P:(c + 1) * P], m.ident[:, :])
                        last.then_inc(agg_turned, 1)

                    def hidden(t):
                        if t == 0:
                            pe.wait_ge(w23_in, 48)
                            pe.wait_ge(bw_made, 1)
                            for k in range(4):
                                last = mm(q_y[:, :], b2w[:, k, :], w3[:, 2 + k, :], start=(k == 0), stop=(k == 3))
                            last.then_inc(b23_made, 1)
                            for c in range(4):
                                out_q = (q_g, q_gT)[c // 2][:, c % 2, :]
                                for k in range(4):
                                    last = mm(out_q, w2T[:, k, c * P:(c + 1) * P], w3[:, 2 + k, :], start=(k == 0), stop=(k == 3))
                                last.then_inc(w23_mm, 1)
                            pe.wait_ge(w23_made, 4)
                        ago(pe, g_made, t, 2)
                        pe.wait_ge(aT_made, t + 1)
                        for c in range(2):
                            mm(q_g[:, t % 2, :], m.xTs[:, c, t * P:(t + 1) * P], w3[:, c, :], start=(c == 0), stop=False)
                        for c in range(4):
                            last = mm(q_g[:, t % 2, :], aT[:, t % 2, c * P:(c + 1) * P], w23[:, c, :], start=False, stop=(c == 3))
                        last.then_inc(g_mm, 1)

                    def turn_g(t):
                        pe.wait_ge(g_made, t + 1)
                        ago(pe, gT_made, t, 2)
                        for c in range(4):
                            last = pe.transpose(q_gT[:, t % 2, c * P:(c + 1) * P], g[:, t % 2, c * P:(c + 1) * P], m.ident[:, :])
                        last.then_inc(g_turned, 1)

                    def update(t):
                        if t == 0:
                            pe.wait_ge(w_in0, 48)
                            pe.wait_ge(b23_made, 2)
                        pe.wait_ge(gT_made, t + 1)
                        ago(pe, y_bias, t, 1)
                        for c in range(4):
                            last = mm(q_y[:, 0:D], gT[:, t % 2, c * P:(c + 1) * P], w4[:, c, :], start=(c == 0), stop=(c == 3))
                        last.then_inc(y_mm, 1)

                    def turn_x1(t):
                        pe.wait_ge(x1_made, t + 1)
                        ago(pe, xT_made, t, 1)
                        for c in range(2):
                            last = pe.transpose(q_xT[:, c * P:(c + 1) * P], m.xs[:, t, c * P:(c + 1) * P], m.ident[:, :])
                        last.then_inc(x1_turned, 1)

                    run_tiles([(turn_agg, 0), (hidden, 1), (turn_g, 3), (update, 4), (turn_x1, 6)])

                @block.scalar
                def _(act):
                    act.dma_start(w2T[:, :, :], W2T.rearrange("(c p) n -> p c n", p=P)).then_inc(w23_in, 16)

                    def copy_aT(t):
                        act.wait_ge(agg_turned, t + 1)
                        ago(act, g_mm, t, 2)
                        nc.scalar.activation(aT[:, t % 2, :], q_aT[:, t % 2, :], ACT.Copy).then_inc(aT_made, 1)
                        if t == 1:
                            for c in (1, 3):
                                act.wait_ge(w23_mm, c + 1)
                                nc.scalar.activation(w23[:, c, :], (q_g, q_gT)[c // 2][:, 1, :], ACT.Copy).then_inc(w23_made, 1)

                    def relu_gT(t):
                        act.wait_ge(g_turned, t + 1)
                        ago(act, y_mm, t, 2)
                        nc.scalar.activation(gT[:, t % 2, :], q_gT[:, t % 2, :], ACT.Relu).then_inc(gT_made, 1)

                    def std(t):
                        act.wait_ge(var_made, t + 1)
                        ago(act, rstd, t, 2)
                        nc.scalar.activation(st[:, t % 2, 8:9], st[:, t % 2, 7:8], ACT.Sqrt, bias=eps[:, 0:1]).then_inc(std_made, 1)

                    def copy_xT(t):
                        act.wait_ge(x1_turned, t + 1)
                        nc.scalar.activation(m.xTs[:, :, t * P:(t + 1) * P], q_xT[:, 0:D].rearrange("p (c n) -> p c n", c=2),
                                             ACT.Copy).then_inc(xT_made, 1)

                    run_tiles([(copy_aT, 0), (relu_gT, 3), (std, 4), (copy_xT, 6)])

                @block.vector
                def _(dve):
                    dve.memset(eps[:, :], EPS_LN)
                    do = Chain(dve, sum_deg)
                    for t in range(NT):
                        do(dve.scalar_tensor_tensor(g[:, 0, 0:STEPS], m.ntb[:, 0:STEPS], float(t * P), m.degs[:, 0:STEPS],
                                                    ALU.is_equal, ALU.mult, accum_out=m.deg[:, t:t + 1]))
                    dve.wait_ge(w23_in, 48)
                    dve.tensor_copy(b2w[:, :, :], b2c[:, :].unsqueeze(2).to_broadcast([P, 4, P])).then_inc(bw_made, 1)
                    dve.wait_ge(b23_made, 1)
                    dve.tensor_copy(b23[:, :], q_y[:, :]).then_inc(b23_made, 1)
                    for c in (0, 2):
                        dve.wait_ge(w23_mm, c + 1)
                        dve.tensor_copy(w23[:, c, :], (q_g, q_gT)[c // 2][:, 0, :]).then_inc(w23_made, 1)
                    dve.wait_ge(w_in0, 48)
                    dve.wait_ge(b23_made, 2)

                    def bias(t):
                        ago(dve, g_made, t, 2)
                        dve.scalar_tensor_tensor(base[:, t % 2, :], b23[:, :], m.deg[:, t:t + 1], b3b[:, :], ALU.mult, ALU.add
                                                 ).then_inc(base_made, 1)

                    def add_bias(t):
                        dve.wait_ge(g_mm, t + 1)
                        dve.wait_ge(base_made, t + 1)
                        ago(dve, g_turned, t, 2)
                        dve.tensor_tensor(g[:, t % 2, :], q_g[:, t % 2, :], base[:, t % 2, :], ALU.add).then_inc(g_made, 1)

                    def residual(t):
                        yt, s6 = y[:, t % 2, :], st[:, t % 2, :]
                        dve.wait_ge(y_mm, t + 1)
                        ago(dve, x1_made, t, 2)
                        dve.tensor_tensor(yt, q_y[:, 0:D], b4b[:, :], ALU.add).then_inc(y_bias, 1)
                        dve.wait_ge(y_bias, t + 1)
                        dve.scalar_tensor_tensor(yt, m.xs[:, t, :], 2.0, yt, ALU.mult, ALU.add).then_inc(y_made, 1)
                        dve.wait_ge(y_made, t + 1)
                        dve.bn_stats(s6[:, 0:6], yt).then_inc(stats, 1)
                        dve.wait_ge(stats, t + 1)
                        dve.bn_aggr(s6[:, 6:8], s6[:, 0:6]).then_inc(var_made, 1)

                    def normalise(t):
                        s6 = st[:, t % 2, :]
                        dve.wait_ge(std_made, t + 1)
                        dve.reciprocal(s6[:, 9:10], s6[:, 8:9]).then_inc(rstd, 1)
                        dve.wait_ge(rstd, t + 1)
                        dve.tensor_scalar(m.xs[:, t, :], y[:, t % 2, :], s6[:, 6:7], s6[:, 9:10], ALU.subtract, ALU.mult
                                          ).then_inc(x1_made, 1)

                    run_tiles([(bias, 0), (normalise, 5), (residual, 4), (add_bias, 1)])

        with ExitStack() as ctx:
            wtd = sb(ctx, "wtd", [P, 2, R * H])
            blk = sb(ctx, "blk", [P, 2, 2 * H])
            row = sb(ctx, "row", [P, 2, R * ROW])
            pr = psum(ctx, "pr", [P, 6, 512])
            pv = psum(ctx, "pv", [P, 512])
            pd = psum(ctx, "pd", [P, 512])
            blk_made, v_made, v_copied, row_mm, row_dve, row_act, d_mm, d_out, dve_c = (
                sem(ctx, n) for n in ("blk_made", "v_made", "v_copied", "row_mm", "row_dve", "row_act", "d_mm",
                                      "d_out", "dve_c"))
            row_wr = [sem(ctx, f"row_wr{k}") for k in range(2)]
            blk0 = sem(ctx, "blk0")
            sdf = sb(ctx, "sdf", [P, 2, NT, R * H])
            s0, s1_, s2_ = (sem(ctx, f"split_s{k}") for k in range(3))
            with nc.Block() as block:
                @block.sync
                def _(sp):
                    for t in range(NT):
                        sp.wait_ge(row_dve, R // 2 * (t + 1))
                        sp.wait_ge(row_act, R // 2 * (t + 1))
                        sp.dma_start(T_dram.rearrange("(r t p) n -> t p r n", r=R, p=P)[t],
                                     row[:, t % 2, :].rearrange("p (r n) -> p r n", r=R)).then_inc(row_wr[t % 2], 16)
                    for k in range(2):
                        sp.wait_ge(row_wr[k], 16 * (NT // 2))

                @block.gpsimd
                def _(pool):
                    pool.memset(blk[:, :, :], 1.0).then_inc(blk0, 1)
                    v = blk[:, :, :].rearrange("p c (s h) -> p c s h", s=2)
                    pool.wait_ge(blk0, 1)
                    pool.affine_select(out=v, in_=v, compare_op=ALU.is_ge, fill=0.0, base=0,
                                       pattern=[[P, 2], [0, 2], [-HD, H]], channel_multiplier=1).then_inc(blk0, 1)
                    pool.wait_ge(blk0, 2)
                    pool.affine_select(out=v, in_=v, compare_op=ALU.is_gt, fill=0.0, base=HD,
                                       pattern=[[-P, 2], [0, 2], [HD, H]], channel_multiplier=-1).then_inc(blk0, 1)
                    pool.memset(m.acc[:, :, :], 0.0)

                @block.vector
                def _(dve):
                    do = Chain(dve, dve_c)
                    dve.wait_ge(w_in, 48)
                    dve.wait_ge(blk0, 3)
                    for c in range(2):
                        for s in range(2):
                            do(dve.tensor_scalar(blk[:, c, s * H:(s + 1) * H], blk[:, c, s * H:(s + 1) * H],
                                                 at[:, s, c:c + 1], None, ALU.mult))
                    dve.sem_inc(blk_made, 1)
                    dve.wait_ge(v_made, 1)
                    v = pv[:, 0:2 * R * 16].rearrange("p (f r n) -> p f r n", f=2, r=R)
                    do(dve.tensor_copy(wt[:, :, :].rearrange("p f (r h w) -> p f r h w", r=R, h=H)[:, 0, :, :, HD], v[:, 0, :, 0:H]))
                    do(dve.tensor_copy(wt[:, :, :].rearrange("p f (r h w) -> p f r h w", r=R, h=H)[:, 1, :, :, HD], v[:, 1, :, 0:H]))
                    do(dve.tensor_copy(wtd[:, 0, :].rearrange("p (r h) -> p r h", r=R), v[:, 0, :, H:2 * H]))
                    do(dve.tensor_copy(wtd[:, 1, :].rearrange("p (r h) -> p r h", r=R), v[:, 1, :, H:2 * H]))
                    dve.sem_inc(v_copied, 1)
                    for t in range(NT):
                        for r in range(0, R, 2):
                            n = t * R + r
                            dve.wait_ge(row_mm, n + 1)
                            if t >= 2:
                                dve.wait_ge(row_wr[t % 2], 16 * (t // 2))
                            dve.tensor_copy(row[:, t % 2, r * ROW:(r + 1) * ROW], pr[:, n % 6, 0:ROW]).then_inc(row_dve, 1)
                        dve.wait_ge(d_mm, t + 1)
                        dve.tensor_copy(sdf[:, 0, t, :], pd[:, 0:R * H]).then_inc(d_out, 1)
                    dve.wait_ge(s0, 1)
                    dve.tensor_tensor(sdf[:, 1, :, :], sdf[:, 0, :, :], m.sdt[:, :, 0, :], ALU.subtract).then_inc(s1_, 1)
                    dve.wait_ge(s2_, 1)
                    dve.tensor_tensor(m.sdt[:, :, 2, :], sdf[:, 1, :, :], m.sdt[:, :, 1, :], ALU.subtract)

                @block.scalar
                def _(act):
                    for t in range(NT):
                        for r in range(1, R, 2):
                            n = t * R + r
                            act.wait_ge(row_mm, n + 1)
                            if t >= 2:
                                act.wait_ge(row_wr[t % 2], 16 * (t // 2))
                            nc.scalar.activation(row[:, t % 2, r * ROW:(r + 1) * ROW], pr[:, n % 6, 0:ROW], ACT.Copy
                                                 ).then_inc(row_act, 1)
                    act.wait_ge(d_out, NT)
                    nc.scalar.activation(m.sdt[:, :, 0, :], sdf[:, 0, :, :], ACT.Copy).then_inc(s0, 1)
                    act.wait_ge(s1_, 1)
                    nc.scalar.activation(m.sdt[:, :, 1, :], sdf[:, 1, :, :], ACT.Copy).then_inc(s2_, 1)

                @block.tensor
                def _(pe):
                    pe.wait_ge(w_in, 48)
                    pe.wait_ge(blk_made, 1)
                    for f in range(2):
                        for r in range(R):
                            for c in range(2):
                                last = mm(pv[:, (f * R + r) * 16:(f * R + r + 1) * 16], wn[:, r, c, f * P:(f + 1) * P],
                                          blk[:, c, :], start=(c == 0), stop=(c == 1))
                    last.then_inc(v_made, 1)
                    pe.wait_ge(v_copied, 1)
                    for t in range(NT):
                        for r in range(R):
                            n = t * R + r
                            if n >= 6:
                                pe.wait_ge((row_dve, row_act)[n % 2], (n - 6) // 2 + 1)
                            for c in range(2):
                                last = mm(pr[:, n % 6, 0:ROW], m.xTs[:, c, t * P:(t + 1) * P], wt[:, c, r * ROW:(r + 1) * ROW],
                                          start=(c == 0), stop=(c == 1))
                            last.then_inc(row_mm, 1)
                        if t:
                            pe.wait_ge(d_out, t)
                        for c in range(2):
                            last = mm(pd[:, 0:R * H], m.xTs[:, c, t * P:(t + 1) * P], wtd[:, c, :], start=(c == 0), stop=(c == 1))
                        last.then_inc(d_mm, 1)

        l1_weights.close()
        with ExitStack() as ctx:
            G = sb(ctx, "G1", [P, 2, GU, ROW])
            ixr = sb(ctx, "ixr1", [P, 2, GU], U32)
            oh = sb(ctx, "oh1", [P, 2, GU, P], BF16)
            ohf = sb(ctx, "ohf", [P, 2, GU, P])
            ohT = sb(ctx, "ohT1", [P, 2, GU, P], BF16)
            sd8 = sb(ctx, "sd8", [P, GU, R * H])
            sc = sb(ctx, "sc", [P, 2, GU * H])
            raw = sb(ctx, "raw", [P, 2, GU * H])
            dT = sb(ctx, "dT", [P, P])
            eq = sb(ctx, "eq", [P, P + 1])
            run = sb(ctx, "run", [P, 2, P])
            rl = sb(ctx, "rl", [P, 3, GU * H], BF16)
            rlf = sb(ctx, "rlf", [P, GU * H])
            cb = sb(ctx, "cb", [P, H * (GU + 1) + 1])
            mb = sb(ctx, "mb", [P, H, GU + 1])
            fw = sb(ctx, "fw", [P, 2, H, GU + 1])
            bw = sb(ctx, "bw", [P, H, GU + 1])
            mx = sb(ctx, "mx", [P, 3, H, GU + 1], BF16)
            mxf = sb(ctx, "mxf", [P, H, GU + 1])
            av = sb(ctx, "av", [P, 2, H, 1])
            w8 = sb(ctx, "w8", [P, 2, GU * H])
            iota_b = sb(ctx, "iota_b", [P, P], BF16)
            ident_b = sb(ctx, "ident_b", [P, P], BF16)
            pt = ctx.enter_context(nc.psum_tensor("pt1", [P, 2, 8, P], BF16))
            psd = psum(ctx, "psd", [P, GU, R * H])
            pq = psum(ctx, "pq", [P, 4, P])
            pm = psum(ctx, "pm", [P, 4, GU * H])
            pw = psum(ctx, "pw", [P, 2, 512])
            s = {k: sem(ctx, "s_" + k) for k in (
                "gate_1",
                "indices_copied", "one_hots", "one_hots_wide", "one_hots_turned", "turned_copied",
                "types_scores", "types_masked", "scores", "scores_turned", "targets_copied",
                "step_max", "step_max_turned", "step_max_0", "step_max_rest", "step_max_1", "step_max_parts",
                "node_max_in", "node_max", "node_max_0", "node_max_rest", "node_max_1", "node_max_parts",
                "edge_max", "less_max", "weights", "weights_capped", "messages", "summed",
                "log_factor", "factor", "rescaled", "accumulated",
                "dve_steps")}
            g_in = [[gather_sem(f"g1_in{b}_{j}") for j in range(GU)] for b in range(2)]
            set1 = sem(ctx, "set1")
            CH = 2
            SCO = 5

            def wait_count(eng, sm, v):
                if not isinstance(v, int) or v > 0:
                    eng.wait_ge(sm, v)

            def load_tiles(eng, regs, gi):
                eng.load(regs, m.nt_i[0:1, bass.ds(gi * GU, GU)])

            def over_groups(eng, body):
                body(-1, 1, None, False, False, True)
                body(0, 0, 0, False, True, True)
                body(1, 1, 0, True, True, True)
                body(2, 0, 1, True, True, True)
                with eng.Fori(1, (GROUPS - 3) // 2) as i:
                    body(i * 2 + 1, 1, i, True, True, True)
                    body(i * 2 + 2, 0, i + 1, True, True, True)
                n = GROUPS - 2
                body(n, n % 2, n // 2, True, True, True)
                body(n + 1, (n + 1) % 2, (n + 1) // 2, True, True, False)
                body(n + 2, (n + 2) % 2, None, True, False, False)

            assert GROUPS % 2 == 1

            with nc.Block() as block:
                @block.gpsimd
                def _(pool):
                    def gather(n, b, u):
                        first = isinstance(u, int) and u == 0
                        if not first:
                            for j in range(GU):
                                pool.wait_ge(g_in[b][j], u * 16)
                        pool.sem_inc(s["gate_1"], 1)
                        pool.tensor_copy(ixr[:, b, :], m.tab_ix[:, bass.ds(n * GU, GU)]).then_inc(s["indices_copied"], 1)
                        pool.wait_ge(s["indices_copied"], n + 1)
                        pool.sem_inc(s["gate_1"], 1)
                        for j in range(GU):
                            if not first:
                                pool.wait_ge(s["summed"], (n - 2) * GU + j + 1)
                                pool.sem_inc(s["gate_1"], 1)
                            pool.indirect_dma_start(G[:, b, j, :], None, T_dram,
                                                    bass.IndirectOffsetOnAxis(ap=ixr[:, b, j:j + 1], axis=0)
                                                    ).then_inc(g_in[b][j], 16)

                    gather(0, 0, 0)
                    gather(1, 1, 0)
                    gather(2, 0, 1)
                    with pool.Fori(1, (GROUPS - 1) // 2) as i:
                        gather(i * 2 + 1, 1, i)
                        gather(i * 2 + 2, 0, i + 1)

                @block.vector
                def _(dve):
                    regs = [dve.alloc_register(f"nt_w{j}") for j in range(GU)]
                    dve.tensor_copy(iota_b[:, :], m.iota[:, :]).then_inc(s["dve_steps"], 1)
                    dve.tensor_copy(ident_b[:, :], m.ident[:, :]).then_inc(set1, 1)
                    dve.memset(eq[:, :], 0.0).then_inc(s["dve_steps"], 1)
                    dve.memset(cb[:, :], 0.0).then_inc(s["dve_steps"], 1)
                    dve.memset(fw[:, :, :, :], 0.0).then_inc(s["dve_steps"], 1)
                    dve.wait_ge(s["dve_steps"], 4)
                    K = 10

                    def body(n, b, u, prev, now, nxt):
                        c = [4]

                        def do(ins):
                            c[0] += 1
                            ins.then_inc(s["dve_steps"], 1)
                            dve.wait_ge(s["dve_steps"], n * K + c[0])

                        def one_hot(j):
                            if j == 0 and (now or prev):
                                wait_count(dve, s["one_hots_wide"], n * 4)
                                dve.wait_ge(s["node_max_in"], n) if prev else None
                            dve.tensor_scalar(oh[:, 1 - b, j, :], iota_b[:, :], m.dl[:, bass.ds((n + 1) * GU + j, 1)], None,
                                              ALU.is_equal).then_inc(s["one_hots"], 1)

                        def largest_weight():
                            dve.wait_ge(s["weights"], n)
                            dve.tensor_scalar(G[:, 1 - b, :, :].rearrange("p u (h w) -> p u h w", h=H)[:, :, :, HD],
                                              w8[:, 1, :].rearrange("p (u h) -> p u h", u=GU), 1.0, None, ALU.min
                                              ).then_inc(s["weights_capped"], 1)
                            dve.wait_ge(s["weights_capped"], n)

                        def messages(k):
                            Gv = G[:, 1 - b, k * CH:(k + 1) * CH, :].rearrange("p u (h w) -> p (u h) w", h=H)
                            dve.tensor_tensor(Gv[:, :, 0:HD], Gv[:, :, 0:HD], Gv[:, :, HD:HD + 1].to_broadcast([P, CH * H, HD]),
                                              ALU.mult).then_inc(s["messages"], 1)

                        def accumulate(j):
                            t = (n - 1) * GU + j
                            nt = dve.snap(regs[j], min_val=0, max_val=NT - 1)
                            a = m.acc[:, bass.ds(nt, 1), :].rearrange("p o n -> p (o n)")
                            if j == 0:
                                ah = a.rearrange("p (h w) -> p h w", h=H)
                                dve.wait_ge(s["factor"], n)
                                wait_count(dve, s["accumulated"], t)
                                dve.tensor_tensor(ah, ah, av[:, 1, :, :].to_broadcast([P, H, HW]), ALU.mult).then_inc(s["rescaled"], 1)
                                dve.wait_ge(s["rescaled"], n)
                            wait_count(dve, s["accumulated"], t)
                            dve.wait_ge(s["summed"], t + 1)
                            dve.tensor_tensor(a, a, pw[:, j % 2, 0:ROW], ALU.add).then_inc(s["accumulated"], 1)

                        def target_scores(k):
                            js = slice(k % 2 * (GU // 2), (k % 2 + 1) * (GU // 2))
                            if k < 2:
                                dve.wait_ge(s["types_scores"], n * 2 + k + 1)
                                dve.tensor_tensor(sd8[:, js, :].rearrange("p u (r h) -> p u r h", r=R),
                                                  psd[:, js, :].rearrange("p u (r h) -> p u r h", r=R),
                                                  m.emask[:, bass.ds(n * GU + js.start, GU // 2), :].unsqueeze(3).to_broadcast(
                                                      [P, GU // 2, R, H]), ALU.mult).then_inc(s["types_masked"], 1)
                            else:
                                dve.wait_ge(s["types_masked"], n * 2 + (k - 1))
                                do(dve.tensor_reduce(raw[:, 0, :].rearrange("p (u h) -> p u h", u=GU)[:, js, :],
                                                     sd8[:, js, :].rearrange("p u (r h) -> p u h r", r=R), AX.X, ALU.add))

                        def scores():
                            for j in range(GU):
                                dve.wait_ge(g_in[b][j], (u + 1) * 16)
                            Gv = G[:, b, :, :].rearrange("p u (h w) -> p u h w", h=H)
                            do(dve.tensor_tensor(raw[:, 1, :].rearrange("p (u h) -> p u h", u=GU), Gv[:, :, :, HD],
                                                 raw[:, 0, :].rearrange("p (u h) -> p u h", u=GU), ALU.add))
                            do(dve.scalar_tensor_tensor(sc[:, 0, :], raw[:, 1, :], 0.2, raw[:, 1, :], ALU.mult, ALU.max))
                            dve.tensor_scalar(sc[:, 1, :].rearrange("p (u h) -> p u h", u=GU),
                                              m.dl[:, bass.ds(n * GU, GU)].unsqueeze(2).to_broadcast([P, GU, H]), 0.0, None,
                                              ALU.add).then_inc(s["scores"], 1)

                        def step_max():
                            dve.wait_ge(s["targets_copied"], n + 1)
                            do(dve.tensor_tensor(eq[:, 1:P], dT[:, 1:P], dT[:, 0:P - 1], ALU.is_equal))
                            do(dve.tensor_tensor_scan(run[:, 0, :], eq[:, 0:P], pq[:, 0, :], 0.0, ALU.mult, ALU.max))
                            dve.scalar_tensor_tensor(run[:, 1, :], eq[:, 1:P + 1], 0.0, run[:, 0, :], ALU.is_equal, ALU.mult
                                                     ).then_inc(s["step_max"], 1)

                        def node_max():
                            cv = cb[:, 0:H * (GU + 1)]
                            do(dve.tensor_scalar(cv.rearrange("p (h u) -> p h u", h=H)[:, :, 1:GU + 1],
                                                 m.cont[:, bass.ds(n * GU, GU)].unsqueeze(1).to_broadcast([P, H, GU]), 0.0, None,
                                                 ALU.add))
                            dve.tensor_copy(mb[:, :, 0:1], fw[:, 1 - b, :, GU:GU + 1])
                            dve.wait_ge(s["node_max_in"], n + 1)
                            do(dve.tensor_copy(mb[:, :, 1:GU + 1], pm[:, 1, :].rearrange("p (u h) -> p h u", u=GU)))
                            f = fw[:, b, :, :].rearrange("p h u -> p (h u)")
                            do(dve.tensor_tensor_scan(f, cv, mb[:, :, :].rearrange("p h u -> p (h u)"), 0.0, ALU.mult, ALU.max))
                            dve.tensor_tensor_scan(bw[:, :, :].rearrange("p h u -> p (h u)")[:, ::-1],
                                                   cb[:, 1:H * (GU + 1) + 1][:, ::-1], f[:, ::-1], 0.0, ALU.mult, ALU.max
                                                   ).then_inc(s["node_max"], 1)
                            wait_count(dve, s["factor"], n)
                            do(dve.tensor_tensor(av[:, 0, :, :], fw[:, b, :, 0:1],
                                                 cv.rearrange("p (h u) -> p h u", h=H)[:, :, 1:2], ALU.mult))
                            dve.wait_ge(s["node_max"], n + 1)
                            dve.tensor_tensor(av[:, 0, :, :], av[:, 0, :, :], bw[:, :, 1:2], ALU.subtract).then_inc(s["log_factor"], 1)

                        def less_part(rest, value, part, rounded, done):
                            dve.wait_ge(rounded, n + 1)
                            dve.tensor_tensor(rest, value, part, ALU.subtract).then_inc(done, 1)

                        if prev:
                            load_tiles(dve, regs, n - 1)
                        for j in range(GU):
                            if nxt:
                                one_hot(j)
                            if prev and j == 0:
                                largest_weight()
                                messages(0)
                            if prev and j % CH == CH - 1 and j + 1 < GU:
                                messages((j + 1) // CH)
                            if prev and j:
                                accumulate(j - 1)
                            if now:
                                if 1 <= j <= 4:
                                    target_scores((0, 2, 1, 3)[j - 1])
                                if j == SCO:
                                    scores()
                                if j == SCO + 2:
                                    step_max()
                                if j == SCO + 4:
                                    less_part(rlf[:, :], pm[:, 0, :], rl[:, 0, :], s["step_max_0"], s["step_max_rest"])
                                if j == SCO + 5:
                                    less_part(rl[:, 2, :], rlf[:, :], rl[:, 1, :], s["step_max_1"], s["step_max_parts"])
                                if j == SCO + 7:
                                    node_max()
                                if j == SCO + 8:
                                    less_part(mxf[:, :, :], bw[:, :, :], mx[:, 0, :, :], s["node_max_0"], s["node_max_rest"])
                                if j == SCO + 9:
                                    less_part(mx[:, 2, :, :], mxf[:, :, :], mx[:, 1, :, :], s["node_max_1"], s["node_max_parts"])
                        if prev:
                            accumulate(GU - 1)
                        if now:
                            dve.wait_ge(s["edge_max"], n + 1)
                            dve.tensor_tensor(w8[:, 0, :], sc[:, 0, :], pm[:, 2, :], ALU.subtract).then_inc(s["less_max"], 1)
                            assert c[0] == K + 4, c

                    over_groups(dve, body)

                @block.scalar
                def _(act):
                    def body(n, b, u, prev, now, nxt):
                        def copy(o, i, waits, done, func=ACT.Copy):
                            act.wait_ge(waits, n + 1)
                            nc.scalar.activation(o, i, func).then_inc(done, 1)

                        def turned(k, n, b):
                            act.wait_ge(s["one_hots_turned"], n * 2 + k + 1)
                            wait_count(act, s["edge_max"], n - 1)
                            nc.scalar.activation(ohT[:, b, 8 * k:8 * k + 8, :], pt[:, k, :, :], ACT.Copy).then_inc(s["turned_copied"], 1)

                        def widen(k):
                            act.wait_ge(s["one_hots"], n * GU + 4 * k + 4)
                            wait_count(act, s["summed"], (n - 2) * GU + 4 * k + 4)
                            nc.scalar.activation(ohf[:, b, 4 * k:4 * k + 4, :], oh[:, b, 4 * k:4 * k + 4, :], ACT.Copy
                                                 ).then_inc(s["one_hots_wide"], 1)

                        if now:
                            turned(1, n, b)
                            for k in range(4):
                                widen(k)
                            copy(dT[:, :], pq[:, 1, :], s["scores_turned"], s["targets_copied"])
                            copy(rl[:, 0, :], pm[:, 0, :], s["step_max_turned"], s["step_max_0"])
                            copy(rl[:, 1, :], rlf[:, :], s["step_max_rest"], s["step_max_1"])
                        if nxt:
                            turned(0, n + 1, 1 - b)
                        if now:
                            copy(mx[:, 0, :, :], bw[:, :, :], s["node_max"], s["node_max_0"])
                            copy(mx[:, 1, :, :], mxf[:, :, :], s["node_max_rest"], s["node_max_1"])
                            wait_count(act, s["rescaled"], n)
                            copy(av[:, 1, :, :], av[:, 0, :, :], s["log_factor"], s["factor"], ACT.Exp)
                            copy(w8[:, 1, :], w8[:, 0, :], s["less_max"], s["weights"], ACT.Exp)

                    over_groups(act, body)

                @block.tensor
                def _(pe):
                    regs = [pe.alloc_register(f"nt_q{j}") for j in range(GU)]
                    pe.wait_ge(set1, 1)

                    def body(n, b, u, prev, now, nxt):
                        def turn(j):
                            pe.wait_ge(s["one_hots"], (n + 1) * GU + j + 1)
                            if j == 0:
                                wait_count(pe, s["turned_copied"], (n + 1) * 2)
                            last = pe.transpose(pt[:, j // 8, j % 8, :], oh[:, 1 - b, j, :], ident_b[:, :])
                            if j % 8 == 7:
                                last.then_inc(s["one_hots_turned"], 1)

                        def target_scores(n, b, k):
                            if k % 4 == 0:
                                if k == 0:
                                    load_tiles(pe, regs, n)
                                wait_count(pe, s["types_masked"], n * 2 - (1 - k // 4))
                                pe.wait_ge(s["turned_copied"], n * 2 + k // 4 + 1)
                            for j in range(2 * k, 2 * k + 2):
                                nt = pe.snap(regs[j], min_val=0, max_val=NT - 1)
                                tab = m.sdt[:, bass.ds(nt, 1), :, :].rearrange("p o k n -> p (o k) n")
                                for q in range(3):
                                    last = mm(psd[:, j, :], ohT[:, b, j, :], tab[:, q, :], start=(q == 0), stop=(q == 2))
                            if k % 4 == 3:
                                last.then_inc(s["types_scores"], 1)

                        def messages(j):
                            t = (n - 1) * GU + j
                            if j % CH == 0:
                                pe.wait_ge(s["messages"], (n - 1) * (GU // CH) + j // CH + 1)
                            if j == 0:
                                pe.wait_ge(s["one_hots_wide"], n * 4)
                            wait_count(pe, s["accumulated"], t - 1)
                            mm(pw[:, j % 2, 0:ROW], ohf[:, 1 - b, j, :], G[:, 1 - b, j, :], start=True, stop=True).then_inc(s["summed"], 1)

                        def turn_scores():
                            pe.wait_ge(s["scores"], n + 1)
                            pe.transpose(pq[:, 0, :], sc[:, 0, :], m.ident[:, :])
                            pe.transpose(pq[:, 1, :], sc[:, 1, :], m.ident[:, :]).then_inc(s["scores_turned"], 1)

                        def turn_max():
                            pe.wait_ge(s["step_max"], n + 1)
                            pe.transpose(pm[:, 0, :], run[:, 1, :], m.ident[:, :]).then_inc(s["step_max_turned"], 1)

                        def node_max():
                            pe.wait_ge(s["step_max_parts"], n + 1)
                            for j in range(GU):
                                for q in range(3):
                                    last = mm(pm[:, 1, j * H:(j + 1) * H], oh[:, b, j, :], rl[:, q, j * H:(j + 1) * H],
                                              start=(q == 0), stop=(q == 2))
                            last.then_inc(s["node_max_in"], 1)

                        def edge_max():
                            pe.wait_ge(s["node_max_parts"], n + 1)
                            for j in range(GU):
                                for q in range(3):
                                    last = mm(pm[:, 2, j * H:(j + 1) * H], ohT[:, b, j, :], mx[:, q, :, j + 1],
                                              start=(q == 0), stop=(q == 2))
                            last.then_inc(s["edge_max"], 1)

                        for j in range(GU):
                            if nxt and j:
                                turn(j - 1)
                            if prev:
                                messages(j)
                            if now and j in (1, 2):
                                for k in (0, 1):
                                    target_scores(n, b, 2 + 2 * j + k)
                            if now:
                                if j == SCO + 1:
                                    turn_scores()
                                if j == SCO + 3:
                                    turn_max()
                                if j == SCO + 6:
                                    node_max()
                                if j == SCO + 10:
                                    edge_max()
                            if nxt and j >= GU - 4:
                                target_scores(n + 1, 1 - b, j - (GU - 4))
                        if nxt:
                            turn(GU - 1)

                    over_groups(pe, body)

        with ExitStack() as ctx:
            den = sb(ctx, "den", [P, 2, NT, H])
            y = sb(ctx, "yf", [P, NT, D])
            st = sb(ctx, "stf", [P, NT, 6])
            mv = sb(ctx, "mv", [P, NT, 2])
            eps = sb(ctx, "epsf", [P, 1])
            std = sb(ctx, "std", [P, 2, NT])
            f_den, f_mul, f_add, f_stats, f_var, f_rstd, f_made, f_out, sq = (
                sem(ctx, "f_" + n) for n in ("den", "mul", "add", "stats", "var", "rstd", "made", "out", "std"))
            FT = 4
            assert NT % FT == 0
            with nc.Block() as block:
                @block.vector
                def _(dve):
                    av = m.acc[:, :, :].rearrange("p t (h w) -> p t h w", h=H)
                    do = Chain(dve, f_den)
                    do(dve.memset(eps[:, :], EPS_LN))
                    do(dve.tensor_scalar(den[:, 0, :, :], av[:, :, :, HD], EPS_DEN, None, ALU.add))
                    do(dve.reciprocal(den[:, 1, :, :], den[:, 0, :, :]))

                    def attend(t):
                        dve.tensor_tensor(y[:, t, :].rearrange("p (h w) -> p h w", h=H), av[:, t, :, 0:HD],
                                          den[:, 1, t, :].unsqueeze(2).to_broadcast([P, H, HD]), ALU.mult).then_inc(f_mul, 1)

                    def add_x1(t):
                        dve.wait_ge(f_mul, t + 1)
                        dve.tensor_tensor(y[:, t, :], y[:, t, :], m.xs[:, t, :], ALU.add).then_inc(f_add, 1)

                    def statistics(t):
                        dve.wait_ge(f_add, t + 1)
                        dve.bn_stats(st[:, t, :], y[:, t, :]).then_inc(f_stats, 1)

                    def variance(t):
                        dve.wait_ge(f_stats, t + 1)
                        dve.bn_aggr(mv[:, t, :], st[:, t, :]).then_inc(f_var, 1)

                    def normalise(f):
                        dve.wait_ge(sq, f + 1)
                        dve.reciprocal(std[:, 1, f * FT:(f + 1) * FT], std[:, 0, f * FT:(f + 1) * FT]).then_inc(f_rstd, 1)
                        dve.wait_ge(f_rstd, f + 1)
                        for t in range(f * FT, (f + 1) * FT):
                            dve.tensor_scalar(y[:, t, :], y[:, t, :], mv[:, t, 0:1], std[:, 1, t:t + 1], ALU.subtract, ALU.mult
                                              ).then_inc(f_made, 1)

                    LAG = 4
                    for i in range(NT + LAG):
                        for f, lag in ((attend, 0), (add_x1, 1), (statistics, 2), (variance, 3)):
                            if 0 <= i - lag < NT:
                                f(i - lag)
                        if i >= LAG + FT and (i - LAG) % FT == 0:
                            normalise((i - LAG) // FT - 1)
                    normalise(NT // FT - 1)

                @block.scalar
                def _(act):
                    for f in range(NT // FT):
                        act.wait_ge(f_var, (f + 1) * FT)
                        nc.scalar.activation(std[:, 0, f * FT:(f + 1) * FT], mv[:, f * FT:(f + 1) * FT, 1], ACT.Sqrt,
                                             bias=eps[:, 0:1]).then_inc(sq, 1)

                @block.sync
                def _(sp):
                    for f in range(NT // FT):
                        first, end = f * FT, min((f + 1) * FT, N // P)
                        sp.wait_ge(f_made, (f + 1) * FT)
                        sp.dma_start(out[first * P:end * P, :].rearrange("(t p) n -> p t n", p=P), y[:, first:end, :]
                                     ).then_inc(f_out, 16)
                    sp.dma_start(out[N // P * P:N, :], y[0:N % P, N // P, :]).then_inc(f_out, 16)
                    sp.wait_ge(f_out, 16 * (NT // FT + 1))


def kernel(**inputs):
    import numpy as np
    import concourse.bacc as bacc
    from concourse.bass_utils import run_bass_kernel_spmd

    a = {k: np.asarray(v) for k, v in inputs.items()}
    pad_e = EP - E
    x = np.pad(a["x"], ((0, NP - N), (0, 0)))
    src, dst, typ = (a[k].astype(np.int32) for k in ("src", "dst", "edge_type_8"))
    dst = np.concatenate([dst, np.full(pad_e, PAD_DST, np.int32)])
    meta = np.stack([np.pad(src, (0, pad_e)), dst, np.pad(typ, (0, pad_e)), np.arange(EP, dtype=np.int32)], axis=1)
    W = a["L1_gnn_W"]
    WT = np.pad(W.reshape(R, H, HD, D).transpose(3, 0, 1, 2), ((0, 0), (0, 0), (0, 0), (0, 1))).reshape(D, R * ROW)
    attn = np.stack([a["L1_gnn_attn_src"].reshape(2, P), a["L1_gnn_attn_dst"].reshape(2, P)]).transpose(2, 0, 1)
    arrays = {
        "x": x, "xT": x.T, "dst": dst.reshape(EP, 1), "dst_tiles": dst.reshape(TILES_E, P).T, "meta": meta,
        "ef": np.pad(a["edge_attr_64"], ((0, pad_e), (0, 0))),
        "efT": np.tile(np.pad(a["edge_attr_64"].T, ((0, 0), (0, pad_e))), (2, 1)),
        "W1": a["L0_gnn_W1"], "b1": a["L0_gnn_b1"], "W2T": a["L0_gnn_W2"].T, "b2": a["L0_gnn_b2"].reshape(4, P).T,
        "W3": a["L0_gnn_W3"], "b3": a["L0_gnn_b3"], "W4": a["L0_gnn_W4"], "b4": a["L0_gnn_b4"],
        "WT": WT, "Wn": W, "attn": attn,
    }
    arrays = {f"in_{k}": np.ascontiguousarray(v) for k, v in arrays.items()}
    nc = bacc.Bacc("TRN2", target_bir_lowering=False, num_devices=1)
    args = [nc.dram_tensor(k, v.shape, mybir.dt.from_np(v.dtype), kind="ExternalInput").ap() for k, v in arrays.items()]
    out = nc.dram_tensor("out", (N, D), F32, kind="ExternalOutput").ap()
    gnn_kernel(nc, *args, out)
    return run_bass_kernel_spmd(nc, [arrays], core_ids=[0]).results[0]["out"]
```
